# Optimizing a Trainium2 kernel written in Bass

```python
import numpy as np
import jax
import jax.numpy as jnp

def _softmax(x, axis=-1):
    return jax.nn.softmax(x, axis=axis)

def _gelu(x):
    return jax.nn.gelu(x, approximate=True)

def _silu(x):
    return jax.nn.silu(x)

def _sigmoid(x):
    return jax.nn.sigmoid(x)

def _layernorm(x, axis=-1, eps=1e-05):
    m = jnp.mean(x, axis=axis, keepdims=True)
    v = jnp.var(x, axis=axis, keepdims=True)
    return (x - m) / jnp.sqrt(v + eps)

def _scatter_add(tgt, idx, src, axis=0):
    return tgt.at[idx].add(src)

def _segment_sum(src, seg, n):
    return jax.ops.segment_sum(src, seg, n)
kernel_name = 'mk_xattn_ffn_d2_seqx_r8_4615c4'

def setup_inputs(seed: int=0):
    np.random.seed(seed)
    _w = jnp.asarray

    def _rec_inputs():
        import jax
        import jax.numpy as jnp
        _rk = jax.random.key(seed)
        x = -0.0003929 + 0.9999 * jax.random.normal(jax.random.fold_in(_rk, 1), (64, 128, 128), jnp.float32)
        _lenS = 128 - jax.random.randint(jax.random.fold_in(_rk, 7), (64,), 0, max(1, 128 // 4) + 1, jnp.int32)
        _lenS2 = 77 - jax.random.randint(jax.random.fold_in(_rk, 8), (64,), 0, max(1, 77 // 4) + 1, jnp.int32)
        _ctx_768P = jax.random.normal(jax.random.fold_in(_rk, 11), (64, 16, 96), jnp.float32)
        _ctx_768c = jax.random.dirichlet(jax.random.fold_in(_rk, 511), 0.3 * jnp.ones((16,), jnp.float32), (64, 77))
        _ctx_768t = jnp.einsum('bsk,bkd->bsd', _ctx_768c, _ctx_768P)
        _ctx_768t = _ctx_768t * jax.lax.rsqrt(jnp.mean(jnp.square(_ctx_768t)) + 1e-12) * 0.953939
        ctx_768 = 0.00095986 + 0.999812 * (_ctx_768t + 0.3 * jax.random.normal(jax.random.fold_in(_rk, 611), (64, 77, 96), jnp.float32))
        _validS = jnp.arange(128)[None, :] < _lenS[:, None]
        _validS2 = jnp.arange(77)[None, :] < _lenS2[:, None]
        _causal = jnp.tril(jnp.ones((128, 128), dtype=bool))
        mask_BxS2_bf1 = jnp.ones((64, 77), dtype=bool)
        return (x, ctx_768, mask_BxS2_bf1)
    x, ctx_768, mask_BxS2_bf1 = _rec_inputs()

    def _L0_xattn_setup():
        import jax, jax.numpy as jnp
        import numpy as np
        DIM = 128
        CTX_DIM = 96
        HEADS = 16
        key = jax.random.key(seed)
        ks = jax.random.split(key, 7)
        B, N, M = (4, 512, 32)
        x = jax.random.normal(ks[0], (B, N, DIM), dtype=jnp.float32)
        context = jax.random.normal(ks[1], (B, M, CTX_DIM), dtype=jnp.float32)
        context_mask = jnp.ones((B, M), dtype=bool)
        s_d = 1.0 / np.sqrt(DIM)
        s_c = 1.0 / np.sqrt(CTX_DIM)
        Wq = jax.random.normal(ks[2], (DIM, DIM), dtype=jnp.float32) * s_d
        Wk = jax.random.normal(ks[3], (CTX_DIM, DIM), dtype=jnp.float32) * s_c
        Wv = jax.random.normal(ks[4], (CTX_DIM, DIM), dtype=jnp.float32) * s_c
        Wo = jax.random.normal(ks[5], (DIM, DIM), dtype=jnp.float32) * s_d
        return {'x': x, 'context': context, 'context_mask': context_mask, 'Wq': Wq, 'Wk': Wk, 'Wv': Wv, 'Wo': Wo}
    _L0_xattn_all = _L0_xattn_setup()
    _L0_xattn_in = {k: v for k, v in _L0_xattn_all.items() if k in ('Wq', 'Wk', 'Wv', 'Wo')}
    del _L0_xattn_all

    def _L0_ffn_setup():
        import jax, jax.numpy as jnp
        import numpy as np
        from jax import lax
        T, B, I, M, O = (32, 64, 128, 128, 128)

        def _xavier(key, shape):
            fan_out, fan_in = shape
            limit = float(np.sqrt(6.0 / (fan_in + fan_out)))
            return jax.random.uniform(key, shape, jnp.float32, -limit, limit)
        key = jax.random.key(seed)
        ks = jax.random.split(key, 9)
        x = jax.random.normal(ks[0], (T, B, I), jnp.float32)
        return {'x': x, 'wf': _xavier(ks[1], (M, I)), 'uf': _xavier(ks[2], (M, M)), 'bf': jnp.zeros((M,), jnp.float32), 'wi': _xavier(ks[3], (M, I)), 'ui': _xavier(ks[4], (M, M)), 'bi': jnp.zeros((M,), jnp.float32), 'wc': _xavier(ks[5], (M, I)), 'uc': _xavier(ks[6], (M, M)), 'bc': jnp.zeros((M,), jnp.float32), 'wo': _xavier(ks[7], (O, I)), 'uo': _xavier(ks[8], (O, M)), 'bo': jnp.zeros((O,), jnp.float32), 'in_c': jnp.zeros((M,), jnp.float32)}
    _L0_ffn_all = _L0_ffn_setup()
    _L0_ffn_in = {k: v for k, v in _L0_ffn_all.items() if k in ('wf', 'uf', 'bf', 'wi', 'ui', 'bi', 'wc', 'uc', 'bc', 'wo', 'uo', 'bo', 'in_c')}
    del _L0_ffn_all

    def _L1_xattn_setup():
        import jax, jax.numpy as jnp
        import numpy as np
        import math
        E = 128
        EV = 128
        FFN = 512
        DINO = 96
        B, S, P = (64, 64, 32)

        def bitnet_linear(x, W, b):
            w_scale = jnp.maximum(jnp.mean(jnp.abs(W)), 1e-05)
            qW = jnp.sign(W) * (jnp.abs(W) > 0.5 * w_scale).astype(W.dtype)
            i_scale = jnp.maximum(jnp.max(jnp.abs(x)), 1e-08) / 127.0
            qx = jnp.clip(jnp.round(x / i_scale), -128.0, 127.0)
            out = jnp.einsum('...i,oi->...o', qx, qW) * (w_scale * i_scale)
            return out + b
        key = jax.random.key(seed)
        ks = iter(jax.random.split(key, 32))

        def lin_w(fin, fout):
            return jax.random.normal(next(ks), (fout, fin), jnp.float32) * math.sqrt(2.0 / fin)
        return {'text_embeddings': jax.random.normal(next(ks), (B, S, E), jnp.float32), 'dinov2_features': jax.random.normal(next(ks), (B, P, DINO), jnp.float32), 'W_d2v': lin_w(DINO, EV), 'b_d2v': jnp.zeros((EV,), jnp.float32), 'W_img': lin_w(EV, E), 'b_img': jnp.zeros((E,), jnp.float32), 'W_txt': lin_w(E, E), 'b_txt': jnp.zeros((E,), jnp.float32), 'W_att0': lin_w(E, E // 2), 'b_att0': jnp.zeros((E // 2,), jnp.float32), 'W_att1': lin_w(E, E // 2), 'b_att1': jnp.zeros((E // 2,), jnp.float32), 'W_f1': lin_w(2 * E, FFN), 'b_f1': jnp.zeros((FFN,), jnp.float32), 'W_f2': lin_w(FFN, E), 'b_f2': jnp.zeros((E,), jnp.float32)}
    _L1_xattn_all = _L1_xattn_setup()
    _L1_xattn_in = {k: v for k, v in _L1_xattn_all.items() if k in ('W_d2v', 'b_d2v', 'W_img', 'b_img', 'W_txt', 'b_txt', 'W_att0', 'b_att0', 'W_att1', 'b_att1', 'W_f1', 'b_f1', 'W_f2', 'b_f2')}
    del _L1_xattn_all

    def _L1_ffn_setup():
        import jax, jax.numpy as jnp
        import numpy as np
        B, T, D, F, E = (2, 128, 128, 512, 8)
        EPS = 1e-06
        key = jax.random.key(seed)
        k = jax.random.split(key, 5)
        scale = 0.02
        return {'x': jax.random.normal(k[0], (B, T, D), dtype=jnp.float32), 'rms_w': jnp.ones((D,), dtype=jnp.float32), 'gate_w': jax.random.normal(k[1], (E, D), dtype=jnp.float32) * scale, 'W1': jax.random.normal(k[2], (E, D, F), dtype=jnp.float32) * scale, 'b1': jnp.zeros((E, F), dtype=jnp.float32), 'W2': jax.random.normal(k[3], (E, F, D), dtype=jnp.float32) * scale, 'b2': jnp.zeros((E, D), dtype=jnp.float32)}
    _L1_ffn_all = _L1_ffn_setup()
    _L1_ffn_in = {k: v for k, v in _L1_ffn_all.items() if k in ('rms_w', 'gate_w', 'W1', 'b1', 'W2', 'b2')}
    del _L1_ffn_all
    return {'x': x, 'ctx_768': ctx_768, 'mask_BxS2_bf1': mask_BxS2_bf1, 'L0_xattn_Wq': _L0_xattn_in['Wq'], 'L0_xattn_Wk': _L0_xattn_in['Wk'], 'L0_xattn_Wv': _L0_xattn_in['Wv'], 'L0_xattn_Wo': _L0_xattn_in['Wo'], 'L0_ffn_wf': _L0_ffn_in['wf'], 'L0_ffn_uf': _L0_ffn_in['uf'], 'L0_ffn_bf': _L0_ffn_in['bf'], 'L0_ffn_wi': _L0_ffn_in['wi'], 'L0_ffn_ui': _L0_ffn_in['ui'], 'L0_ffn_bi': _L0_ffn_in['bi'], 'L0_ffn_wc': _L0_ffn_in['wc'], 'L0_ffn_uc': _L0_ffn_in['uc'], 'L0_ffn_bc': _L0_ffn_in['bc'], 'L0_ffn_wo': _L0_ffn_in['wo'], 'L0_ffn_uo': _L0_ffn_in['uo'], 'L0_ffn_bo': _L0_ffn_in['bo'], 'L0_ffn_in_c': _L0_ffn_in['in_c'], 'L1_xattn_W_d2v': _L1_xattn_in['W_d2v'], 'L1_xattn_b_d2v': _L1_xattn_in['b_d2v'], 'L1_xattn_W_img': _L1_xattn_in['W_img'], 'L1_xattn_b_img': _L1_xattn_in['b_img'], 'L1_xattn_W_txt': _L1_xattn_in['W_txt'], 'L1_xattn_b_txt': _L1_xattn_in['b_txt'], 'L1_xattn_W_att0': _L1_xattn_in['W_att0'], 'L1_xattn_b_att0': _L1_xattn_in['b_att0'], 'L1_xattn_W_att1': _L1_xattn_in['W_att1'], 'L1_xattn_b_att1': _L1_xattn_in['b_att1'], 'L1_xattn_W_f1': _L1_xattn_in['W_f1'], 'L1_xattn_b_f1': _L1_xattn_in['b_f1'], 'L1_xattn_W_f2': _L1_xattn_in['W_f2'], 'L1_xattn_b_f2': _L1_xattn_in['b_f2'], 'L1_ffn_rms_w': _L1_ffn_in['rms_w'], 'L1_ffn_gate_w': _L1_ffn_in['gate_w'], 'L1_ffn_W1': _L1_ffn_in['W1'], 'L1_ffn_b1': _L1_ffn_in['b1'], 'L1_ffn_W2': _L1_ffn_in['W2'], 'L1_ffn_b2': _L1_ffn_in['b2']}

def reference(x, ctx_768, mask_BxS2_bf1, L0_xattn_Wq, L0_xattn_Wk, L0_xattn_Wv, L0_xattn_Wo, L0_ffn_wf, L0_ffn_uf, L0_ffn_bf, L0_ffn_wi, L0_ffn_ui, L0_ffn_bi, L0_ffn_wc, L0_ffn_uc, L0_ffn_bc, L0_ffn_wo, L0_ffn_uo, L0_ffn_bo, L0_ffn_in_c, L1_xattn_W_d2v, L1_xattn_b_d2v, L1_xattn_W_img, L1_xattn_b_img, L1_xattn_W_txt, L1_xattn_b_txt, L1_xattn_W_att0, L1_xattn_b_att0, L1_xattn_W_att1, L1_xattn_b_att1, L1_xattn_W_f1, L1_xattn_b_f1, L1_xattn_W_f2, L1_xattn_b_f2, L1_ffn_rms_w, L1_ffn_gate_w, L1_ffn_W1, L1_ffn_b1, L1_ffn_W2, L1_ffn_b2):
    import jax
    import jax.numpy as jnp

    def _L0_xattn_ref(x, context, context_mask, Wq, Wk, Wv, Wo):
        import jax, jax.numpy as jnp
        import numpy as np
        DIM = 128
        CTX_DIM = 96
        HEADS = 16
        B, N, _ = x.shape
        M = context.shape[1]
        hd = DIM // HEADS
        scale = hd ** (-0.5)
        q = (x @ Wq).reshape(B, N, HEADS, hd).transpose(0, 2, 1, 3)
        k = (context @ Wk).reshape(B, M, HEADS, hd).transpose(0, 2, 1, 3)
        v = (context @ Wv).reshape(B, M, HEADS, hd).transpose(0, 2, 1, 3)
        scores = jnp.einsum('bhid,bhjd->bhij', q, k) * scale
        max_neg = -jnp.finfo(scores.dtype).max
        scores = jnp.where(context_mask[:, None, None, :], scores, max_neg)
        attn = jax.nn.softmax(scores, axis=-1)
        out = jnp.einsum('bhij,bhjd->bhid', attn, v)
        out = out.transpose(0, 2, 1, 3).reshape(B, N, DIM)
        return out @ Wo

    def _L0_ffn_ref(x, wf, uf, bf, wi, ui, bi, wc, uc, bc, wo, uo, bo, in_c):
        import jax, jax.numpy as jnp
        import numpy as np
        from jax import lax
        T, B, I, M, O = (32, 64, 128, 128, 128)

        def _xavier(key, shape):
            fan_out, fan_in = shape
            limit = float(np.sqrt(6.0 / (fan_in + fan_out)))
            return jax.random.uniform(key, shape, jnp.float32, -limit, limit)
        batch = x.shape[1]
        c0 = jnp.broadcast_to(in_c, (batch, in_c.shape[0]))

        def step(c, xt):
            ft = jax.nn.sigmoid(xt @ wf.T + c @ uf.T + bf)
            it = jax.nn.sigmoid(xt @ wi.T + c @ ui.T + bi)
            gt = jnp.tanh(xt @ wc.T + c @ uc.T + bc)
            c = ft * c + it * gt
            return (c, None)
        c_final, _ = lax.scan(step, c0, x)
        h = jnp.tanh(jnp.einsum('tbi,oi->tbo', x, wo) + c_final @ uo.T + bo)
        return h

    def _L1_xattn_ref(text_embeddings, dinov2_features, W_d2v, b_d2v, W_img, b_img, W_txt, b_txt, W_att0, b_att0, W_att1, b_att1, W_f1, b_f1, W_f2, b_f2):
        import jax, jax.numpy as jnp
        import numpy as np
        import math
        E = 128
        EV = 128
        FFN = 512
        DINO = 96
        B, S, P = (64, 64, 32)

        def bitnet_linear(x, W, b):
            w_scale = jnp.maximum(jnp.mean(jnp.abs(W)), 1e-05)
            qW = jnp.sign(W) * (jnp.abs(W) > 0.5 * w_scale).astype(W.dtype)
            i_scale = jnp.maximum(jnp.max(jnp.abs(x)), 1e-08) / 127.0
            qx = jnp.clip(jnp.round(x / i_scale), -128.0, 127.0)
            out = jnp.einsum('...i,oi->...o', qx, qW) * (w_scale * i_scale)
            return out + b
        b, s, e = text_embeddings.shape
        vis = bitnet_linear(dinov2_features, W_d2v, b_d2v)
        image_embeds = bitnet_linear(vis, W_img, b_img)
        fused = bitnet_linear(text_embeddings, W_txt, b_txt)
        inv_sqrt_e = 1.0 / math.sqrt(e)
        for Wa, ba in ((W_att0, b_att0), (W_att1, b_att1)):
            kv = bitnet_linear(image_embeds, Wa, ba)
            k = jnp.concatenate([kv, kv], axis=-1)
            scores = jnp.einsum('bse,bpe->bsp', fused, k) * inv_sqrt_e
            attn = jax.nn.softmax(scores, axis=-1)
            fused = fused + 0.1 * jnp.einsum('bsp,bpe->bse', attn, k)
        avg_img = jnp.mean(image_embeds, axis=1, keepdims=True)
        concatenated = jnp.concatenate([fused, jnp.broadcast_to(avg_img, (b, s, e))], axis=-1)
        h = jax.nn.relu(bitnet_linear(concatenated, W_f1, b_f1))
        return bitnet_linear(h, W_f2, b_f2)

    def _L1_ffn_ref(x, rms_w, gate_w, W1, b1, W2, b2):
        import jax, jax.numpy as jnp
        import numpy as np
        B, T, D, F, E = (2, 128, 128, 512, 8)
        EPS = 1e-06
        ms = jnp.mean(x * x, axis=-1, keepdims=True)
        xn = x * jax.lax.rsqrt(ms + EPS) * rms_w
        logits = jnp.einsum('btd,ed->bte', xn, gate_w)
        scores = jax.nn.softmax(logits, axis=-1)
        top1_idx = jnp.argmax(scores, axis=-1)
        top1_score = jnp.max(scores, axis=-1)
        out = jnp.zeros_like(xn)
        for e in range(E):
            h = jax.nn.silu(jnp.einsum('btd,df->btf', xn, W1[e]) + b1[e])
            ye = jnp.einsum('btf,fd->btd', h, W2[e]) + b2[e]
            out = jnp.where((top1_idx == e)[..., None], ye, out)
        return out * top1_score[..., None]
    x = x + _L0_xattn_ref(_layernorm(x, axis=-1), ctx_768, mask_BxS2_bf1, L0_xattn_Wq, L0_xattn_Wk, L0_xattn_Wv, L0_xattn_Wo)
    x = x + _L0_ffn_ref(_layernorm(x, axis=-1), L0_ffn_wf, L0_ffn_uf, L0_ffn_bf, L0_ffn_wi, L0_ffn_ui, L0_ffn_bi, L0_ffn_wc, L0_ffn_uc, L0_ffn_bc, L0_ffn_wo, L0_ffn_uo, L0_ffn_bo, L0_ffn_in_c)
    x = x + _L1_xattn_ref(_layernorm(x, axis=-1), ctx_768, L1_xattn_W_d2v, L1_xattn_b_d2v, L1_xattn_W_img, L1_xattn_b_img, L1_xattn_W_txt, L1_xattn_b_txt, L1_xattn_W_att0, L1_xattn_b_att0, L1_xattn_W_att1, L1_xattn_b_att1, L1_xattn_W_f1, L1_xattn_b_f1, L1_xattn_W_f2, L1_xattn_b_f2)
    x = x + _L1_ffn_ref(_layernorm(x, axis=-1), L1_ffn_rms_w, L1_ffn_gate_w, L1_ffn_W1, L1_ffn_b1, L1_ffn_W2, L1_ffn_b2)
    return x

_drawn_inputs = setup_inputs


def setup_inputs(seed=0):
    import zlib

    import numpy as np

    out = dict(_drawn_inputs(seed))
    spreads = {'L0_ffn_bf': (0.0, 0.591),
     'L0_ffn_bi': (0.0, 0.586),
     'L0_ffn_bc': (0.0, 0.1),
     'L0_ffn_bo': (0.0, 0.1),
     'L0_ffn_in_c': (0.0, 0.8),
     'L1_xattn_b_d2v': (0.0, 0.292),
     'L1_xattn_b_img': (0.0, 0.1),
     'L1_xattn_b_txt': (0.0, 0.1),
     'L1_xattn_b_att0': (0.0, 0.8),
     'L1_xattn_b_att1': (0.0, 0.8),
     'L1_xattn_b_f1': (0.0, 0.1),
     'L1_xattn_b_f2': (0.0, 0.1),
     'L1_ffn_rms_w': (1.0, 0.6),
     'L1_ffn_b1': (0.0, 0.8),
     'L1_ffn_b2': (0.0, 0.618)}
    factors = {'L1_xattn_W_att0': 3.395,
     'L1_xattn_W_att1': 3.447,
     'L1_ffn_gate_w': 4.047,
     'L1_ffn_W1': 8.0,
     'L1_ffn_W2': 7.659}
    for name, (base, spread) in spreads.items():
        noise = np.random.default_rng([zlib.crc32(name.encode()), seed]).standard_normal(out[name].shape)
        drawn = base * np.exp(spread * noise) if base else spread * noise
        out[name] = jnp.asarray(drawn.astype(out[name].dtype))
    for name, factor in factors.items():
        out[name] = (out[name] * factor).astype(out[name].dtype)
    return out
```

```python
from contextlib import ExitStack

import numpy as np

import concourse.bass as bass
from concourse import mybir

P = 128
B, S, D = 64, 128, 128
M, CD = 77, 96
H, HD = 16, 8
Q = 4
F = 512
E = 8
NT = B * S
NC = B * M
PW = H * M + (P - M) + 1
CW = 448
NCC = NC // CW
G4 = 4
NG = B // G4
TILES = B + E - 1
SORTED = -(-TILES // 2) * 2 * P
ROWS = (TILES + 1) * P
RW = D + 4
MEAN, SCORE, TOKEN, RSTD = range(4)
MAGIC = 12582912.0
BIG = 3.3895313892515355e38

ALU = mybir.AluOpType
ACT = mybir.ActivationFunctionType
BF16 = mybir.dt.bfloat16
F32 = mybir.dt.float32
I32 = mybir.dt.int32
U8 = mybir.dt.uint8
AX = mybir.AxisListType
RMAX = bass.bass_isa.ReduceOp.max
RADD = bass.bass_isa.ReduceOp.add

WEIGHTS = ("d2v", "img", "txt", "att0", "att1", "f1", "f2")


def batches(eng, depth, body, count=B, unroll=2):
    lo = -(-depth // unroll) * unroll
    turns = (count - lo) // unroll
    for i in range(lo):
        body(i, i % unroll, lambda n, i=i: 0 <= i - n < count)
    with eng.Fori(0, turns) as turn:
        for u in range(unroll):
            body(turn * unroll + (lo + u), u, lambda n: True)
    for i in range(lo + turns * unroll, count + depth - 1):
        body(i, i % unroll, lambda n, i=i: 0 <= i - n < count)


def wait(eng, sem, value):
    if isinstance(value, int) and value <= 0:
        return
    eng.wait_ge(sem, value)


C_ID, C_KM, C_VM, C_TRI, C_IOTA, C_INV, C_T = 0, 128, 144, 656, 784, 792, 800
C_TILE = C_T + 64
C_W = C_TILE + TILES


def constants():
    c = np.zeros((P, C_W), np.float32)
    p = np.arange(P)
    c[:, C_ID:C_ID + P] = np.eye(P)
    for q in range(Q):
        for g in range(Q):
            c[:, C_KM + 4 * q + g] = p // HD == 4 * g + q
        c[:, C_VM + q * D:C_VM + (q + 1) * D] = (np.arange(D) % 32) // HD == q
    c[:, C_TRI:C_TRI + P] = p[:, None] < p[None, :]
    c[:, C_IOTA:C_IOTA + E] = np.arange(E)
    for n, count in enumerate((CD * D, D * D, D * D, D * 64, D * 64, 2 * D * F, F * D)):
        c[:, C_INV + n] = 1.0 / count
    c[:, C_T:C_T + 64] = np.arange(64) * P
    c[:, C_TILE:C_TILE + TILES] = np.arange(TILES)
    return c


class Chain:

    def __init__(self, sem):
        self.sem, self.n = sem, 0

    def __call__(self, eng, ins):
        self.n += 1
        ins.then_inc(self.sem, 1)
        eng.wait_ge(self.sem, self.n)


def xattn_ffn_kernel(nc, a, out):
    with ExitStack() as ctx:
        def sb(name, shape, dt=F32):
            return ctx.enter_context(nc.sbuf_tensor(name, shape, dt))

        def sem(name):
            return ctx.enter_context(nc.semaphore(name))

        psum = ctx.enter_context(nc.psum_tensor("psum", [P, 8, 512], F32))
        ps = [psum[:, n, :] for n in range(8)]

        X = sb("X", [P, B, RW])
        R2 = sb("R2", [P, B * D])
        R3 = sb("R3", [P, B * D])
        cst = sb("cst", [P, C_W])
        ident = cst[:, C_ID:C_ID + P]
        kT = sb("kT", [P, NC])
        qimg = sb("qimg", [P, NC], BF16)
        maskneg = sb("maskneg", [P, NC], BF16)
        work = sb("work", [P, 2 * PW + 2 * H * M])
        prob = [work[:, n * PW:(n + 1) * PW] for n in range(2)]
        kblk = [work[:, 2 * PW + n * H * M:2 * PW + (n + 1) * H * M] for n in range(2)]
        vm = [sb(f"vm{n}", [P, Q, D]) for n in range(2)]
        pts = [sb(f"pts{n}", [P, 512]) for n in range(2)]
        small = sb("small", [P, 12, P])
        raw = sb("raw", [P, 2048])
        tern = sb("tern", [P, 2176], BF16)
        sc = sb("sc", [P, 64])
        bcol = sb("bcol", [P, 16])
        brep = sb("brep", [P, 6, P])
        onesb = sb("onesb", [P, P], BF16)
        brow = sb("brow", [1, 3, P])
        bback = sb("bback", [1, 3, P])
        bsplit = sb("bsplit", [P, 3, P], BF16)
        identb = sb("identb", [P, P], BF16)
        warm = sb("warm", [P, 1])
        avgT = sb("avgT", [P, B])

        WQ, WK, WV, WO, WF, WI, WC, UF, UI, UC, WOF, UO = (small[:, n, :] for n in range(12))
        rawd = {"d2v": raw[0:CD, 0:128], "img": raw[:, 128:256], "txt": raw[:, 256:384],
                "att0": raw[:, 384:448], "att1": raw[:, 448:512],
                "f1": raw[:, 512:1536], "f2": raw[:, 1536:2048]}
        ternd = {"d2v": tern[0:CD, 0:128], "img": tern[:, 128:256], "txt": tern[:, 256:384],
                 "att0": tern[:, 384:512], "att1": tern[:, 512:640],
                 "f1": tern[:, 640:1664], "f2": tern[:, 1664:2176]}
        ctxT = R3[0:CD, 0:NC]
        V = R2[0:M, :]

        WSUM, WS, THR, NTHR = 0, 8, 16, 24
        AMAX, AALL, IS, INV, K_TMP, EPS5, EPS6, NHALF, K_TXT, K_A0, K_A1, S_IMG, K_F1, K_H, K_F2 = \
            range(32, 47)
        K_A = (K_A0, K_A1)
        B_F1 = 48

        def col(n, rows=P):
            return sc[0:rows, n:n + 1]

        s_load, s_ctx, s_x = sem("s_load"), sem("s_ctx"), sem("s_x")
        s_dve, s_act = sem("s_dve"), sem("s_act")
        s_tick = sem("s_tick")
        dlink = Chain(s_dve)
        s_allin, s_allout = sem("s_allin"), sem("s_allout")

        def quantum(dve, n):
            dve.wait_ge(s_allout, n)
            dlink(dve, dve.tensor_scalar(col(IS), col(AALL), 1e-8, 1.0 / 127.0, ALU.max, ALU.mult))
            dlink(dve, dve.reciprocal(col(INV), col(IS)))

        CH = 352
        NCH = NC // CH
        STREAMS = ("kT", "vis", "img")
        s_mask = sem("s_mask")
        s_bank = sem("s_bank")
        s_prod = sem("s_prod")
        s_quant = sem("s_quant")
        s_tern = sem("s_tern")
        s_kvis = sem("s_kvis")
        s_vprod, s_vbank = sem("s_vprod"), sem("s_vbank")
        s_wred, s_wsum = sem("s_wred"), sem("s_wsum")
        maskb = raw[:].bitcast(U8)[0:1, 0:NC]
        NLOAD = 1 + 12 + 3

        with nc.Block() as block:
            @block.sync
            def _(sp):
                sp.dma_start(maskb, a["mask"]).then_inc(s_mask, 16)
                sp.dma_start(ctxT, a["ctxT"]).then_inc(s_ctx, 16)
                sp.dma_start(cst[:], a["cst"]).then_inc(s_load, 16)
                for b in range(0, B, 16):
                    sp.dma_start(X[:, b:b + 16, 0:D], a["x"][b * S:(b + 16) * S, :]
                                 .rearrange("(b s) d -> s b d", s=S)).then_inc(s_x, 16)
                sp.wait_ge(s_mask, 17)
                for name in WEIGHTS:
                    dst, src = rawd[name], a["w_" + name]
                    if name in ("f1", "f2"):
                        k = src.shape[0] // P
                        dst = dst.rearrange("p (k n) -> p k n", k=k)
                        src = src.rearrange("(k p) n -> p k n", p=P)
                    sp.dma_start(dst, src).then_inc(s_tern, 16)
                sp.wait_ge(s_x, 16 * 4)

            @block.scalar
            def _(act):
                for n, name in enumerate(("wq", "wk", "wv", "wo", "wf", "wi", "wc", "uf", "ui", "uc",
                                          "wof", "uo")):
                    rows = CD if name in ("wk", "wv") else P
                    act.dma_start(small[0:rows, n, :], a[name]).then_inc(s_load, 16)
                act.dma_start(bcol[:], a["bcol"]).then_inc(s_load, 16)
                act.dma_start(brow[:], a["bgate"]).then_inc(s_load, 16)
                act.dma_start(brep[:], a["brow"].to_broadcast([P, 6, P])).then_inc(s_load, 16)
                act.wait_ge(s_load, 16 * NLOAD)
                act.activation(warm[:], bcol[:, 0:1], ACT.Exp).then_inc(s_act, 1)
                for n, name in enumerate(STREAMS):
                    if n:
                        act.wait_ge(s_kvis, n)
                    dst = kT if name == "kT" else work
                    with act.Fori(0, NCH // 2) as turn:
                        for u in range(2):
                            act.wait_ge(s_prod, turn * 2 + (n * NCH + u + 1))
                            act.activation(
                                dst[:, bass.ds((turn * 2 + u) * CH, CH)], ps[u][:, 0:CH],
                                ACT.Identity, bias=bcol[:, n - 1:n] if n else 0.0,
                                scale=col(K_TMP) if n else 1.0).then_inc(s_bank, 1)
                    if n == 0:
                        for g in range(NG):
                            act.wait_ge(s_vprod, g + 1)
                            act.copy(V[:, g * G4 * D:(g + 1) * G4 * D], ps[2 + g % 2][0:M, :]
                                     ).then_inc(s_vbank, 1)

            @block.gpsimd
            def _(pool):
                pool.wait_ge(s_allin, 1)
                pool.partition_all_reduce(col(AALL), col(AMAX), P, RMAX).then_inc(s_allout, 1)
                pool.wait_ge(s_wred, 1)
                pool.partition_all_reduce(sc[:, WS:WS + 8], sc[:, WSUM:WSUM + 8], P, RADD
                                          ).then_inc(s_wsum, 1)
                for n in (2, 3):
                    pool.wait_ge(s_allin, n)
                    pool.partition_all_reduce(col(AALL), col(AMAX), P, RMAX).then_inc(s_allout, 1)

            @block.tensor
            def _(pe):
                pe.wait_ge(s_load, 16 * NLOAD)
                pe.wait_ge(s_ctx, 16)
                pe.wait_ge(s_bank, 2)
                for n, (name, w) in enumerate((("kT", WK[0:CD]), ("vis", ternd["d2v"]),
                                               ("img", ternd["img"]))):
                    if n:
                        pe.wait_ge(s_quant, n)
                    src = ctxT if n == 0 else qimg[0:CD, :] if n == 1 else qimg
                    with pe.Fori(0, NCH // 2) as turn:
                        for u in range(2):
                            pe.wait_ge(s_bank, turn * 2 + (n * NCH + u + 1))
                            pe.matmul(ps[u][:, 0:CH], w, src[:, bass.ds((turn * 2 + u) * CH, CH)],
                                      start=True, stop=True).then_inc(s_prod, 1)
                    if n == 0:
                        for b in range(B):
                            g, j = divmod(b, G4)
                            if j == 0:
                                wait(pe, s_vbank, g - 1)
                            mm = pe.matmul(ps[2 + g % 2][0:M, j * D:(j + 1) * D],
                                           ctxT[:, b * M:(b + 1) * M], WV[0:CD], start=True, stop=True)
                            if j == G4 - 1:
                                mm.then_inc(s_vprod, 1)

            @block.vector
            def _(dve):
                dlink(dve, dve.memset(sc[:], 0.0))
                for t in (onesb, bsplit, maskneg, vm[0], vm[1]):
                    dve.memset(t[:], float(t is onesb)).then_inc(s_dve, 1)
                    dlink.n += 1
                dve.memset(col(EPS5), 1e-5).then_inc(s_bank, 1)
                dve.memset(col(EPS6), 1e-6).then_inc(s_bank, 1)
                dve.wait_ge(s_ctx, 16)
                dve.tensor_reduce(col(AMAX, CD), ctxT, AX.X, ALU.max,
                                  apply_absolute_value=True).then_inc(s_allin, 1)
                dlink(dve, dve.memset(col(NHALF), -0.5))
                dve.wait_ge(s_mask, 16)
                dve.tensor_scalar(maskneg[0:1, :], maskb, -1.0, BIG, ALU.add, ALU.mult
                                  ).then_inc(s_mask, 1)
                quantum(dve, 1)
                dlink(dve, dve.tensor_scalar(work[0:CD, 0:NC], ctxT, col(INV, CD), MAGIC,
                                             ALU.mult, ALU.add))
                dlink(dve, dve.tensor_scalar(qimg[0:CD, :], work[0:CD, 0:NC], MAGIC, None,
                                             ALU.subtract))
                dve.wait_ge(s_tern, 16 * len(WEIGHTS))
                for n, name in enumerate(WEIGHTS):
                    w = rawd[name]
                    dlink(dve, dve.tensor_reduce(sc[0:w.shape[0], WSUM + n:WSUM + n + 1], w, AX.X,
                                                 ALU.add, apply_absolute_value=True))
                dve.wait_ge(s_load, 16 * NLOAD)
                dve.tensor_copy(identb[:], ident).then_inc(s_wred, 1)
                dve.wait_ge(s_wsum, 1)
                dlink(dve, dve.tensor_tensor(sc[:, WS:WS + 7], sc[:, WS:WS + 7],
                                             cst[:, C_INV:C_INV + 7], ALU.mult))
                dlink(dve, dve.tensor_scalar(sc[:, WS:WS + 7], sc[:, WS:WS + 7], 1e-5, None, ALU.max))
                dve.tensor_tensor(col(K_TMP), col(IS), col(WS + 0), ALU.mult).then_inc(s_kvis, 1)
                dlink(dve, dve.tensor_scalar(sc[:, THR:THR + 7], sc[:, WS:WS + 7], 0.5, None, ALU.mult))
                dlink(dve, dve.tensor_scalar(sc[:, NTHR:NTHR + 7], sc[:, WS:WS + 7], -0.5, None,
                                             ALU.mult))
                for n, name in enumerate(WEIGHTS):
                    w, t = rawd[name], ternd[name]
                    r, c = w.shape
                    below = R3[0:r, NC:NC + c]
                    dlink(dve, dve.tensor_scalar(below, w, col(NTHR + n, r), None, ALU.is_lt))
                    for twice in range(t.shape[1] // c):
                        dlink(dve, dve.scalar_tensor_tensor(
                            out=t[:, twice * c:(twice + 1) * c], in0=w, scalar=col(THR + n, r),
                            in1=below, op0=ALU.is_gt, op1=ALU.subtract))
                dlink(dve, dve.tensor_scalar(small[:, 4:6, :], small[:, 4:6, :], 0.5, None, ALU.mult))
                dlink(dve, dve.tensor_scalar(small[:, 7:9, :], small[:, 7:9, :], 0.25, None, ALU.mult))
                dlink(dve, dve.tensor_scalar(small[:, 9:10, :], small[:, 9:10, :], 0.5, None, ALU.mult))
                dlink(dve, dve.tensor_scalar(small[:, 11:12, :], small[:, 11:12, :], 0.5, None,
                                             ALU.mult))
                dlink(dve, dve.tensor_scalar(brow[0:1, 0:2, :], brow[0:1, 0:2, :], 0.5, None,
                                             ALU.mult))
                for part in range(3):
                    rows = bsplit[32 * part:32 * part + 1, :, :]
                    dlink(dve, dve.tensor_copy(rows, brow[0:1, :, :]))
                    if part < 2:
                        dlink(dve, dve.tensor_copy(bback[0:1], rows))
                        dlink(dve, dve.tensor_tensor(brow[0:1, :, :], brow[0:1, :, :], bback[0:1],
                                                     ALU.subtract))
                dve.memset(work[:, NC:NC + 1], 0.0).then_inc(s_quant, 1)
                for n in (1, 2):
                    dve.wait_ge(s_bank, 2 + (n + 1) * NCH)
                    dve.tensor_reduce(col(AMAX), work[:, 0:NC], AX.X, ALU.max,
                                      apply_absolute_value=True).then_inc(s_allin, 1)
                    if n == 2:
                        dlink(dve, dve.tensor_reduce(
                            avgT[:], work[:, 0:NC].rearrange("p (b m) -> p b m", m=M), AX.X, ALU.add))
                        dlink(dve, dve.tensor_scalar(avgT[:], avgT[:], 1.0 / M, None, ALU.mult))
                    quantum(dve, n + 1)
                    if n == 1:
                        dve.tensor_tensor(col(K_TMP), col(IS), col(WS + 1), ALU.mult
                                          ).then_inc(s_kvis, 1)
                    dlink(dve, dve.tensor_scalar(work[:, 0:NC], work[:, 0:NC], col(INV), MAGIC,
                                                 ALU.mult, ALU.add))
                    dve.tensor_scalar(qimg[:], work[:, 0:NC], MAGIC, None, ALU.subtract
                                      ).then_inc(s_quant, 1)
                dlink(dve, dve.tensor_tensor(col(K_A0), col(IS), col(WS + 3), ALU.mult))
                dlink(dve, dve.tensor_tensor(col(K_A1), col(IS), col(WS + 4), ALU.mult))
                dlink(dve, dve.tensor_copy(col(S_IMG), col(AALL)))

        HX = R3
        xn = [sb(f"xn{n}", [P, D]) for n in range(2)]
        qT = [sb(f"qT{n}", [P, S]) for n in range(2)]
        xnT, x1n, x1nT = sb("xnT", [P, S]), sb("x1n", [P, D]), sb("x1nT", [P, S])
        attT, rrep = sb("attT", [P, S]), sb("rrep", [P, S])
        gate = sb("gate", [P, 3, S])
        state, keep, fresh = sb("state", [P, S]), sb("keep", [P, S]), sb("fresh", [P, S])
        peak = sb("peak", [P, Q, Q])
        total, rtot = sb("total", [P, H]), sb("rtot", [P, H])
        rwide = sb("rwide", [P, H, HD])
        stat1, stat2 = sb("stat1", [P, 6]), sb("stat2", [P, 6])
        mom1 = [sb(f"mom1_{n}", [P, 2]) for n in range(2)]
        mom2 = [sb(f"mom2_{n}", [P, 2]) for n in range(2)]
        rs1 = [sb(f"rs1_{n}", [P, 1]) for n in range(2)]
        rs2 = [sb(f"rs2_{n}", [P, 1]) for n in range(2)]
        ve1, ve2 = sb("ve1", [P, 1]), sb("ve2", [P, 1])
        QW = Q * M
        QSCALE = float(HD) ** -0.5
        bank_s, bank_t = ps[0:2], ps[2:4]
        bank_x, bank_o, bank_w, bank_g = ps[4], ps[6], ps[5], ps[7]

        names = ("stat1 mom1 ve1 rs1 xn xnp xnT qp q kb vm score peak sub exp pt pte pv total rtot rp "
                 "rwide rrep att wo x1 stat2 mom2 ve2 rs2 x1n x1p x1nT gates tanh hx mix state")
        e = {n: sem("e_" + n) for n in names.split()}

        def cols(b):
            return bass.ds(b * D, D)

        Xf = X[:].rearrange("p b w -> p (b w)")

        def row(b):
            return Xf[:, bass.ds(b * RW, D)]

        def rows4(g):
            return Xf[:, bass.ds(g * (G4 * RW), G4 * RW)].rearrange("p (j w) -> p j w", j=G4)[:, :, 0:D]

        with nc.Block() as block:
            @block.vector
            def _(dve):
                dlink(dve, dve.memset(prob[0][:, H * M:PW], 0.0))
                dlink(dve, dve.memset(prob[1][:, H * M:PW], 0.0))
                dve.memset(state[:], 0.0).then_inc(e["mix"], 2)
                dve.wait_ge(e["mix"], 2)
                dve.tensor_scalar(state[:], state[:], 1.0, bcol[:, 9:10], ALU.mult, ALU.add
                                  ).then_inc(e["mix"], 1)
                dve.wait_ge(e["mix"], 3)
                dve.tensor_scalar(state[:], state[:], 2.0, None, ALU.mult).then_inc(e["state"], 1)
                MIX0 = 3

                def body(i, par, live):
                    b0, b1, b2, b3, b4 = (i - n for n in range(5))
                    odd = 1 - par
                    if live(0):
                        wait(dve, e["mom1"], b0)
                        dve.sem_inc(s_tick, 1)
                        dve.bn_stats(stat1[:], row(b0)).then_inc(e["stat1"], 1)
                        dve.wait_ge(e["stat1"], b0 + 1)
                        wait(dve, e["xn"], b0 - 1)
                        dve.sem_inc(s_tick, 1)
                        dve.bn_aggr(mom1[par][:], stat1[:]).then_inc(e["mom1"], 1)
                    if live(1):
                        dve.wait_ge(e["rs1"], b1 + 1)
                        wait(dve, e["xnp"], b1 - 1)
                        dve.tensor_scalar(xn[odd][:], row(b1), mom1[odd][:, 0:1], rs1[odd][:],
                                          ALU.subtract, ALU.mult).then_inc(e["xn"], 1)
                    if live(4):
                        dve.wait_ge(e["rs2"], b4 + 1)
                        wait(dve, e["x1p"], b4)
                        dve.tensor_scalar(x1n[:], row(b4), mom2[par][:, 0:1], rs2[par][:],
                                          ALU.subtract, ALU.mult).then_inc(e["x1n"], 1)
                    if live(3):
                        dve.wait_ge(e["exp"], b3 * 2 + 2)
                        wait(dve, e["rtot"], b3)
                        dve.tensor_reduce(
                            total[:].rearrange("p (g q) -> p q g", q=Q),
                            prob[odd][:, 0:H * M].rearrange("p (q g m) -> p q g m", q=Q, g=Q),
                            AX.X, ALU.add).then_inc(e["total"], 1)
                        dve.wait_ge(e["total"], b3 + 1)
                        wait(dve, e["rwide"], b3)
                        dve.reciprocal(rtot[:], total[:]).then_inc(e["rtot"], 1)
                    if live(2):
                        wait(dve, e["pt"], b2 * 4 - 4)
                        for q in range(Q):
                            s4 = bank_s[q % 2][:, 0:QW].rearrange("p (g m) -> p g m", g=Q)
                            dve.wait_ge(e["score"], b2 * 4 + (q + 1))
                            wait(dve, e["sub"], b2 * 4 + (q - 3))
                            dve.tensor_reduce(peak[:, q, :], s4, AX.X, ALU.max).then_inc(e["peak"], 1)
                            dve.wait_ge(e["peak"], b2 * 4 + (q + 1))
                            dve.tensor_tensor(
                                prob[par][:, q * QW:(q + 1) * QW].rearrange("p (g m) -> p g m", g=Q),
                                s4, peak[:, q, :, None].to_broadcast([P, Q, M]), ALU.subtract
                                ).then_inc(e["sub"], 1)
                    if live(3):
                        dve.wait_ge(e["pv"], b3 * 4 + 4)
                        dve.wait_ge(e["rrep"], b3 + 1)
                        wait(dve, e["wo"], b3)
                        dve.tensor_tensor(attT[:], bank_o[:, 0:S], rrep[:], ALU.mult
                                          ).then_inc(e["att"], 1)
                        dve.wait_ge(e["wo"], b3 + 1)
                        dve.tensor_tensor(row(b3), row(b3), bank_w[:, 128:256], ALU.add
                                          ).then_inc(e["x1"], 1)
                        dve.wait_ge(e["x1"], b3 + 1)
                        wait(dve, e["mom2"], b3)
                        dve.sem_inc(s_tick, 1)
                        dve.bn_stats(stat2[:], row(b3)).then_inc(e["stat2"], 1)
                        dve.wait_ge(e["stat2"], b3 + 1)
                        wait(dve, e["x1n"], b3 - 1)
                        dve.sem_inc(s_tick, 1)
                        dve.bn_aggr(mom2[odd][:], stat2[:]).then_inc(e["mom2"], 1)
                    if live(4):
                        dve.wait_ge(e["tanh"], b4 + 1)
                        dve.wait_ge(e["state"], b4 + 1)
                        dve.scalar_tensor_tensor(out=keep[:], in0=gate[:, 0, :], scalar=1.0,
                                                 in1=state[:], op0=ALU.add, op1=ALU.mult
                                                 ).then_inc(e["mix"], 1)
                        dve.scalar_tensor_tensor(out=fresh[:], in0=gate[:, 1, :], scalar=1.0,
                                                 in1=gate[:, 2, :], op0=ALU.add, op1=ALU.mult
                                                 ).then_inc(e["mix"], 1)
                        dve.wait_ge(e["mix"], b4 * 2 + (2 + MIX0))
                        dve.scalar_tensor_tensor(out=state[:], in0=keep[:], scalar=0.5,
                                                 in1=fresh[:], op0=ALU.mult, op1=ALU.add
                                                 ).then_inc(e["state"], 1)

                batches(dve, 5, body)

            @block.scalar
            def _(act):
                act.activation(warm[:], bcol[:, 0:1], ACT.Exp).then_inc(s_act, 1)

                def body(i, par, live):
                    b1, b2, b3, b4 = (i - n for n in range(1, 5))
                    odd = 1 - par

                    def turned(q):
                        act.wait_ge(e["pt"], b3 * 4 + (q + 1))
                        wait(act, e["pv"], b3 * 4 + (q - 1))
                        act.copy(pts[q % 2][:], bank_t[q % 2][:]).then_inc(e["pte"], 1)

                    def exponentials(half):
                        act.wait_ge(e["sub"], b2 * 4 + (2 * half + 2))
                        part = prob[par][:, 2 * half * QW:(2 * half + 2) * QW]
                        act.activation(part, part, ACT.Exp).then_inc(e["exp"], 1)

                    if live(1):
                        act.wait_ge(e["xnp"], b1 + 1)
                        wait(act, e["qp"], b1)
                        act.copy(xnT[:], bank_x[:, 0:128]).then_inc(e["xnT"], 1)
                        act.wait_ge(e["qp"], b1 + 1)
                        wait(act, e["score"], b1 * 4 - 4)
                        act.activation(qT[odd][:], bank_x[:, 128:256], ACT.Copy, scale=QSCALE
                                       ).then_inc(e["q"], 1)
                    if live(4):
                        act.wait_ge(e["x1p"], b4 + 1)
                        wait(act, e["gates"], b4)
                        act.copy(x1nT[:], bank_x[:, 256:384]).then_inc(e["x1nT"], 1)
                    if live(3):
                        turned(0)
                        act.wait_ge(e["rtot"], b3 + 1)
                        wait(act, e["rp"], b3)
                        act.copy(rwide[:], rtot[:, :, None].to_broadcast([P, H, HD])
                                 ).then_inc(e["rwide"], 1)
                        turned(1)
                    if live(2):
                        exponentials(0)
                    if live(3):
                        turned(2)
                        act.wait_ge(e["rp"], b3 + 1)
                        wait(act, e["att"], b3)
                        act.copy(rrep[:], bank_w[:, 0:128]).then_inc(e["rrep"], 1)
                        turned(3)
                    if live(4):
                        act.wait_ge(e["gates"], b4 + 1)
                        wait(act, e["mix"], b4 * 2 + 3)
                        act.activation(gate[:], bank_g[:, 0:384].rearrange("p (g s) -> p g s", g=3),
                                       ACT.Tanh).then_inc(e["tanh"], 1)
                        act.copy(HX[:, cols(b4)], bank_g[:, 384:512]).then_inc(e["hx"], 1)
                    if live(2):
                        exponentials(1)

                batches(act, 5, body)

            @block.gpsimd
            def _(pool):
                def body(i, par, live):
                    b0, b1, b2, b3 = (i - n for n in range(4))
                    odd = 1 - par
                    if live(0):
                        pool.wait_ge(e["mom1"], b0 + 1)
                        wait(pool, e["rs1"], b0)
                        pool.tensor_tensor(ve1[:], mom1[par][:, 1:2], col(EPS5), ALU.add
                                           ).then_inc(e["ve1"], 1)
                        pool.wait_ge(e["ve1"], b0 + 1)
                        wait(pool, e["xn"], b0 - 1)
                        pool.tensor_tensor(rs1[par][:], ve1[:], col(NHALF), ALU.pow
                                           ).then_inc(e["rs1"], 1)
                    if live(1):
                        wait(pool, e["score"], b1 * 4 - 4)
                        pool.tensor_tensor(
                            kblk[odd].rearrange("p (h m) -> p h m", m=M),
                            kT[:, None, bass.ds(b1 * M, M)].to_broadcast([P, H, M]),
                            cst[:, C_KM:C_KM + H, None].to_broadcast([P, H, M]), ALU.mult
                            ).then_inc(e["kb"], 1)
                    if live(3):
                        pool.wait_ge(e["mom2"], b3 + 1)
                        wait(pool, e["rs2"], b3)
                        pool.tensor_tensor(ve2[:], mom2[odd][:, 1:2], col(EPS5), ALU.add
                                           ).then_inc(e["ve2"], 1)
                        pool.wait_ge(e["ve2"], b3 + 1)
                        wait(pool, e["x1n"], b3 - 1)
                        pool.tensor_tensor(rs2[odd][:], ve2[:], col(NHALF), ALU.pow
                                           ).then_inc(e["rs2"], 1)
                    if live(2):
                        wait(pool, e["pv"], b2 * 4 - 4)
                        pool.tensor_tensor(
                            vm[par][0:M], V[:, None, cols(b2)].to_broadcast([M, Q, D]),
                            cst[0:M, C_VM:C_VM + Q * D].rearrange("p (q d) -> p q d", q=Q), ALU.mult
                            ).then_inc(e["vm"], 1)

                batches(pool, 5, body)

            @block.tensor
            def _(pe):
                def body(i, par, live):
                    b1, b2, b3, b4 = (i - n for n in range(1, 5))
                    odd = 1 - par

                    def scores(q):
                        bank = bank_s[q % 2][:, 0:QW]
                        wait(pe, e["sub"], b2 * 4 + (q - 1))
                        pe.matmul(bank.rearrange("p (g m) -> p g m", g=Q), onesb[:],
                                  maskneg[:, None, bass.ds(b2 * M, M)].to_broadcast([P, Q, M]),
                                  start=True, stop=False)
                        pe.matmul(bank, qT[par][:], kblk[par][:, q * QW:(q + 1) * QW],
                                  start=False, stop=True).then_inc(e["score"], 1)

                    def turn(q):
                        wait(pe, e["pte"], b3 * 4 + (q - 1))
                        for g in range(Q):
                            at = (Q * q + g) * M
                            mm = pe.transpose(bank_t[q % 2][:, g * S:(g + 1) * S],
                                              prob[odd][:, at:at + P], ident)
                        mm.then_inc(e["pt"], 1)

                    def values(q):
                        pe.wait_ge(e["pte"], b3 * 4 + (q + 1))
                        for g in range(Q):
                            mm = pe.matmul(bank_o[32 * g:32 * g + 32, 0:S],
                                           vm[odd][:, q, 32 * g:32 * g + 32],
                                           pts[q % 2][:, g * S:(g + 1) * S],
                                           start=(q == 0), stop=(q == Q - 1))
                        mm.then_inc(e["pv"], 1)

                    if live(1):
                        pe.wait_ge(e["xn"], b1 + 1)
                        wait(pe, e["q"], b1)
                        wait(pe, e["x1nT"], i - 4)
                        pe.transpose(bank_x[:, 0:128], xn[odd][:], ident).then_inc(e["xnp"], 1)
                    if live(2):
                        pe.wait_ge(e["kb"], b2 + 1)
                        pe.wait_ge(e["q"], b2 + 1)
                        scores(0)
                        scores(1)
                    if live(1):
                        pe.wait_ge(e["xnT"], b1 + 1)
                        pe.matmul(bank_x[:, 128:256], WQ, xnT[:], start=True, stop=True
                                  ).then_inc(e["qp"], 1)
                    if live(3):
                        pe.wait_ge(e["exp"], b3 * 2 + 2)
                        turn(0)
                        turn(1)
                    if live(4):
                        pe.wait_ge(e["x1n"], b4 + 1)
                        if live(1):
                            pe.wait_ge(e["q"], b1 + 1)
                        pe.transpose(bank_x[:, 256:384], x1n[:], ident).then_inc(e["x1p"], 1)
                    if live(2):
                        scores(2)
                    if live(3):
                        wait(pe, e["att"], b3)
                        pe.wait_ge(e["vm"], b3 + 1)
                        values(0)
                        turn(2)
                        values(1)
                    if live(2):
                        scores(3)
                    if live(3):
                        turn(3)
                        pe.wait_ge(e["rwide"], b3 + 1)
                        wait(pe, e["x1"], b3)
                        pe.matmul(bank_w[:, 0:128], rwide[:].rearrange("p h d -> p (h d)"), ident,
                                  start=True, stop=True).then_inc(e["rp"], 1)
                        values(2)
                    if live(4):
                        pe.wait_ge(e["x1nT"], b4 + 1)
                        wait(pe, e["tanh"], b4)
                        wait(pe, e["hx"], b4)
                        for n in range(3):
                            pe.matmul(bank_g[:, n * S:(n + 1) * S], bsplit[:, n, :], onesb[:],
                                      start=(n == 0), stop=False, skip_group_check=True)
                        for n, w in enumerate((WF, WI, WC)):
                            pe.matmul(bank_g[:, n * S:(n + 1) * S], w, x1nT[:], start=False,
                                      stop=False, skip_group_check=True)
                        pe.matmul(bank_g[:, 384:512], x1nT[:], WOF, start=False, stop=False,
                                  skip_group_check=True)
                        pe.wait_ge(e["state"], b4 + 1)
                        for n, w in enumerate((UF, UI, UC)):
                            mm = pe.matmul(bank_g[:, n * S:(n + 1) * S], w, state[:], start=False,
                                           stop=(n == 2), skip_group_check=True)
                        mm.then_inc(e["gates"], 1)
                    if live(3):
                        values(3)
                        pe.wait_ge(e["att"], b3 + 1)
                        pe.matmul(bank_w[:, 128:256], attT[:], WO, start=True, stop=True
                                  ).then_inc(e["wo"], 1)

                batches(pe, 5, body)

        GW = G4 * D
        cfin = sb("cfin", [P, D])
        mom3 = [sb(f"mom3_{n}", [P, G4, 2]) for n in range(2)]
        stat3 = sb("stat3", [P, G4, 6])
        ve3, rs3 = sb("ve3", [P, G4]), [sb(f"rs3_{n}", [P, G4]) for n in range(2)]
        shift3 = [sb(f"shift3_{n}", [P, G4]) for n in range(2)]
        mags = sb("mags", [P, NG])
        f = {n: sem("f_" + n) for n in "cf cfin pre tanh x2 stat mom ve rs shift ln mag".split()}

        def group(t, g):
            return t[:, bass.ds(g * GW, GW)]

        def four(ap):
            return ap.rearrange("p (j d) -> p j d", j=G4)

        with nc.Block() as block:
            @block.tensor
            def _(pe):
                pe.matmul(ps[0][:, 0:D], state[:], UO, start=True, stop=True).then_inc(f["cf"], 1)

            @block.vector
            def _(dve):
                dve.wait_ge(f["cf"], 1)
                dve.tensor_tensor(cfin[:], ps[0][:, 0:D], brep[:, 0, :], ALU.add
                                  ).then_inc(f["cfin"], 1)
                dve.wait_ge(f["cfin"], 1)

                def body(i, par, live):
                    odd = 1 - par
                    if live(0):
                        dve.tensor_tensor(four(group(HX, i)), four(group(HX, i)),
                                          cfin[:, None, :].to_broadcast([P, G4, D]), ALU.add
                                          ).then_inc(f["pre"], 1)
                    if live(1):
                        g = i - 1
                        dve.wait_ge(f["x2"], g + 1)
                        wait(dve, f["mom"], g * G4)
                        for j in range(G4):
                            dve.sem_inc(s_tick, 1)
                            dve.bn_stats(stat3[:, j, :], row(g * G4 + j)
                                         ).then_inc(f["stat"], 1)
                        dve.wait_ge(f["stat"], g * G4 + G4)
                        wait(dve, f["ln"], g - 1)
                        for j in range(G4):
                            dve.sem_inc(s_tick, 1)
                            dve.bn_aggr(mom3[odd][:, j, :], stat3[:, j, :]).then_inc(f["mom"], 1)
                    if live(2):
                        g = i - 2
                        dve.wait_ge(f["rs"], g + 1)
                        wait(dve, f["ln"], g - 1)
                        dve.scalar_tensor_tensor(
                            out=shift3[par][:], in0=mom3[par][:, :, 0], scalar=-1.0,
                            in1=rs3[par][:], op0=ALU.mult, op1=ALU.mult).then_inc(f["shift"], 1)
                    if live(4):
                        g = i - 4
                        dve.wait_ge(f["ln"], g + 1)
                        dve.tensor_reduce(mags[:, bass.ds(g, 1)], group(R3, g), AX.X, ALU.max,
                                          apply_absolute_value=True).then_inc(f["mag"], 1)

                batches(dve, 5, body, NG)
                dve.wait_ge(f["mag"], NG)
                dve.tensor_reduce(col(AMAX), mags[:], AX.X, ALU.max).then_inc(s_allin, 1)
                quantum(dve, 4)
                dlink(dve, dve.tensor_tensor(col(K_TXT), col(IS), col(WS + 2), ALU.mult))

            @block.scalar
            def _(act):
                act.activation(warm[:], bcol[:, 0:1], ACT.Exp).then_inc(s_act, 1)

                def body(i, par, live):
                    if live(0):
                        act.wait_ge(f["pre"], i + 1)
                        act.activation(group(HX, i), group(HX, i), ACT.Tanh).then_inc(f["tanh"], 1)
                    if live(3):
                        g = i - 3
                        act.wait_ge(f["shift"], g + 1)
                        for j in range(G4):
                            ins = act.activation(
                                R3[:, bass.ds((g * G4 + j) * D, D)], row(g * G4 + j),
                                ACT.Identity, bias=shift3[1 - par][:, j:j + 1],
                                scale=rs3[1 - par][:, j:j + 1])
                        ins.then_inc(f["ln"], 1)

                batches(act, 5, body, NG)

            @block.gpsimd
            def _(pool):
                def body(i, par, live):
                    if live(0):
                        pool.wait_ge(f["tanh"], i + 1)
                        pool.tensor_tensor(rows4(i), rows4(i), four(group(HX, i)), ALU.add
                                           ).then_inc(f["x2"], 1)
                    if live(2):
                        g = i - 2
                        pool.wait_ge(f["mom"], g * G4 + G4)
                        wait(pool, f["rs"], g)
                        pool.tensor_tensor(ve3[:], mom3[par][:, :, 1], col(EPS5).to_broadcast([P, G4]),
                                           ALU.add).then_inc(f["ve"], 1)
                        pool.wait_ge(f["ve"], g + 1)
                        wait(pool, f["ln"], g - 1)
                        pool.tensor_tensor(rs3[par][:], ve3[:], col(NHALF).to_broadcast([P, G4]),
                                           ALU.pow).then_inc(f["rs"], 1)

                batches(pool, 5, body, NG)
                pool.wait_ge(s_allin, 4)
                pool.partition_all_reduce(col(AALL), col(AMAX), P, RMAX).then_inc(s_allout, 1)

        FT = R2
        MW = G4 * M
        EW = MW + (P - M) + 1
        ISE = float(D) ** -0.5
        used = {"work": 0, "kT": 0, "maskneg": 0}
        room = {"work": work[:], "kT": kT[:], "maskneg": maskneg[:].bitcast(F32)}

        def lend(width, dt=F32):
            words = -(-width * 2 // 4) if dt == BF16 else width
            for name, tile in room.items():
                at = used[name]
                if at + words <= tile.shape[1]:
                    used[name] += words
                    t = tile[:, at:at + words]
                    return t.bitcast(dt)[:, 0:width] if dt != F32 else t
            raise AssertionError("no room")

        tq = lend(GW)
        qx = [lend(GW, BF16) for n in range(2)]
        qxT = lend(GW, BF16)
        fus = [[lend(GW) for n in range(4)], [vm[n][:].rearrange("p q d -> p (q d)") for n in range(2)]
               + [pts[n][:] for n in range(2)]]
        kx = [lend(MW) for n in range(2)]
        kp = [lend(2 * GW).rearrange("p (t c) -> p t c", t=2) for n in range(2)]
        p3 = [[lend(EW) for t in range(2)] for n in range(2)]
        p3T = [lend(GW) for n in range(2)]
        mx = [sb(f"mx{n}", [P, G4]) for n in range(2)]
        sm = [sb(f"sm{n}", [P, G4]) for n in range(2)]
        rc = [sb(f"rc{n}", [P, G4]) for n in range(2)]
        b01 = sb("b01", [P, 2])
        LAY = ("a", "b")
        h = {n: sem("h_" + n) for n in "tq qx qp qT fp fused done mag".split()}
        for n in "kp_ kx kv_ kv score peak sub exp sum rec norm pt pte out add".split():
            for l in LAY:
                h[n + l] = sem("h_" + n + l)

        with nc.Block() as block:
            @block.vector
            def _(dve):
                for n in range(2):
                    dlink(dve, dve.memset(kp[n], 0.0))
                    for t in range(2):
                        dlink(dve, dve.memset(p3[n][t][:, MW:EW], 0.0))
                dlink(dve, dve.tensor_scalar(b01[:], bcol[:, 3:5], 0.1, None, ALU.mult))
                dve.memset(sm[0][:], 0.0).then_inc(h["done"], 1)

                def softmax(l, g, ph):
                    L, p = LAY[l], p3[l][ph % 2][:, 0:MW].rearrange("p (j m) -> p j m", m=M)
                    s4 = ps[3][:, 0:MW].rearrange("p (j m) -> p j m", m=M)
                    dve.wait_ge(h["score" + L], g + 1)
                    wait(dve, h["sub" + L], g)
                    dve.tensor_reduce(mx[l][:], s4, AX.X, ALU.max).then_inc(h["peak" + L], 1)
                    dve.wait_ge(h["peak" + L], g + 1)
                    wait(dve, h["pt" + L], g - 1)
                    dve.tensor_tensor(p, s4, mx[l][:, :, None].to_broadcast([P, G4, M]), ALU.subtract
                                      ).then_inc(h["sub" + L], 1)

                def normalise(l, g, ph):
                    L, p = LAY[l], p3[l][ph % 2][:, 0:MW].rearrange("p (j m) -> p j m", m=M)
                    dve.wait_ge(h["exp" + L], g + 1)
                    wait(dve, h["rec" + L], g)
                    dve.tensor_reduce(sm[l][:], p, AX.X, ALU.add).then_inc(h["sum" + L], 1)
                    dve.wait_ge(h["sum" + L], g + 1)
                    wait(dve, h["norm" + L], g)
                    dve.reciprocal(rc[l][:], sm[l][:]).then_inc(h["rec" + L], 1)
                    dve.wait_ge(h["rec" + L], g + 1)
                    dve.scalar_tensor_tensor(
                        out=p, in0=p, scalar=0.1, in1=rc[l][:, :, None].to_broadcast([P, G4, M]),
                        op0=ALU.mult, op1=ALU.mult).then_inc(h["norm" + L], 1)

                def body(i, ph, live):
                    g0, g1, g2, g3, g4, g5 = (i - n for n in range(6))
                    if live(0):
                        dve.wait_ge(h["tq"], g0 + 1)
                        wait(dve, h["qp"], g0 - 1)
                        dve.tensor_scalar(qx[ph % 2], tq, MAGIC, None, ALU.subtract
                                          ).then_inc(h["qx"], 1)
                    if live(2):
                        softmax(0, g2, ph)
                    if live(4):
                        softmax(1, g4, ph)
                    if live(3):
                        dve.wait_ge(h["outa"], g3 + 1)
                        wait(dve, h["adda"], g3 - 3)
                        wait(dve, h["addb"], g3 - 3)
                        dve.scalar_tensor_tensor(out=fus[1][(ph + 1) % 4], in0=ps[6][:],
                                                 scalar=b01[:, 0:1], in1=fus[0][(ph + 1) % 4],
                                                 op0=ALU.add, op1=ALU.add).then_inc(h["adda"], 1)
                    if live(5):
                        dve.wait_ge(h["outb"], g5 + 1)
                        dve.scalar_tensor_tensor(out=group(FT, g5), in0=ps[6][:],
                                                 scalar=b01[:, 1:2], in1=fus[1][(ph + 3) % 4],
                                                 op0=ALU.add, op1=ALU.add).then_inc(h["addb"], 1)
                    if live(2):
                        normalise(0, g2, ph)
                    if live(4):
                        normalise(1, g4, ph)
                    if live(5):
                        dve.wait_ge(h["addb"], g5 + 1)
                        dve.tensor_reduce(mags[:, bass.ds(g5, 1)], group(FT, g5), AX.X, ALU.max,
                                          apply_absolute_value=True).then_inc(h["mag"], 1)

                batches(dve, 6, body, NG, 4)

            @block.scalar
            def _(act):
                act.activation(warm[:], bcol[:, 0:1], ACT.Exp).then_inc(s_act, 1)
                act.wait_ge(h["done"], 1)

                def keys(l, g, ph):
                    L = LAY[l]
                    act.wait_ge(h["kp_" + L], g + 1)
                    wait(act, h["score" + L], g)
                    act.activation(kx[l], ps[2][:, 0:MW], ACT.Identity,
                                   bias=bcol[:, 3 + l:4 + l], scale=col(K_A[l])
                                   ).then_inc(h["kx" + L], 1)
                    act.wait_ge(h["kv_" + L], g + 1)
                    wait(act, h["out" + L], g - 1)
                    act.activation(kp[l][0:M, ph % 2, :], ps[4][0:M, :], ACT.Copy,
                                   scale=col(K_A[l], M)).then_inc(h["kv" + L], 1)

                def exponential(l, g, ph):
                    L, p = LAY[l], p3[l][ph % 2][:, 0:MW]
                    act.wait_ge(h["sub" + L], g + 1)
                    act.activation(p, p, ACT.Exp, scale=ISE).then_inc(h["exp" + L], 1)

                def turned(l, g, ph):
                    L = LAY[l]
                    act.wait_ge(h["pt" + L], g + 1)
                    wait(act, h["out" + L], g)
                    act.copy(p3T[l], ps[5][:]).then_inc(h["pte" + L], 1)

                def body(i, ph, live):
                    g0, g1, g2, g3, g4, g5 = (i - n for n in range(6))
                    if live(1):
                        act.wait_ge(h["qp"], g1 + 1)
                        wait(act, h["fp"], g1)
                        act.copy(qxT, ps[0][:].bitcast(BF16)[:, 0:GW]).then_inc(h["qT"], 1)
                        act.wait_ge(h["fp"], g1 + 1)
                        wait(act, h["adda"], g1 - 3)
                        act.activation(fus[0][(ph + 3) % 4], ps[1][:], ACT.Identity,
                                       bias=bcol[:, 2:3], scale=col(K_TXT)).then_inc(h["fused"], 1)
                    if live(0):
                        wait(act, h["qx"], g0)
                        act.activation(tq, group(R3, g0), ACT.Copy, bias=MAGIC, scale=col(INV)
                                       ).then_inc(h["tq"], 1)
                    if live(2):
                        keys(0, g2, ph)
                    if live(3):
                        turned(0, g3, ph)
                    if live(4):
                        keys(1, g4, ph)
                    if live(5):
                        turned(1, g5, ph)
                    if live(2):
                        exponential(0, g2, ph)
                    if live(4):
                        exponential(1, g4, ph)

                batches(act, 6, body, NG, 4)

            @block.tensor
            def _(pe):
                pe.wait_ge(h["done"], 1)
                tb = ps[0][:].bitcast(BF16)

                def keys(l, g):
                    L, w = LAY[l], ternd["att" + str(l)]
                    pe.matmul(ps[2][:, 0:MW], w, qimg[:, bass.ds(g * MW, MW)], start=True, stop=True
                              ).then_inc(h["kp_" + L], 1)
                    for j in range(G4):
                        mm = pe.matmul(ps[4][0:M, j * D:(j + 1) * D],
                                       qimg[:, bass.ds((g * G4 + j) * M, M)], w, start=True, stop=True)
                    mm.then_inc(h["kv_" + L], 1)

                def scores(l, g, ph):
                    L = LAY[l]
                    pe.wait_ge(h["kx" + L], g + 1)
                    for j in range(G4):
                        mm = pe.matmul(ps[3][:, j * M:(j + 1) * M], fus[l][ph][:, j * S:(j + 1) * S],
                                       kx[l][:, j * M:(j + 1) * M], start=True, stop=True)
                    mm.then_inc(h["score" + L], 1)

                def turn(l, g, ph):
                    L = LAY[l]
                    pe.wait_ge(h["norm" + L], g + 1)
                    for j in range(G4):
                        mm = pe.transpose(ps[5][:, j * S:(j + 1) * S],
                                          p3[l][ph % 2][:, j * M:j * M + P], ident)
                    mm.then_inc(h["pt" + L], 1)

                def values(l, g, ph):
                    L = LAY[l]
                    pe.wait_ge(h["pte" + L], g + 1)
                    for j in range(G4):
                        mm = pe.matmul(ps[6][:, j * S:(j + 1) * S],
                                       kp[l][:, ph % 2, j * D:(j + 1) * D],
                                       p3T[l][:, j * S:(j + 1) * S], start=True, stop=True)
                    mm.then_inc(h["out" + L], 1)

                def upto(n):
                    return min(n, NG) if isinstance(n, int) else n

                def body(i, ph, live):
                    g0, g1, g2, g3, g4, g5 = (i - n for n in range(6))
                    if live(1):
                        pe.wait_ge(h["qT"], g1 + 1)
                        wait(pe, h["fused"], g1)
                        pe.matmul(ps[1][:], ternd["txt"], qxT, start=True, stop=True
                                  ).then_inc(h["fp"], 1)
                    if live(0):
                        pe.wait_ge(h["qx"], g0 + 1)
                        wait(pe, h["qT"], g0)
                        for j in range(G4):
                            mm = pe.transpose(tb[:, j * S:(j + 1) * S],
                                              qx[ph % 2][:, j * D:(j + 1) * D], identb[:])
                        mm.then_inc(h["qp"], 1)
                    if live(2):
                        wait(pe, h["kvb"], g2 - 2)
                        wait(pe, h["kxb"], g2 - 2)
                        keys(0, g2)
                    if live(3):
                        wait(pe, h["pteb"], g3 - 2)
                        turn(0, g3, (ph + 1) % 4)
                    if live(2):
                        pe.wait_ge(h["fused"], g2 + 1)
                        wait(pe, h["subb"], g2 - 2)
                        scores(0, g2, (ph + 2) % 4)
                    if live(4):
                        pe.wait_ge(h["kxa"], upto(g4 + 3))
                        pe.wait_ge(h["kva"], upto(g4 + 3))
                        keys(1, g4)
                    if live(3):
                        wait(pe, h["addb"], g3 - 2)
                        values(0, g3, (ph + 1) % 4)
                    if live(5):
                        pe.wait_ge(h["ptea"], upto(g5 + 3))
                        turn(1, g5, (ph + 3) % 4)
                    if live(4):
                        pe.wait_ge(h["suba"], upto(g4 + 3))
                        pe.wait_ge(h["adda"], g4 + 1)
                        scores(1, g4, ph)
                    if live(5):
                        pe.wait_ge(h["adda"], upto(g5 + 3))
                        values(1, g5, (ph + 3) % 4)

                batches(pe, 6, body, NG, 4)

        for n in used:
            used[n] = 0
        qf = R3[:].bitcast(BF16)
        qavg = lend(B, BF16)
        tq = [lend(GW) for n in range(2)]
        hpk = lend(NG * 4)
        hm = lend(4)
        f1w = ternd["f1"].rearrange("p (k n) -> p k n", k=2)
        f2w = ternd["f2"].rearrange("p (k n) -> p k n", k=4)
        m = {n: sem("m_" + n) for n in "qavg tq qf f1 peak b2 blank fill".split()}
        blank = sb("blank", [P, RW])
        sorted_rows = nc.dram_tensor("sorted_rows", (SORTED, RW), F32, kind="Internal").ap()

        def hidden(pe, bank, g, c):
            pe.matmul(bank, f1w[:, 0, c * P:(c + 1) * P], group(qf, g), start=True, stop=False)
            return pe.matmul(four(bank), f1w[:, 1, c * P:(c + 1) * P],
                             qavg[:, bass.ds(g * G4, G4), None].to_broadcast([P, G4, S]),
                             start=False, stop=True)

        with nc.Block() as block:
            @block.sync
            def _(sp):
                sp.wait_ge(m["blank"], 2)
                sp.dma_start(sorted_rows.rearrange("(p k) w -> p k w", p=P),
                             blank[:, None, :].to_broadcast([P, SORTED // P, RW])
                             ).then_inc(m["fill"], 16)
                sp.wait_ge(m["fill"], 16)

            @block.vector
            def _(dve):
                dlink(dve, dve.tensor_reduce(hm[:, 0:1], mags[:], AX.X, ALU.max))
                dlink(dve, dve.tensor_reduce(hm[:, 1:2], avgT[:], AX.X, ALU.max,
                                             apply_absolute_value=True))
                dve.tensor_tensor(col(AMAX), hm[:, 0:1], hm[:, 1:2], ALU.max).then_inc(s_allin, 1)
                quantum(dve, 5)
                dlink(dve, dve.tensor_tensor(col(K_F1), col(IS), col(WS + 5), ALU.mult))
                dlink(dve, dve.tensor_scalar(avgT[:], avgT[:], col(INV), MAGIC, ALU.mult, ALU.add))
                dve.tensor_scalar(qavg, avgT[:], MAGIC, None, ALU.subtract).then_inc(m["qavg"], 1)

                def body(i, par, live):
                    if live(0):
                        dve.wait_ge(m["tq"], i + 1)
                        dve.tensor_scalar(group(qf, i), tq[par], MAGIC, None, ALU.subtract
                                          ).then_inc(m["qf"], 1)
                    if live(1):
                        g = i - 1
                        dve.wait_ge(m["f1"], g + 1)
                        dve.tensor_reduce(hpk[:, bass.ds(g * 4, 4)],
                                          psum[:, 4 * (1 - par):4 * (1 - par) + 4, :], AX.X, ALU.max
                                          ).then_inc(m["peak"], 1)

                batches(dve, 2, body, NG)
                dve.wait_ge(m["peak"], NG)
                dlink(dve, dve.tensor_reduce(hm, hpk.rearrange("p (g c) -> p c g", c=4), AX.X, ALU.max))
                dlink(dve, dve.scalar_tensor_tensor(out=hm, in0=hm, scalar=col(K_F1),
                                                    in1=bcol[:, 5:9], op0=ALU.mult, op1=ALU.add))
                dlink(dve, dve.tensor_reduce(hm[:, 0:1], hm, AX.X, ALU.max))
                dve.tensor_scalar(col(AMAX), hm[:, 0:1], 0.0, None, ALU.max).then_inc(s_allin, 1)
                quantum(dve, 6)
                dlink(dve, dve.tensor_tensor(col(K_H), col(K_F1), col(INV), ALU.mult))
                dlink(dve, dve.tensor_tensor(col(K_F2), col(IS), col(WS + 6), ALU.mult))
                dlink(dve, dve.tensor_scalar(sc[:, B_F1:B_F1 + 4], bcol[:, 5:9], col(INV), None,
                                             ALU.mult))

            @block.scalar
            def _(act):
                act.wait_ge(m["qavg"], 1)

                def body(i, par, live):
                    if live(0):
                        wait(act, m["qf"], i - 1)
                        act.activation(tq[par], group(FT, i), ACT.Copy, bias=MAGIC, scale=col(INV)
                                       ).then_inc(m["tq"], 1)

                batches(act, 2, body, NG)

            @block.gpsimd
            def _(pool):
                pool.wait_ge(s_allin, 5)
                pool.partition_all_reduce(col(AALL), col(AMAX), P, RMAX).then_inc(s_allout, 1)
                with pool.Fori(0, NG) as g:
                    pool.tensor_tensor(rows4(g), rows4(g), brep[:, 1:2, :].to_broadcast([P, G4, D]),
                                       ALU.add).then_inc(m["b2"], 1)
                pool.wait_ge(s_allin, 6)
                pool.partition_all_reduce(col(AALL), col(AMAX), P, RMAX).then_inc(s_allout, 1)
                pool.memset(blank[:], 0.0).then_inc(m["blank"], 1)
                pool.wait_ge(m["blank"], 1)
                pool.memset(blank[:].bitcast(I32)[:, D + TOKEN:D + TOKEN + 1], NT).then_inc(m["blank"], 1)
                pool.iota(X[:].bitcast(I32)[:, :, D + TOKEN], [[P, B]], base=0, channel_multiplier=1
                          ).then_inc(m["b2"], 1)

            @block.tensor
            def _(pe):
                pe.wait_ge(m["qavg"], 1)

                def body(i, par, live):
                    if live(1):
                        g = i - 1
                        pe.wait_ge(m["qf"], g + 1)
                        wait(pe, m["peak"], g - 1)
                        for c in range(4):
                            mm = hidden(pe, ps[4 * (1 - par) + c], g, c)
                        mm.then_inc(m["f1"], 1)

                batches(pe, 2, body, NG)

        for n in used:
            used[n] = 0
        qavg = lend(B, BF16)
        W1 = R2[:, 0:E * F]
        W2 = R2[:, E * F:2 * E * F]
        relu = [lend(GW) for n in range(4)]
        qh = [lend(4 * GW, BF16).rearrange("p (c t) -> p c t", c=4) for n in range(2)]
        xs = lend(GW)
        xsT = lend(GW)
        stat4 = sb("stat4", [P, G4, 6])
        mom4 = sb("mom4", [P, G4, 2])
        gw = sb("gw", [P, E])
        ms2 = sb("ms2", [P, G4])
        logit = sb("logit", [P, E, B])
        x = {n: sem("x_" + n) for n in
             "w gw f1 relu qh f2 x3 xs stat mom ms mean rs xp xsT gate logit".split()}

        def extra(n, g=None):
            if g is None:
                return X[:, :, D + n]
            return Xf[:, bass.ds(g * (G4 * RW), G4 * RW)].rearrange(
                "p (j w) -> p j w", j=G4)[:, :, D + n]

        with nc.Block() as block:
            @block.sync
            def _(sp):
                for e_ in range(E):
                    sp.dma_start(W1[:, e_ * F:(e_ + 1) * F], a["w1"][e_]).then_inc(x["w"], 16)
                    sp.dma_start(W2[:, e_ * F:(e_ + 1) * F].rearrange("p (c d) -> p c d", c=4),
                                 a["w2"][e_].rearrange("(c p) d -> p c d", p=P)).then_inc(x["w"], 16)
                sp.dma_start(gw[:], a["gw"]).then_inc(x["gw"], 16)
                sp.wait_ge(x["w"], 32 * E)

            @block.vector
            def _(dve):
                dve.wait_ge(x["gw"], 16)
                dve.tensor_scalar(gw[:], gw[:], bcol[:, 10:11], None, ALU.mult).then_inc(x["gw"], 1)

                def body(i, par, live):
                    g1, g2, g3, g4 = (i - n for n in range(1, 5))
                    if live(3):
                        dve.wait_ge(x["rs"], g3 + 1)
                        dve.wait_ge(x["mean"], g3 + 1)
                        wait(dve, x["xp"], g3)
                        for j in range(G4):
                            dve.tensor_scalar(xs[:, j * D:(j + 1) * D], row(g3 * G4 + j),
                                              extra(MEAN, g3)[:, j:j + 1], extra(RSTD, g3)[:, j:j + 1],
                                              ALU.subtract, ALU.mult).then_inc(x["xs"], 1)
                    if live(1):
                        dve.wait_ge(x["f2"], g1 + 1)
                        dve.scalar_tensor_tensor(out=rows4(g1), in0=four(ps[4]), scalar=col(K_F2),
                                                 in1=rows4(g1), op0=ALU.mult, op1=ALU.add
                                                 ).then_inc(x["x3"], 1)
                    if live(2):
                        dve.wait_ge(x["x3"], g2 + 1)
                        wait(dve, x["mom"], g2 * G4)
                        for j in range(G4):
                            dve.sem_inc(s_tick, 1)
                            dve.bn_stats(stat4[:, j, :], row(g2 * G4 + j)).then_inc(x["stat"], 1)
                        dve.wait_ge(x["stat"], g2 * G4 + G4)
                        wait(dve, x["ms"], g2)
                        wait(dve, x["mean"], g2)
                        for j in range(G4):
                            dve.sem_inc(s_tick, 1)
                            dve.bn_aggr(mom4[:, j, :], stat4[:, j, :]).then_inc(x["mom"], 1)
                        dve.wait_ge(x["mom"], g2 * G4 + G4)
                        wait(dve, x["rs"], g2)
                        dve.tensor_scalar(ms2[:], mom4[:, :, 1], 1.0 + 1e-6, 1e-11, ALU.mult, ALU.add
                                          ).then_inc(x["ms"], 1)
                        dve.tensor_copy(extra(MEAN, g2), mom4[:, :, 0]).then_inc(x["mean"], 1)
                    if live(0):
                        wait(dve, x["f2"], i - 1)
                        for c in range(4):
                            dve.wait_ge(x["relu"], i * 4 + (c + 1))
                            dve.tensor_scalar(qh[par][:, c, :], relu[c], MAGIC, MAGIC, ALU.add,
                                              ALU.subtract).then_inc(x["qh"], 1)
                    if live(4):
                        dve.wait_ge(x["gate"], g4 + 1)
                        dve.tensor_copy(logit[:, :, bass.ds(g4 * G4, G4)],
                                        ps[6][:, 0:G4 * E].rearrange("p (j e) -> p e j", e=E)
                                        ).then_inc(x["logit"], 1)

                batches(dve, 5, body, NG)

            @block.scalar
            def _(act):
                def body(i, par, live):
                    g3 = i - 3
                    if live(0):
                        for c in range(4):
                            act.wait_ge(x["f1"], i * 4 + (c + 1))
                            wait(act, x["qh"], i * 4 + (c - 3))
                            act.activation(relu[c], ps[c], ACT.Relu, scale=col(K_H),
                                           bias=col(B_F1 + c)).then_inc(x["relu"], 1)
                    if live(3):
                        act.wait_ge(x["xp"], g3 + 1)
                        wait(act, x["gate"], g3)
                        act.copy(xsT, ps[5]).then_inc(x["xsT"], 1)

                batches(act, 5, body, NG)

            @block.gpsimd
            def _(pool):
                def body(i, par, live):
                    g2 = i - 2
                    if live(2):
                        pool.wait_ge(x["ms"], g2 + 1)
                        pool.tensor_tensor(extra(RSTD, g2), ms2[:], col(NHALF).to_broadcast([P, G4]),
                                           ALU.pow).then_inc(x["rs"], 1)

                batches(pool, 5, body, NG)

            @block.tensor
            def _(pe):
                pe.wait_ge(x["gw"], 17)

                def body(i, par, live):
                    g1, g3 = i - 1, i - 3
                    if live(0):
                        for c in range(4):
                            wait(pe, x["relu"], i * 4 + (c - 3))
                            hidden(pe, ps[c], i, c).then_inc(x["f1"], 1)
                    if live(3):
                        pe.wait_ge(x["xs"], g3 * G4 + G4)
                        wait(pe, x["xsT"], g3)
                        for j in range(G4):
                            mm = pe.transpose(ps[5][:, j * S:(j + 1) * S], xs[:, j * D:(j + 1) * D],
                                              ident)
                        mm.then_inc(x["xp"], 1)
                    if live(1):
                        pe.wait_ge(x["qh"], g1 * 4 + 4)
                        wait(pe, x["x3"], g1)
                        for j in range(G4):
                            for c in range(4):
                                mm = pe.matmul(ps[4][:, j * D:(j + 1) * D],
                                               qh[1 - par][:, c, j * S:(j + 1) * S], f2w[:, c, :],
                                               start=(c == 0), stop=(c == 3))
                        mm.then_inc(x["f2"], 1)
                    if live(3):
                        pe.wait_ge(x["xsT"], g3 + 1)
                        wait(pe, x["logit"], g3)
                        for j in range(G4):
                            mm = pe.matmul(ps[6][:, j * E:(j + 1) * E], xsT[:, j * S:(j + 1) * S],
                                           gw[:], start=True, stop=True)
                        mm.then_inc(x["gate"], 1)

                batches(pe, 5, body, NG)

        for n in used:
            used[n] = 0
        EB = E * B
        cube = lambda t: t.rearrange("p (e b) -> p e b", e=E)
        pe_, choice, count, thr, before = (lend(EB) for n in range(5))
        ohb = lend(EB, BF16)
        trib = lend(P, BF16)
        ones = lend(EB)
        best, total5, rec5, pick, pos = (lend(B) for n in range(5))
        ends, tiles, incl, shift = lend(E + 1), lend(E), lend(E), lend(E)
        cmp = lend(TILES * E)
        et = lend(TILES)
        posi = sb("posi", [P, B], I32)
        wat = sb("wat", [1, TILES], I32)
        FD = F + D
        be, bback6 = (R3[0:E, E * F + n * FD:E * F + (n + 1) * FD] for n in range(2))
        bpart = [R3[:].bitcast(BF16)[0:E, 2 * (E * F + 2 * FD) + n * FD:
                                     2 * (E * F + 2 * FD) + (n + 1) * FD] for n in range(3)]
        bsum = R3[:].bitcast(BF16)[:, 0:2 * E * F].rearrange("p (k e f) -> p k e f", k=2, e=E)
        B1S, B2S = (R3[:].bitcast(BF16)[:, k * E * F:(k + 1) * E * F] for k in range(2))
        lflat = logit[:].rearrange("p e b -> p (e b)")
        o = {n: sem("o_" + n) for n in "bias parts rows sub exp oh count pos sorted".split()}

        with nc.Block() as block:
            @block.sync
            def _(sp):
                sp.dma_start(be[:, 0:F], a["b1"]).then_inc(o["bias"], 16)
                sp.dma_start(be[:, F:F + D], a["b2"]).then_inc(o["bias"], 16)
                sp.wait_ge(o["parts"], 4)
                for n in range(3):
                    sp.dma_start(bsum[n:n + 1, 0, :, :], bpart[n][:, 0:F]).then_inc(o["rows"], 16)
                    sp.dma_start(bsum[n:n + 1, 1, :, 0:D], bpart[n][:, F:F + D]
                                 ).then_inc(o["rows"], 16)
                sp.wait_ge(o["rows"], 96)

            @block.vector
            def _(dve):
                wide = lambda t: t[:, None, :].to_broadcast([P, E, B])
                dlink(dve, dve.tensor_reduce(best, logit[:].rearrange("p e b -> p b e"), AX.X, ALU.max))
                dve.tensor_tensor(logit[:], logit[:], wide(best), ALU.subtract).then_inc(o["sub"], 1)
                dlink(dve, dve.tensor_scalar(W1, W1, bcol[:, 10:11], None, ALU.mult))
                dlink(dve, dve.tensor_copy(trib, cst[:, C_TRI:C_TRI + P]))
                dlink(dve, dve.memset(ones, 1.0))
                dlink(dve, dve.memset(ends[:, 0:1], 0.0))
                dve.wait_ge(o["exp"], 1)
                dlink(dve, dve.tensor_reduce(total5, cube(pe_).rearrange("p e b -> p b e"), AX.X,
                                             ALU.add))
                dlink(dve, dve.reciprocal(rec5, total5))
                dlink(dve, dve.tensor_tensor(cube(pe_), cube(pe_), wide(rec5), ALU.mult))
                dlink(dve, dve.tensor_reduce(best, cube(pe_).rearrange("p e b -> p b e"), AX.X,
                                             ALU.max))
                dlink(dve, dve.tensor_scalar(extra(SCORE), best, 0.5, None, ALU.mult))
                dlink(dve, dve.tensor_tensor(cube(choice), cube(pe_), wide(best), ALU.is_equal))
                dlink(dve, dve.scalar_tensor_tensor(
                    out=cube(choice), in0=cube(choice), scalar=-float(E),
                    in1=cst[:, C_IOTA:C_IOTA + E, None].to_broadcast([P, E, B]),
                    op0=ALU.mult, op1=ALU.add))
                dlink(dve, dve.tensor_reduce(pick, cube(choice).rearrange("p e b -> p b e"), AX.X,
                                             ALU.min))
                dve.tensor_tensor(cube(ohb), cube(choice), wide(pick), ALU.is_equal
                                  ).then_inc(o["oh"], 1)
                dve.wait_ge(o["oh"], 1)
                dve.wait_ge(o["count"], 1)
                dlink(dve, dve.tensor_tensor_scan(count, ones, ps[1], 0.0, ALU.mult, ALU.add))
                dlink(dve, dve.tensor_copy(ends[:, 1:E + 1], cube(count)[:, :, B - 1]))
                dlink(dve, dve.tensor_tensor(tiles, ends[:, 1:E + 1], ends[:, 0:E], ALU.subtract))
                dlink(dve, dve.tensor_tensor(
                    cube(thr), tiles[:, :, None].to_broadcast([P, E, B]),
                    cst[:, None, C_T:C_T + B].to_broadcast([P, E, B]), ALU.is_gt))
                dlink(dve, dve.tensor_reduce(tiles, cube(thr), AX.X, ALU.add))
                dlink(dve, dve.tensor_tensor_scan(incl, ones[:, 0:E], tiles, 0.0, ALU.mult, ALU.add))
                dlink(dve, dve.tensor_tensor(shift, incl, tiles, ALU.subtract))
                dlink(dve, dve.scalar_tensor_tensor(out=shift, in0=shift, scalar=float(P),
                                                    in1=ends[:, 0:E], op0=ALU.mult, op1=ALU.subtract))
                dlink(dve, dve.tensor_tensor(count, count, ps[1], ALU.subtract))
                dlink(dve, dve.tensor_tensor(count, count, ps[0], ALU.add))
                dlink(dve, dve.tensor_tensor(cube(count), cube(count),
                                             shift[:, :, None].to_broadcast([P, E, B]), ALU.add))
                dlink(dve, dve.tensor_tensor(count, count, ohb, ALU.mult))
                dlink(dve, dve.tensor_reduce(pos, cube(count).rearrange("p e b -> p b e"), AX.X,
                                             ALU.add))
                dve.tensor_copy(posi[:], pos).then_inc(o["pos"], 1)
                dlink(dve, dve.tensor_tensor(
                    cmp[0:1].rearrange("p (t e) -> p t e", e=E),
                    cst[0:1, C_TILE:C_TILE + TILES, None].to_broadcast([1, TILES, E]),
                    incl[0:1, None, :].to_broadcast([1, TILES, E]), ALU.is_ge))
                dlink(dve, dve.tensor_reduce(et[0:1], cmp[0:1].rearrange("p (t e) -> p t e", e=E),
                                             AX.X, ALU.add))
                dlink(dve, dve.tensor_scalar(et[0:1], et[0:1], float(E - 1), None, ALU.min))
                dlink(dve, dve.tensor_scalar(wat[:], et[0:1], float(F), None, ALU.mult))
                dve.memset(R3[:, 0:E * F], 0.0).then_inc(o["parts"], 1)
                dve.wait_ge(o["bias"], 32)
                dlink(dve, dve.tensor_scalar(be[:, F:F + D], be[:, F:F + D], 2.0, None, ALU.mult))
                for n in range(3):
                    dve.tensor_copy(bpart[n], be).then_inc(o["parts"], 1)
                    if n < 2:
                        dve.wait_ge(o["parts"], n + 2)
                        dlink(dve, dve.tensor_copy(bback6, bpart[n]))
                        dlink(dve, dve.tensor_tensor(be, be, bback6, ALU.subtract))

            @block.scalar
            def _(act):
                act.activation(warm[:], bcol[:, 0:1], ACT.Exp).then_inc(s_act, 1)
                act.wait_ge(o["sub"], 1)
                act.activation(pe_, lflat, ACT.Exp).then_inc(o["exp"], 1)

            @block.tensor
            def _(pe):
                pe.wait_ge(o["oh"], 1)
                pe.matmul(ps[0], trib, ohb, start=True, stop=True)
                pe.matmul(ps[1], onesb[:], ohb, start=True, stop=True).then_inc(o["count"], 1)

            @block.gpsimd
            def _(pool):
                pool.wait_ge(o["pos"], 1)
                for b in range(B):
                    pool.indirect_dma_start(sorted_rows[:], bass.IndirectOffsetOnAxis(
                        posi[:, b:b + 1], 0), X[:, b, :], None).then_inc(o["sorted"], 16)
                pool.wait_ge(o["sorted"], 16 * B)

        for n in used:
            used[n] = 0
        SLOTS = 8
        srow = [lend(RW) for n in range(SLOTS)]
        srows = work[:, 0:SLOTS * RW].rearrange("p (s w) -> p s w", w=RW)
        xn6 = [lend(D) for n in range(2)]
        xnT6 = [lend(P) for n in range(2)]
        u6 = [lend(F) for n in range(2)]
        th6 = [lend(F) for n in range(2)]
        hT6 = [lend(F) for n in range(2)]
        put = [lend(D) for n in range(4)]
        e = {n: sem("moe_" + n) for n in
             "load xn xt xnT w1 u tr tanh h w2 out put0 put1 taken".split()}

        def pairs(i, ph, n=0):
            return (i - ph % 2) * 8 + 16 * (n + 1)

        def expert(pe, i):
            return pe.value_load(wat[0:1, bass.ds(i, 1)], min_val=0, max_val=(E - 1) * F)

        with nc.Block() as block:
            @block.sync
            def _(sp):
                def body(i, ph, live):
                    if ph % 2 == 0 and live(0):
                        wait(sp, e["put0"], i * 8 - 8 * (SLOTS - 2))
                        wait(sp, e["put1"], i * 8 - 8 * (SLOTS - 2))
                        wait(sp, e["load"], i * 8)
                        sp.dma_start(srows[:, ph:ph + 2, :],
                                     sorted_rows[bass.ds(i * P, 2 * P), :].rearrange(
                                         "(t p) w -> p t w", p=P)).then_inc(e["load"], 16)

                batches(sp, 1, body, TILES + 1, SLOTS)

            @block.vector
            def _(dve):
                def body(i, ph, live):
                    g4, g5, odd = i - 4, i - 5, (ph + 1) % 2
                    if live(4):
                        dve.wait_ge(e["tanh"], g4 + 1)
                        wait(dve, e["w2"], g4 - 1)
                        dve.scalar_tensor_tensor(out=hT6[ph % 2], in0=th6[ph % 2], scalar=1.0,
                                                 in1=ps[2 + ph % 2], op0=ALU.add, op1=ALU.mult
                                                 ).then_inc(e["h"], 1)
                    if live(5):
                        r = srow[(ph + 3) % SLOTS]
                        dve.wait_ge(e["w2"], g5 + 1)
                        wait(dve, e["put%d" % odd], pairs(g5 - 4, odd))
                        dve.scalar_tensor_tensor(out=put[(ph + 3) % 4], in0=ps[6 + odd][:, 0:D],
                                                 scalar=r[:, D + SCORE:D + SCORE + 1],
                                                 in1=r[:, 0:D], op0=ALU.mult, op1=ALU.add
                                                 ).then_inc(e["out"], 1)
                    if live(0):
                        r = srow[ph]
                        dve.wait_ge(e["load"], pairs(i, ph))
                        wait(dve, e["xt"], i - 1)
                        dve.tensor_scalar(xn6[ph % 2], r[:, 0:D], r[:, D + MEAN:D + MEAN + 1],
                                          r[:, D + RSTD:D + RSTD + 1], ALU.subtract, ALU.mult
                                          ).then_inc(e["xn"], 1)

                batches(dve, 6, body, TILES, SLOTS)

            @block.scalar
            def _(act):
                act.activation(warm[:], bcol[:, 0:1], ACT.Tanh).then_inc(s_act, 1)

                def body(i, ph, live):
                    g1, g2, g4, odd = i - 1, i - 2, i - 4, (ph + 1) % 2
                    if live(4):
                        act.wait_ge(e["tr"], g4 + 1)
                        wait(act, e["h"], g4 - 1)
                        act.activation(th6[ph % 2], ps[2 + ph % 2], ACT.Tanh, scale=0.5
                                       ).then_inc(e["tanh"], 1)
                    if live(2):
                        act.wait_ge(e["w1"], g2 + 1)
                        wait(act, e["tr"], g2 - 1)
                        act.copy(u6[ph % 2], ps[ph % 2]).then_inc(e["u"], 1)
                    if live(1):
                        act.wait_ge(e["xt"], g1 + 1)
                        wait(act, e["w1"], g1 - 1)
                        act.copy(xnT6[odd], ps[5][:, 0:P]).then_inc(e["xnT"], 1)

                batches(act, 6, body, TILES, SLOTS)

            @block.tensor
            def _(pe):
                def body(i, ph, live):
                    g1, g2, g3, g5, odd = i - 1, i - 2, i - 3, i - 5, (ph + 1) % 2
                    if live(5):
                        at = expert(pe, g5)
                        pe.wait_ge(e["h"], g5 + 1)
                        wait(pe, e["out"], g5 - 1)
                        y = ps[6 + odd][:, 0:D]
                        pe.matmul(y, onesb[:], B2S[:, bass.ds(at, D)], start=True, stop=False)
                        for c in range(4):
                            mm = pe.matmul(y, hT6[odd][:, c * P:(c + 1) * P],
                                           W2[:, bass.ds(at + c * D, D)], start=False,
                                           stop=(c == 3))
                        mm.then_inc(e["w2"], 1)
                    if live(2):
                        at = expert(pe, g2)
                        pe.wait_ge(e["xnT"], g2 + 1)
                        wait(pe, e["u"], g2 - 1)
                        pe.matmul(ps[ph % 2], onesb[:], B1S[:, bass.ds(at, F)], start=True,
                                  stop=False)
                        pe.matmul(ps[ph % 2], xnT6[ph % 2], W1[:, bass.ds(at, F)], start=False,
                                  stop=True).then_inc(e["w1"], 1)
                    if live(3):
                        pe.wait_ge(e["u"], g3 + 1)
                        wait(pe, e["h"], g3 - 1)
                        for c in range(4):
                            mm = pe.transpose(ps[2 + odd][:, c * P:(c + 1) * P],
                                              u6[odd][:, c * P:(c + 1) * P], ident)
                        mm.then_inc(e["tr"], 1)
                    if live(1):
                        pe.wait_ge(e["xn"], g1 + 1)
                        wait(pe, e["xnT"], g1)
                        pe.transpose(ps[5][:, 0:P], xn6[odd], ident).then_inc(e["xt"], 1)

                batches(pe, 6, body, TILES, SLOTS)

            @block.gpsimd
            def _(pool):
                def body(i, ph, live):
                    if live(5):
                        g5, odd = i - 5, (ph + 1) % 2
                        done = e["put%d" % odd]
                        pool.wait_ge(e["out"], g5 + 1)
                        wait(pool, done, pairs(g5 - 2, odd))
                        pool.sem_inc(e["taken"], 1)
                        r = srow[(ph + 3) % SLOTS].bitcast(I32)
                        pool.indirect_dma_start(
                            out[:], bass.IndirectOffsetOnAxis(r[:, D + TOKEN:D + TOKEN + 1], 0),
                            put[(ph + 3) % 4], None,
                            bounds_check=NT - 1, oob_is_err=False).then_inc(done, 16)

                batches(pool, 6, body, TILES, SLOTS)
                pool.wait_ge(e["put0"], 16 * (-(-TILES // 2)))
                pool.wait_ge(e["put1"], 16 * (TILES // 2))


def _laid_out(i):
    c = np.ascontiguousarray
    t = lambda w: c(np.asarray(w).T)
    g = {k: np.asarray(v) for k, v in i.items()}
    zero = np.zeros(P, np.float32)
    a = {
        "x": c(g["x"].reshape(NT, D)),
        "ctxT": t(g["ctx_768"].reshape(NC, CD)),
        "mask": c(g["mask_BxS2_bf1"].reshape(1, NC)).view(np.uint8),
        "cst": constants(),
        "wq": c(g["L0_xattn_Wq"]), "wk": c(g["L0_xattn_Wk"]),
        "wv": c(g["L0_xattn_Wv"]), "wo": c(g["L0_xattn_Wo"]),
        "wof": t(g["L0_ffn_wo"]), "uo": t(g["L0_ffn_uo"]),
        "bgate": c(np.stack([g["L0_ffn_bf"], g["L0_ffn_bi"], g["L0_ffn_bc"]])[None]),
    }
    for n in "fic":
        a["w" + n] = t(g["L0_ffn_w" + n])
        a["u" + n] = t(g["L0_ffn_u" + n])
    for n in WEIGHTS:
        a["w_" + n] = t(g["L1_xattn_W_" + n])
    a["w1"], a["w2"], a["gw"] = c(g["L1_ffn_W1"]), c(g["L1_ffn_W2"]), t(g["L1_ffn_gate_w"])
    a["b1"], a["b2"] = (c(g["L1_ffn_b" + n]) for n in "12")
    ba = [np.concatenate([g["L1_xattn_b_att" + n]] * 2) for n in "01"]
    cols = [g["L1_xattn_b_d2v"], g["L1_xattn_b_img"], g["L1_xattn_b_txt"], *ba,
            *g["L1_xattn_b_f1"].reshape(4, P), g["L0_ffn_in_c"], g["L1_ffn_rms_w"]]
    a["bcol"] = c(np.stack(cols + [zero] * (16 - len(cols)), 1))
    a["brow"] = c(np.stack([g["L0_ffn_bo"], g["L1_xattn_b_f2"], g["L1_ffn_rms_w"], *ba, zero])[None])
    return a


def kernel(**inputs):
    import concourse.bacc as bacc
    from concourse.bass_utils import run_bass_kernel_spmd as run

    arrays = _laid_out(inputs)
    nc = bacc.Bacc("TRN2", target_bir_lowering=False, num_devices=1)
    a = {n: nc.dram_tensor("in_" + n, v.shape, mybir.dt.from_np(v.dtype), kind="ExternalInput").ap()
         for n, v in arrays.items()}
    out = nc.dram_tensor("out", (NT, D), F32, kind="ExternalOutput").ap()
    xattn_ffn_kernel(nc, a, out)
    r = run(nc, [{"in_" + n: v for n, v in arrays.items()}], core_ids=[0])
    return r.results[0]["out"].reshape(B, S, D)
```

```python
from contextlib import ExitStack

import numpy as np

import concourse.bass as bass
from concourse import mybir

P = 128
B, S, D = 64, 128, 128
M, CD = 77, 96
H, HD = 16, 8
Q = 4
F = 512
E = 8
NT = B * S
NC = B * M
PW = H * M + (P - M) + 1
CW = 448
NCC = NC // CW
G4 = 4
NG = B // G4
TILES = B + E - 1
SORTED = -(-TILES // 2) * 2 * P
ROWS = (TILES + 1) * P
RW = D + 4
MEAN, SCORE, TOKEN, RSTD = range(4)
MAGIC = 12582912.0
BIG = 3.3895313892515355e38

ALU = mybir.AluOpType
ACT = mybir.ActivationFunctionType
BF16 = mybir.dt.bfloat16
F32 = mybir.dt.float32
I32 = mybir.dt.int32
U8 = mybir.dt.uint8
AX = mybir.AxisListType
RMAX = bass.bass_isa.ReduceOp.max
RADD = bass.bass_isa.ReduceOp.add

WEIGHTS = ("d2v", "img", "txt", "att0", "att1", "f1", "f2")


def batches(eng, depth, body, count=B, unroll=2):
    lo = -(-depth // unroll) * unroll
    turns = (count - lo) // unroll
    for i in range(lo):
        body(i, i % unroll, lambda n, i=i: 0 <= i - n < count)
    with eng.Fori(0, turns) as turn:
        for u in range(unroll):
            body(turn * unroll + (lo + u), u, lambda n: True)
    for i in range(lo + turns * unroll, count + depth - 1):
        body(i, i % unroll, lambda n, i=i: 0 <= i - n < count)


def wait(eng, sem, value):
    if isinstance(value, int) and value <= 0:
        return
    eng.wait_ge(sem, value)


C_ID, C_KM, C_VM, C_TRI, C_IOTA, C_INV, C_T = 0, 128, 144, 656, 784, 792, 800
C_TILE = C_T + 64
C_W = C_TILE + TILES


def constants():
    c = np.zeros((P, C_W), np.float32)
    p = np.arange(P)
    c[:, C_ID:C_ID + P] = np.eye(P)
    for q in range(Q):
        for g in range(Q):
            c[:, C_KM + 4 * q + g] = p // HD == 4 * g + q
        c[:, C_VM + q * D:C_VM + (q + 1) * D] = (np.arange(D) % 32) // HD == q
    c[:, C_TRI:C_TRI + P] = p[:, None] < p[None, :]
    c[:, C_IOTA:C_IOTA + E] = np.arange(E)
    for n, count in enumerate((CD * D, D * D, D * D, D * 64, D * 64, 2 * D * F, F * D)):
        c[:, C_INV + n] = 1.0 / count
    c[:, C_T:C_T + 64] = np.arange(64) * P
    c[:, C_TILE:C_TILE + TILES] = np.arange(TILES)
    return c


class Chain:

    def __init__(self, sem):
        self.sem, self.n = sem, 0

    def __call__(self, eng, ins):
        self.n += 1
        ins.then_inc(self.sem, 1)
        eng.wait_ge(self.sem, self.n)


def xattn_ffn_kernel(nc, a, out):
    with ExitStack() as ctx:
        def sb(name, shape, dt=F32):
            return ctx.enter_context(nc.sbuf_tensor(name, shape, dt))

        def sem(name):
            return ctx.enter_context(nc.semaphore(name))

        psum = ctx.enter_context(nc.psum_tensor("psum", [P, 8, 512], F32))
        ps = [psum[:, n, :] for n in range(8)]

        X = sb("X", [P, B, RW])
        R2 = sb("R2", [P, B * D])
        R3 = sb("R3", [P, B * D])
        cst = sb("cst", [P, C_W])
        ident = cst[:, C_ID:C_ID + P]
        kT = sb("kT", [P, NC])
        qimg = sb("qimg", [P, NC], BF16)
        maskneg = sb("maskneg", [P, NC], BF16)
        work = sb("work", [P, 2 * PW + 2 * H * M])
        prob = [work[:, n * PW:(n + 1) * PW] for n in range(2)]
        kblk = [work[:, 2 * PW + n * H * M:2 * PW + (n + 1) * H * M] for n in range(2)]
        vm = [sb(f"vm{n}", [P, Q, D]) for n in range(2)]
        pts = [sb(f"pts{n}", [P, 512]) for n in range(2)]
        small = sb("small", [P, 12, P])
        raw = sb("raw", [P, 2048])
        tern = sb("tern", [P, 2176], BF16)
        sc = sb("sc", [P, 64])
        bcol = sb("bcol", [P, 16])
        brep = sb("brep", [P, 6, P])
        onesb = sb("onesb", [P, P], BF16)
        brow = sb("brow", [1, 3, P])
        bback = sb("bback", [1, 3, P])
        bsplit = sb("bsplit", [P, 3, P], BF16)
        identb = sb("identb", [P, P], BF16)
        warm = sb("warm", [P, 1])
        avgT = sb("avgT", [P, B])

        WQ, WK, WV, WO, WF, WI, WC, UF, UI, UC, WOF, UO = (small[:, n, :] for n in range(12))
        rawd = {"d2v": raw[0:CD, 0:128], "img": raw[:, 128:256], "txt": raw[:, 256:384],
                "att0": raw[:, 384:448], "att1": raw[:, 448:512],
                "f1": raw[:, 512:1536], "f2": raw[:, 1536:2048]}
        ternd = {"d2v": tern[0:CD, 0:128], "img": tern[:, 128:256], "txt": tern[:, 256:384],
                 "att0": tern[:, 384:512], "att1": tern[:, 512:640],
                 "f1": tern[:, 640:1664], "f2": tern[:, 1664:2176]}
        ctxT = R3[0:CD, 0:NC]
        V = R2[0:M, :]

        WSUM, WS, THR, NTHR = 0, 8, 16, 24
        AMAX, AALL, IS, INV, K_TMP, EPS5, EPS6, NHALF, K_TXT, K_A0, K_A1, S_IMG, K_F1, K_H, K_F2 = \
            range(32, 47)
        K_A = (K_A0, K_A1)
        B_F1 = 48

        def col(n, rows=P):
            return sc[0:rows, n:n + 1]

        s_load, s_ctx, s_x = sem("s_load"), sem("s_ctx"), sem("s_x")
        s_dve, s_act = sem("s_dve"), sem("s_act")
        s_tick = sem("s_tick")
        dlink = Chain(s_dve)
        s_allin, s_allout = sem("s_allin"), sem("s_allout")

        def quantum(dve, n):
            dve.wait_ge(s_allout, n)
            dlink(dve, dve.tensor_scalar(col(IS), col(AALL), 1e-8, 1.0 / 127.0, ALU.max, ALU.mult))
            dlink(dve, dve.reciprocal(col(INV), col(IS)))

        CH = 352
        NCH = NC // CH
        STREAMS = ("kT", "vis", "img")
        s_mask = sem("s_mask")
        s_bank = sem("s_bank")
        s_prod = sem("s_prod")
        s_quant = sem("s_quant")
        s_tern = sem("s_tern")
        s_kvis = sem("s_kvis")
        s_vprod, s_vbank = sem("s_vprod"), sem("s_vbank")
        s_wred, s_wsum = sem("s_wred"), sem("s_wsum")
        maskb = raw[:].bitcast(U8)[0:1, 0:NC]
        NLOAD = 1 + 12 + 3

        with nc.Block() as block:
            @block.sync
            def _(sp):
                sp.dma_start(maskb, a["mask"]).then_inc(s_mask, 16)
                sp.dma_start(ctxT, a["ctxT"]).then_inc(s_ctx, 16)
                sp.dma_start(cst[:], a["cst"]).then_inc(s_load, 16)
                for b in range(0, B, 16):
                    sp.dma_start(X[:, b:b + 16, 0:D], a["x"][b * S:(b + 16) * S, :]
                                 .rearrange("(b s) d -> s b d", s=S)).then_inc(s_x, 16)
                sp.wait_ge(s_mask, 17)
                for name in WEIGHTS:
                    dst, src = rawd[name], a["w_" + name]
                    if name in ("f1", "f2"):
                        k = src.shape[0] // P
                        dst = dst.rearrange("p (k n) -> p k n", k=k)
                        src = src.rearrange("(k p) n -> p k n", p=P)
                    sp.dma_start(dst, src).then_inc(s_tern, 16)
                sp.wait_ge(s_x, 16 * 4)

            @block.scalar
            def _(act):
                for n, name in enumerate(("wq", "wk", "wv", "wo", "wf", "wi", "wc", "uf", "ui", "uc",
                                          "wof", "uo")):
                    rows = CD if name in ("wk", "wv") else P
                    act.dma_start(small[0:rows, n, :], a[name]).then_inc(s_load, 16)
                act.dma_start(bcol[:], a["bcol"]).then_inc(s_load, 16)
                act.dma_start(brow[:], a["bgate"]).then_inc(s_load, 16)
                act.dma_start(brep[:], a["brow"].to_broadcast([P, 6, P])).then_inc(s_load, 16)
                act.wait_ge(s_load, 16 * NLOAD)
                act.activation(warm[:], bcol[:, 0:1], ACT.Exp).then_inc(s_act, 1)
                for n, name in enumerate(STREAMS):
                    if n:
                        act.wait_ge(s_kvis, n)
                    dst = kT if name == "kT" else work
                    with act.Fori(0, NCH // 2) as turn:
                        for u in range(2):
                            act.wait_ge(s_prod, turn * 2 + (n * NCH + u + 1))
                            act.activation(
                                dst[:, bass.ds((turn * 2 + u) * CH, CH)], ps[u][:, 0:CH],
                                ACT.Identity, bias=bcol[:, n - 1:n] if n else 0.0,
                                scale=col(K_TMP) if n else 1.0).then_inc(s_bank, 1)
                    if n == 0:
                        for g in range(NG):
                            act.wait_ge(s_vprod, g + 1)
                            act.copy(V[:, g * G4 * D:(g + 1) * G4 * D], ps[2 + g % 2][0:M, :]
                                     ).then_inc(s_vbank, 1)

            @block.gpsimd
            def _(pool):
                pool.wait_ge(s_allin, 1)
                pool.partition_all_reduce(col(AALL), col(AMAX), P, RMAX).then_inc(s_allout, 1)
                pool.wait_ge(s_wred, 1)
                pool.partition_all_reduce(sc[:, WS:WS + 8], sc[:, WSUM:WSUM + 8], P, RADD
                                          ).then_inc(s_wsum, 1)
                for n in (2, 3):
                    pool.wait_ge(s_allin, n)
                    pool.partition_all_reduce(col(AALL), col(AMAX), P, RMAX).then_inc(s_allout, 1)

            @block.tensor
            def _(pe):
                pe.wait_ge(s_load, 16 * NLOAD)
                pe.wait_ge(s_ctx, 16)
                pe.wait_ge(s_bank, 2)
                for n, (name, w) in enumerate((("kT", WK[0:CD]), ("vis", ternd["d2v"]),
                                               ("img", ternd["img"]))):
                    if n:
                        pe.wait_ge(s_quant, n)
                    src = ctxT if n == 0 else qimg[0:CD, :] if n == 1 else qimg
                    with pe.Fori(0, NCH // 2) as turn:
                        for u in range(2):
                            pe.wait_ge(s_bank, turn * 2 + (n * NCH + u + 1))
                            pe.matmul(ps[u][:, 0:CH], w, src[:, bass.ds((turn * 2 + u) * CH, CH)],
                                      start=True, stop=True).then_inc(s_prod, 1)
                    if n == 0:
                        for b in range(B):
                            g, j = divmod(b, G4)
                            if j == 0:
                                wait(pe, s_vbank, g - 1)
                            mm = pe.matmul(ps[2 + g % 2][0:M, j * D:(j + 1) * D],
                                           ctxT[:, b * M:(b + 1) * M], WV[0:CD], start=True, stop=True)
                            if j == G4 - 1:
                                mm.then_inc(s_vprod, 1)

            @block.vector
            def _(dve):
                dlink(dve, dve.memset(sc[:], 0.0))
                for t in (onesb, bsplit, maskneg, vm[0], vm[1]):
                    dve.memset(t[:], float(t is onesb)).then_inc(s_dve, 1)
                    dlink.n += 1
                dve.memset(col(EPS5), 1e-5).then_inc(s_bank, 1)
                dve.memset(col(EPS6), 1e-6).then_inc(s_bank, 1)
                dve.wait_ge(s_ctx, 16)
                dve.tensor_reduce(col(AMAX, CD), ctxT, AX.X, ALU.max,
                                  apply_absolute_value=True).then_inc(s_allin, 1)
                dlink(dve, dve.memset(col(NHALF), -0.5))
                dve.wait_ge(s_mask, 16)
                dve.tensor_scalar(maskneg[0:1, :], maskb, -1.0, BIG, ALU.add, ALU.mult
                                  ).then_inc(s_mask, 1)
                quantum(dve, 1)
                dlink(dve, dve.tensor_scalar(work[0:CD, 0:NC], ctxT, col(INV, CD), MAGIC,
                                             ALU.mult, ALU.add))
                dlink(dve, dve.tensor_scalar(qimg[0:CD, :], work[0:CD, 0:NC], MAGIC, None,
                                             ALU.subtract))
                dve.wait_ge(s_tern, 16 * len(WEIGHTS))
                for n, name in enumerate(WEIGHTS):
                    w = rawd[name]
                    dlink(dve, dve.tensor_reduce(sc[0:w.shape[0], WSUM + n:WSUM + n + 1], w, AX.X,
                                                 ALU.add, apply_absolute_value=True))
                dve.wait_ge(s_load, 16 * NLOAD)
                dve.tensor_copy(identb[:], ident).then_inc(s_wred, 1)
                dve.wait_ge(s_wsum, 1)
                dlink(dve, dve.tensor_tensor(sc[:, WS:WS + 7], sc[:, WS:WS + 7],
                                             cst[:, C_INV:C_INV + 7], ALU.mult))
                dlink(dve, dve.tensor_scalar(sc[:, WS:WS + 7], sc[:, WS:WS + 7], 1e-5, None, ALU.max))
                dve.tensor_tensor(col(K_TMP), col(IS), col(WS + 0), ALU.mult).then_inc(s_kvis, 1)
                dlink(dve, dve.tensor_scalar(sc[:, THR:THR + 7], sc[:, WS:WS + 7], 0.5, None, ALU.mult))
                dlink(dve, dve.tensor_scalar(sc[:, NTHR:NTHR + 7], sc[:, WS:WS + 7], -0.5, None,
                                             ALU.mult))
                for n, name in enumerate(WEIGHTS):
                    w, t = rawd[name], ternd[name]
                    r, c = w.shape
                    below = R3[0:r, NC:NC + c]
                    dlink(dve, dve.tensor_scalar(below, w, col(NTHR + n, r), None, ALU.is_lt))
                    for twice in range(t.shape[1] // c):
                        dlink(dve, dve.scalar_tensor_tensor(
                            out=t[:, twice * c:(twice + 1) * c], in0=w, scalar=col(THR + n, r),
                            in1=below, op0=ALU.is_gt, op1=ALU.subtract))
                dlink(dve, dve.tensor_scalar(small[:, 4:6, :], small[:, 4:6, :], 0.5, None, ALU.mult))
                dlink(dve, dve.tensor_scalar(small[:, 7:9, :], small[:, 7:9, :], 0.25, None, ALU.mult))
                dlink(dve, dve.tensor_scalar(small[:, 9:10, :], small[:, 9:10, :], 0.5, None, ALU.mult))
                dlink(dve, dve.tensor_scalar(small[:, 11:12, :], small[:, 11:12, :], 0.5, None,
                                             ALU.mult))
                dlink(dve, dve.tensor_scalar(brow[0:1, 0:2, :], brow[0:1, 0:2, :], 0.5, None,
                                             ALU.mult))
                for part in range(3):
                    rows = bsplit[32 * part:32 * part + 1, :, :]
                    dlink(dve, dve.tensor_copy(rows, brow[0:1, :, :]))
                    if part < 2:
                        dlink(dve, dve.tensor_copy(bback[0:1], rows))
                        dlink(dve, dve.tensor_tensor(brow[0:1, :, :], brow[0:1, :, :], bback[0:1],
                                                     ALU.subtract))
                dve.memset(work[:, NC:NC + 1], 0.0).then_inc(s_quant, 1)
                for n in (1, 2):
                    dve.wait_ge(s_bank, 2 + (n + 1) * NCH)
                    dve.tensor_reduce(col(AMAX), work[:, 0:NC], AX.X, ALU.max,
                                      apply_absolute_value=True).then_inc(s_allin, 1)
                    if n == 2:
                        dlink(dve, dve.tensor_reduce(
                            avgT[:], work[:, 0:NC].rearrange("p (b m) -> p b m", m=M), AX.X, ALU.add))
                        dlink(dve, dve.tensor_scalar(avgT[:], avgT[:], 1.0 / M, None, ALU.mult))
                    quantum(dve, n + 1)
                    if n == 1:
                        dve.tensor_tensor(col(K_TMP), col(IS), col(WS + 1), ALU.mult
                                          ).then_inc(s_kvis, 1)
                    dlink(dve, dve.tensor_scalar(work[:, 0:NC], work[:, 0:NC], col(INV), MAGIC,
                                                 ALU.mult, ALU.add))
                    dve.tensor_scalar(qimg[:], work[:, 0:NC], MAGIC, None, ALU.subtract
                                      ).then_inc(s_quant, 1)
                dlink(dve, dve.tensor_tensor(col(K_A0), col(IS), col(WS + 3), ALU.mult))
                dlink(dve, dve.tensor_tensor(col(K_A1), col(IS), col(WS + 4), ALU.mult))
                dlink(dve, dve.tensor_copy(col(S_IMG), col(AALL)))

        HX = R3
        xn = [sb(f"xn{n}", [P, D]) for n in range(2)]
        qT = [sb(f"qT{n}", [P, S]) for n in range(2)]
        xnT, x1n, x1nT = sb("xnT", [P, S]), sb("x1n", [P, D]), sb("x1nT", [P, S])
        attT, rrep = sb("attT", [P, S]), sb("rrep", [P, S])
        gate = sb("gate", [P, 3, S])
        state, keep, fresh = sb("state", [P, S]), sb("keep", [P, S]), sb("fresh", [P, S])
        peak = sb("peak", [P, Q, Q])
        total, rtot = sb("total", [P, H]), sb("rtot", [P, H])
        rwide = sb("rwide", [P, H, HD])
        stat1, stat2 = sb("stat1", [P, 6]), sb("stat2", [P, 6])
        mom1 = [sb(f"mom1_{n}", [P, 2]) for n in range(2)]
        mom2 = [sb(f"mom2_{n}", [P, 2]) for n in range(2)]
        rs1 = [sb(f"rs1_{n}", [P, 1]) for n in range(2)]
        rs2 = [sb(f"rs2_{n}", [P, 1]) for n in range(2)]
        ve1, ve2 = sb("ve1", [P, 1]), sb("ve2", [P, 1])
        QW = Q * M
        QSCALE = float(HD) ** -0.5
        bank_s, bank_t = ps[0:2], ps[2:4]
        bank_x, bank_o, bank_w, bank_g = ps[4], ps[6], ps[5], ps[7]

        names = ("stat1 mom1 ve1 rs1 xn xnp xnT qp q kb vm score peak sub exp pt pte pv total rtot rp "
                 "rwide rrep att wo x1 stat2 mom2 ve2 rs2 x1n x1p x1nT gates tanh hx mix state")
        e = {n: sem("e_" + n) for n in names.split()}

        def cols(b):
            return bass.ds(b * D, D)

        Xf = X[:].rearrange("p b w -> p (b w)")

        def row(b):
            return Xf[:, bass.ds(b * RW, D)]

        def rows4(g):
            return Xf[:, bass.ds(g * (G4 * RW), G4 * RW)].rearrange("p (j w) -> p j w", j=G4)[:, :, 0:D]

        with nc.Block() as block:
            @block.vector
            def _(dve):
                dlink(dve, dve.memset(prob[0][:, H * M:PW], 0.0))
                dlink(dve, dve.memset(prob[1][:, H * M:PW], 0.0))
                dve.memset(state[:], 0.0).then_inc(e["mix"], 2)
                dve.wait_ge(e["mix"], 2)
                dve.tensor_scalar(state[:], state[:], 1.0, bcol[:, 9:10], ALU.mult, ALU.add
                                  ).then_inc(e["mix"], 1)
                dve.wait_ge(e["mix"], 3)
                dve.tensor_scalar(state[:], state[:], 2.0, None, ALU.mult).then_inc(e["state"], 1)
                MIX0 = 3

                def body(i, par, live):
                    b0, b1, b2, b3, b4, b5, b6 = (i - n for n in range(7))
                    odd = 1 - par

                    def peaks(q):
                        dve.wait_ge(e["score"], b2 * 4 + (q + 1))
                        wait(dve, e["sub"], b2 * 4 + (q - 3))
                        s4 = bank_s[q % 2][:, 0:QW].rearrange("p (g m) -> p g m", g=Q)
                        dve.tensor_reduce(peak[:, q, :], s4, AX.X, ALU.max).then_inc(e["peak"], 1)

                    def less(q):
                        dve.wait_ge(e["peak"], b2 * 4 + (q + 1))
                        if q == 0:
                            wait(dve, e["pt"], b2 * 4 - 4)
                        s4 = bank_s[q % 2][:, 0:QW].rearrange("p (g m) -> p g m", g=Q)
                        dve.tensor_tensor(
                            prob[par][:, q * QW:(q + 1) * QW].rearrange("p (g m) -> p g m", g=Q),
                            s4, peak[:, q, :, None].to_broadcast([P, Q, M]), ALU.subtract
                            ).then_inc(e["sub"], 1)

                    if live(2):
                        peaks(0)
                    if live(1):
                        dve.wait_ge(e["rs1"], b1 + 1)
                        wait(dve, e["xnp"], b1 - 1)
                        dve.tensor_scalar(xn[odd][:], row(b1), mom1[odd][:, 0:1], rs1[odd][:],
                                          ALU.subtract, ALU.mult).then_inc(e["xn"], 1)
                    if live(2):
                        less(0)
                        peaks(1)
                    if live(5):
                        dve.wait_ge(e["rs2"], b5 + 1)
                        wait(dve, e["x1p"], b5)
                        dve.tensor_scalar(x1n[:], row(b5), mom2[odd][:, 0:1], rs2[odd][:],
                                          ALU.subtract, ALU.mult).then_inc(e["x1n"], 1)
                    if live(2):
                        less(1)
                    if live(4):
                        dve.wait_ge(e["pv"], b4 * 4 + 4)
                        dve.wait_ge(e["rrep"], b4 + 1)
                        wait(dve, e["wo"], b4)
                        dve.tensor_tensor(attT[:], bank_o[:, 0:S], rrep[:], ALU.mult
                                          ).then_inc(e["att"], 1)
                    if live(3):
                        dve.wait_ge(e["exp"], b3 * 2 + 2)
                        wait(dve, e["rtot"], b3)
                        dve.tensor_reduce(
                            total[:].rearrange("p (g q) -> p q g", q=Q),
                            prob[odd][:, 0:H * M].rearrange("p (q g m) -> p q g m", q=Q, g=Q),
                            AX.X, ALU.add).then_inc(e["total"], 1)
                    if live(3):
                        dve.wait_ge(e["total"], b3 + 1)
                        wait(dve, e["rwide"], b3)
                        dve.reciprocal(rtot[:], total[:]).then_inc(e["rtot"], 1)
                    if live(6):
                        dve.wait_ge(e["tanh"], b6 + 1)
                        dve.wait_ge(e["state"], b6 + 1)
                        dve.scalar_tensor_tensor(out=keep[:], in0=gate[:, 0, :], scalar=1.0,
                                                 in1=state[:], op0=ALU.add, op1=ALU.mult
                                                 ).then_inc(e["mix"], 1)
                        dve.scalar_tensor_tensor(out=fresh[:], in0=gate[:, 1, :], scalar=1.0,
                                                 in1=gate[:, 2, :], op0=ALU.add, op1=ALU.mult
                                                 ).then_inc(e["mix"], 1)
                    if live(4):
                        dve.wait_ge(e["wo"], b4 + 1)
                        dve.tensor_tensor(row(b4), row(b4), bank_w[:, 128:256], ALU.add
                                          ).then_inc(e["x1"], 1)
                    if live(6):
                        dve.wait_ge(e["mix"], b6 * 2 + (2 + MIX0))
                        dve.scalar_tensor_tensor(out=state[:], in0=keep[:], scalar=0.5,
                                                 in1=fresh[:], op0=ALU.mult, op1=ALU.add
                                                 ).then_inc(e["state"], 1)
                    if live(2):
                        peaks(2)
                    if live(4):
                        dve.wait_ge(e["x1"], b4 + 1)
                        wait(dve, e["mom2"], b4)
                        dve.sem_inc(s_tick, 1)
                        dve.bn_stats(stat2[:], row(b4)).then_inc(e["stat2"], 1)
                    if live(2):
                        less(2)
                        peaks(3)
                    if live(4):
                        dve.wait_ge(e["stat2"], b4 + 1)
                        wait(dve, e["x1n"], b4 - 1)
                        dve.sem_inc(s_tick, 1)
                        dve.bn_aggr(mom2[par][:], stat2[:]).then_inc(e["mom2"], 1)
                    if live(2):
                        less(3)
                    if live(0):
                        wait(dve, e["mom1"], b0)
                        dve.sem_inc(s_tick, 1)
                        dve.bn_stats(stat1[:], row(b0)).then_inc(e["stat1"], 1)
                    if live(0):
                        dve.wait_ge(e["stat1"], b0 + 1)
                        wait(dve, e["xn"], b0 - 1)
                        dve.sem_inc(s_tick, 1)
                        dve.bn_aggr(mom1[par][:], stat1[:]).then_inc(e["mom1"], 1)

                batches(dve, 7, body)

            @block.scalar
            def _(act):
                act.activation(warm[:], bcol[:, 0:1], ACT.Exp).then_inc(s_act, 1)

                def body(i, par, live):
                    b1, b2, b3, b4, b5, b6 = (i - n for n in range(1, 7))
                    odd = 1 - par

                    def turned(q):
                        act.wait_ge(e["pt"], b3 * 4 + (q + 1))
                        wait(act, e["pv"], b3 * 4 + (q - 1))
                        act.copy(pts[q % 2][:], bank_t[q % 2][:]).then_inc(e["pte"], 1)

                    def exponentials(half):
                        act.wait_ge(e["sub"], b2 * 4 + (2 * half + 2))
                        part = prob[par][:, 2 * half * QW:(2 * half + 2) * QW]
                        act.activation(part, part, ACT.Exp).then_inc(e["exp"], 1)

                    if live(4):
                        act.wait_ge(e["rp"], b4 + 1)
                        wait(act, e["att"], b4)
                        act.copy(rrep[:], bank_w[:, 0:128]).then_inc(e["rrep"], 1)
                    if live(3):
                        turned(0)
                        turned(1)
                    if live(6):
                        act.wait_ge(e["gates"], b6 + 1)
                        wait(act, e["mix"], b6 * 2 + 3)
                        act.activation(gate[:], bank_g[:, 0:384].rearrange("p (g s) -> p g s", g=3),
                                       ACT.Tanh).then_inc(e["tanh"], 1)
                        act.copy(HX[:, cols(b6)], bank_g[:, 384:512]).then_inc(e["hx"], 1)
                    if live(1):
                        act.wait_ge(e["xnp"], b1 + 1)
                        wait(act, e["qp"], b1)
                        act.copy(xnT[:], bank_x[:, 0:128]).then_inc(e["xnT"], 1)
                    if live(2):
                        exponentials(0)
                    if live(3):
                        turned(2)
                    if live(5):
                        act.wait_ge(e["x1p"], b5 + 1)
                        wait(act, e["gates"], b5)
                        act.copy(x1nT[:], bank_x[:, 256:384]).then_inc(e["x1nT"], 1)
                    if live(3):
                        turned(3)
                    if live(1):
                        act.wait_ge(e["qp"], b1 + 1)
                        wait(act, e["score"], b1 * 4 - 4)
                        act.activation(qT[odd][:], bank_x[:, 128:256], ACT.Copy, scale=QSCALE
                                       ).then_inc(e["q"], 1)
                    if live(2):
                        exponentials(1)
                    if live(3):
                        act.wait_ge(e["rtot"], b3 + 1)
                        wait(act, e["rp"], b3)
                        act.copy(rwide[:], rtot[:, :, None].to_broadcast([P, H, HD])
                                 ).then_inc(e["rwide"], 1)

                batches(act, 7, body)

            @block.gpsimd
            def _(pool):
                def body(i, par, live):
                    b0, b1, b2, b3, b4 = (i - n for n in range(5))
                    odd = 1 - par
                    if live(1):
                        wait(pool, e["score"], b1 * 4 - 4)
                        pool.tensor_tensor(
                            kblk[odd].rearrange("p (h m) -> p h m", m=M),
                            kT[:, None, bass.ds(b1 * M, M)].to_broadcast([P, H, M]),
                            cst[:, C_KM:C_KM + H, None].to_broadcast([P, H, M]), ALU.mult
                            ).then_inc(e["kb"], 1)
                    if live(2):
                        wait(pool, e["pv"], b2 * 4 - 4)
                        pool.tensor_tensor(
                            vm[par][0:M], V[:, None, cols(b2)].to_broadcast([M, Q, D]),
                            cst[0:M, C_VM:C_VM + Q * D].rearrange("p (q d) -> p q d", q=Q), ALU.mult
                            ).then_inc(e["vm"], 1)
                    if live(4):
                        pool.wait_ge(e["mom2"], b4 + 1)
                        wait(pool, e["rs2"], b4)
                        pool.tensor_tensor(ve2[:], mom2[par][:, 1:2], col(EPS5), ALU.add
                                           ).then_inc(e["ve2"], 1)
                        pool.wait_ge(e["ve2"], b4 + 1)
                        wait(pool, e["x1n"], b4 - 1)
                        pool.tensor_tensor(rs2[par][:], ve2[:], col(NHALF), ALU.pow
                                           ).then_inc(e["rs2"], 1)
                    if live(0):
                        pool.wait_ge(e["mom1"], b0 + 1)
                        wait(pool, e["rs1"], b0)
                        pool.tensor_tensor(ve1[:], mom1[par][:, 1:2], col(EPS5), ALU.add
                                           ).then_inc(e["ve1"], 1)
                        pool.wait_ge(e["ve1"], b0 + 1)
                        wait(pool, e["xn"], b0 - 1)
                        pool.tensor_tensor(rs1[par][:], ve1[:], col(NHALF), ALU.pow
                                           ).then_inc(e["rs1"], 1)

                batches(pool, 7, body)

            @block.tensor
            def _(pe):
                def body(i, par, live):
                    b1, b2, b3, b4, b5, b6 = (i - n for n in range(1, 7))
                    odd = 1 - par

                    def scores(q):
                        bank = bank_s[q % 2][:, 0:QW]
                        wait(pe, e["sub"], b2 * 4 + (q - 1))
                        pe.matmul(bank.rearrange("p (g m) -> p g m", g=Q), onesb[:],
                                  maskneg[:, None, bass.ds(b2 * M, M)].to_broadcast([P, Q, M]),
                                  start=True, stop=False)
                        pe.matmul(bank, qT[par][:], kblk[par][:, q * QW:(q + 1) * QW],
                                  start=False, stop=True).then_inc(e["score"], 1)

                    def turn(q):
                        wait(pe, e["pte"], b3 * 4 + (q - 1))
                        for g in range(Q):
                            at = (Q * q + g) * M
                            mm = pe.transpose(bank_t[q % 2][:, g * S:(g + 1) * S],
                                              prob[odd][:, at:at + P], ident)
                        mm.then_inc(e["pt"], 1)

                    def values(q):
                        pe.wait_ge(e["pte"], b3 * 4 + (q + 1))
                        for g in range(Q):
                            mm = pe.matmul(bank_o[32 * g:32 * g + 32, 0:S],
                                           vm[odd][:, q, 32 * g:32 * g + 32],
                                           pts[q % 2][:, g * S:(g + 1) * S],
                                           start=(q == 0), stop=(q == Q - 1))
                        mm.then_inc(e["pv"], 1)

                    if live(2):
                        pe.wait_ge(e["kb"], b2 + 1)
                        pe.wait_ge(e["q"], b2 + 1)
                        scores(0)
                        scores(1)
                    if live(4):
                        pe.wait_ge(e["rwide"], b4 + 1)
                        wait(pe, e["x1"], b4)
                        pe.matmul(bank_w[:, 0:128], rwide[:].rearrange("p h d -> p (h d)"), ident,
                                  start=True, stop=True).then_inc(e["rp"], 1)
                    if live(6):
                        pe.wait_ge(e["x1nT"], b6 + 1)
                        wait(pe, e["tanh"], b6)
                        wait(pe, e["hx"], b6)
                        for n in range(3):
                            pe.matmul(bank_g[:, n * S:(n + 1) * S], bsplit[:, n, :], onesb[:],
                                      start=(n == 0), stop=False, skip_group_check=True)
                        for n, w in enumerate((WF, WI, WC)):
                            pe.matmul(bank_g[:, n * S:(n + 1) * S], w, x1nT[:], start=False,
                                      stop=False, skip_group_check=True)
                        pe.matmul(bank_g[:, 384:512], x1nT[:], WOF, start=False, stop=False,
                                  skip_group_check=True)
                        pe.wait_ge(e["state"], b6 + 1)
                        for n, w in enumerate((UF, UI, UC)):
                            mm = pe.matmul(bank_g[:, n * S:(n + 1) * S], w, state[:], start=False,
                                           stop=(n == 2), skip_group_check=True)
                        mm.then_inc(e["gates"], 1)
                    if live(3):
                        pe.wait_ge(e["exp"], b3 * 2 + 2)
                        turn(0)
                        turn(1)
                    if live(4):
                        pe.wait_ge(e["att"], b4 + 1)
                        pe.matmul(bank_w[:, 128:256], attT[:], WO, start=True, stop=True
                                  ).then_inc(e["wo"], 1)
                    if live(1):
                        pe.wait_ge(e["xn"], b1 + 1)
                        wait(pe, e["q"], b1)
                        wait(pe, e["x1nT"], i - 5)
                        pe.transpose(bank_x[:, 0:128], xn[odd][:], ident).then_inc(e["xnp"], 1)
                    if live(3):
                        wait(pe, e["att"], b3)
                        pe.wait_ge(e["vm"], b3 + 1)
                        values(0)
                    if live(2):
                        scores(2)
                    if live(3):
                        turn(2)
                        values(1)
                    if live(5):
                        pe.wait_ge(e["x1n"], b5 + 1)
                        if live(1):
                            pe.wait_ge(e["xnT"], b1 + 1)
                        else:
                            pe.wait_ge(e["q"], B)
                            pe.wait_ge(e["x1nT"], b5)
                        pe.transpose(bank_x[:, 256:384], x1n[:], ident).then_inc(e["x1p"], 1)
                    if live(2):
                        scores(3)
                    if live(3):
                        turn(3)
                    if live(1):
                        pe.wait_ge(e["xnT"], b1 + 1)
                        if live(5):
                            pe.wait_ge(e["x1nT"], b5 + 1)
                        pe.matmul(bank_x[:, 128:256], WQ, xnT[:], start=True, stop=True
                                  ).then_inc(e["qp"], 1)
                    if live(3):
                        values(2)
                        values(3)

                batches(pe, 7, body)

        GW = G4 * D
        cfin = sb("cfin", [P, D])
        mom3 = [sb(f"mom3_{n}", [P, G4, 2]) for n in range(2)]
        stat3 = sb("stat3", [P, G4, 6])
        ve3, rs3 = sb("ve3", [P, G4]), [sb(f"rs3_{n}", [P, G4]) for n in range(2)]
        shift3 = [sb(f"shift3_{n}", [P, G4]) for n in range(2)]
        mags = sb("mags", [P, NG])
        f = {n: sem("f_" + n) for n in "cf cfin pre tanh x2 stat mom ve rs shift ln mag".split()}

        def group(t, g):
            return t[:, bass.ds(g * GW, GW)]

        def four(ap):
            return ap.rearrange("p (j d) -> p j d", j=G4)

        with nc.Block() as block:
            @block.tensor
            def _(pe):
                pe.matmul(ps[0][:, 0:D], state[:], UO, start=True, stop=True).then_inc(f["cf"], 1)

            @block.vector
            def _(dve):
                dve.wait_ge(f["cf"], 1)
                dve.tensor_tensor(cfin[:], ps[0][:, 0:D], brep[:, 0, :], ALU.add
                                  ).then_inc(f["cfin"], 1)
                dve.wait_ge(f["cfin"], 1)

                def body(i, par, live):
                    odd = 1 - par
                    g2, g3, g5 = i - 2, i - 3, i - 5
                    if live(3):
                        dve.wait_ge(f["rs"], g3 + 1)
                        wait(dve, f["ln"], g3 - 1)
                        dve.scalar_tensor_tensor(
                            out=shift3[odd][:], in0=mom3[odd][:, :, 0], scalar=-1.0,
                            in1=rs3[odd][:], op0=ALU.mult, op1=ALU.mult).then_inc(f["shift"], 1)
                    if live(0):
                        dve.tensor_tensor(four(group(HX, i)), four(group(HX, i)),
                                          cfin[:, None, :].to_broadcast([P, G4, D]), ALU.add
                                          ).then_inc(f["pre"], 1)
                    if live(2):
                        dve.wait_ge(f["x2"], g2 + 1)
                        wait(dve, f["mom"], g2 * G4)
                        for j in range(G4):
                            dve.sem_inc(s_tick, 1)
                            dve.bn_stats(stat3[:, j, :], row(g2 * G4 + j)
                                         ).then_inc(f["stat"], 1)
                    if live(5):
                        dve.wait_ge(f["ln"], g5 + 1)
                        dve.tensor_reduce(mags[:, bass.ds(g5, 1)], group(R3, g5), AX.X, ALU.max,
                                          apply_absolute_value=True).then_inc(f["mag"], 1)
                    if live(2):
                        dve.wait_ge(f["stat"], g2 * G4 + G4)
                        wait(dve, f["ln"], g2 - 1)
                        for j in range(G4):
                            dve.sem_inc(s_tick, 1)
                            dve.bn_aggr(mom3[par][:, j, :], stat3[:, j, :]).then_inc(f["mom"], 1)

                batches(dve, 6, body, NG)
                dve.wait_ge(f["mag"], NG)
                dve.tensor_reduce(col(AMAX), mags[:], AX.X, ALU.max).then_inc(s_allin, 1)
                quantum(dve, 4)
                dlink(dve, dve.tensor_tensor(col(K_TXT), col(IS), col(WS + 2), ALU.mult))

            @block.scalar
            def _(act):
                act.activation(warm[:], bcol[:, 0:1], ACT.Exp).then_inc(s_act, 1)

                def body(i, par, live):
                    if live(0):
                        act.wait_ge(f["pre"], i + 1)
                        act.activation(group(HX, i), group(HX, i), ACT.Tanh).then_inc(f["tanh"], 1)
                    if live(3):
                        g = i - 3
                        act.wait_ge(f["shift"], g + 1)
                        for j in range(G4):
                            ins = act.activation(
                                R3[:, bass.ds((g * G4 + j) * D, D)], row(g * G4 + j),
                                ACT.Identity, bias=shift3[1 - par][:, j:j + 1],
                                scale=rs3[1 - par][:, j:j + 1])
                        ins.then_inc(f["ln"], 1)

                batches(act, 6, body, NG)

            @block.gpsimd
            def _(pool):
                def body(i, par, live):
                    g1, g2 = i - 1, i - 2
                    if live(1):
                        pool.wait_ge(f["tanh"], g1 + 1)
                        pool.tensor_tensor(rows4(g1), rows4(g1), four(group(HX, g1)), ALU.add
                                           ).then_inc(f["x2"], 1)
                    if live(2):
                        pool.wait_ge(f["mom"], g2 * G4 + G4)
                        wait(pool, f["rs"], g2)
                        pool.tensor_tensor(ve3[:], mom3[par][:, :, 1], col(EPS5).to_broadcast([P, G4]),
                                           ALU.add).then_inc(f["ve"], 1)
                        pool.wait_ge(f["ve"], g2 + 1)
                        wait(pool, f["ln"], g2 - 1)
                        pool.tensor_tensor(rs3[par][:], ve3[:], col(NHALF).to_broadcast([P, G4]),
                                           ALU.pow).then_inc(f["rs"], 1)

                batches(pool, 6, body, NG)
                pool.wait_ge(s_allin, 4)
                pool.partition_all_reduce(col(AALL), col(AMAX), P, RMAX).then_inc(s_allout, 1)

        FT = R2
        MW = G4 * M
        EW = MW + (P - M) + 1
        ISE = float(D) ** -0.5
        used = {"work": 0, "kT": 0, "maskneg": 0}
        room = {"work": work[:], "kT": kT[:], "maskneg": maskneg[:].bitcast(F32)}

        def lend(width, dt=F32):
            words = -(-width * 2 // 4) if dt == BF16 else width
            for name, tile in room.items():
                at = used[name]
                if at + words <= tile.shape[1]:
                    used[name] += words
                    t = tile[:, at:at + words]
                    return t.bitcast(dt)[:, 0:width] if dt != F32 else t
            raise AssertionError("no room")

        tq = lend(GW)
        qx = [lend(GW, BF16) for n in range(2)]
        qxT = lend(GW, BF16)
        fus = [[lend(GW) for n in range(4)], [vm[n][:].rearrange("p q d -> p (q d)") for n in range(2)]
               + [pts[n][:] for n in range(2)]]
        kx = [lend(MW) for n in range(2)]
        kp = [lend(2 * GW).rearrange("p (t c) -> p t c", t=2) for n in range(2)]
        p3 = [[lend(EW) for t in range(2)] for n in range(2)]
        p3T = [lend(GW) for n in range(2)]
        mx = [sb(f"mx{n}", [P, G4]) for n in range(2)]
        sm = [sb(f"sm{n}", [P, G4]) for n in range(2)]
        rc = [sb(f"rc{n}", [P, G4]) for n in range(2)]
        b01 = sb("b01", [P, 2])
        scored = ps[3][:, 0:MW], ps[7][:, 0:MW]
        valued = ps[6], ps[1]
        LAY = ("a", "b")
        h = {n: sem("h_" + n) for n in "tq qx qp qT fp fused done mag".split()}
        for n in "kp_ kx kv_ kv score peak sub exp sum rec norm pt pte out add".split():
            for l in LAY:
                h[n + l] = sem("h_" + n + l)

        with nc.Block() as block:
            @block.vector
            def _(dve):
                for n in range(2):
                    dlink(dve, dve.memset(kp[n], 0.0))
                    for t in range(2):
                        dlink(dve, dve.memset(p3[n][t][:, MW:EW], 0.0))
                dlink(dve, dve.tensor_scalar(b01[:], bcol[:, 3:5], 0.1, None, ALU.mult))
                dve.memset(sm[0][:], 0.0).then_inc(h["done"], 1)

                def peaks(l, g):
                    L, s4 = LAY[l], scored[l].rearrange("p (j m) -> p j m", m=M)
                    dve.wait_ge(h["score" + L], g + 1)
                    wait(dve, h["sub" + L], g)
                    dve.tensor_reduce(mx[l][:], s4, AX.X, ALU.max).then_inc(h["peak" + L], 1)

                def less(l, g, par):
                    L, s4 = LAY[l], scored[l].rearrange("p (j m) -> p j m", m=M)
                    p = p3[l][par][:, 0:MW].rearrange("p (j m) -> p j m", m=M)
                    dve.wait_ge(h["peak" + L], g + 1)
                    wait(dve, h["pt" + L], g - 1)
                    dve.tensor_tensor(p, s4, mx[l][:, :, None].to_broadcast([P, G4, M]), ALU.subtract
                                      ).then_inc(h["sub" + L], 1)

                def normalise(l, g, par):
                    L, p = LAY[l], p3[l][par][:, 0:MW].rearrange("p (j m) -> p j m", m=M)
                    dve.wait_ge(h["exp" + L], g + 1)
                    wait(dve, h["rec" + L], g)
                    dve.tensor_reduce(sm[l][:], p, AX.X, ALU.add).then_inc(h["sum" + L], 1)
                    dve.wait_ge(h["sum" + L], g + 1)
                    wait(dve, h["norm" + L], g)
                    dve.reciprocal(rc[l][:], sm[l][:]).then_inc(h["rec" + L], 1)
                    dve.wait_ge(h["rec" + L], g + 1)
                    dve.scalar_tensor_tensor(
                        out=p, in0=p, scalar=0.1, in1=rc[l][:, :, None].to_broadcast([P, G4, M]),
                        op0=ALU.mult, op1=ALU.mult).then_inc(h["norm" + L], 1)

                def body(i, ph, live):
                    g0, g2, g4, g5, g7 = (i - n for n in (0, 2, 4, 5, 7))
                    par, odd = ph % 2, (ph + 1) % 2
                    if live(4):
                        dve.wait_ge(h["outa"], g4 + 1)
                        wait(dve, h["addb"], g4 - 3)
                        dve.scalar_tensor_tensor(out=fus[1][ph], in0=valued[0], scalar=b01[:, 0:1],
                                                 in1=fus[0][ph], op0=ALU.add, op1=ALU.add
                                                 ).then_inc(h["adda"], 1)
                    if live(2):
                        peaks(0, g2)
                    if live(5):
                        peaks(1, g5)
                    if live(2):
                        less(0, g2, par)
                    if live(5):
                        less(1, g5, odd)
                    if live(7):
                        dve.wait_ge(h["outb"], g7 + 1)
                        dve.scalar_tensor_tensor(out=group(FT, g7), in0=valued[1],
                                                 scalar=b01[:, 1:2], in1=fus[1][(ph + 1) % 4],
                                                 op0=ALU.add, op1=ALU.add).then_inc(h["addb"], 1)
                    if live(0):
                        dve.wait_ge(h["tq"], g0 + 1)
                        wait(dve, h["qp"], g0 - 1)
                        dve.tensor_scalar(qx[par], tq, MAGIC, None, ALU.subtract).then_inc(h["qx"], 1)
                    if live(2):
                        normalise(0, g2, par)
                    if live(7):
                        dve.wait_ge(h["addb"], g7 + 1)
                        dve.tensor_reduce(mags[:, bass.ds(g7, 1)], group(FT, g7), AX.X, ALU.max,
                                          apply_absolute_value=True).then_inc(h["mag"], 1)
                    if live(5):
                        normalise(1, g5, odd)

                batches(dve, 8, body, NG, 4)

            @block.scalar
            def _(act):
                act.activation(warm[:], bcol[:, 0:1], ACT.Exp).then_inc(s_act, 1)
                act.wait_ge(h["done"], 1)

                def keys(l, g):
                    L = LAY[l]
                    act.wait_ge(h["kp_" + L], g + 1)
                    wait(act, h["score" + L], g)
                    act.activation(kx[l], ps[2][:, 0:MW], ACT.Identity,
                                   bias=bcol[:, 3 + l:4 + l], scale=col(K_A[l])
                                   ).then_inc(h["kx" + L], 1)

                def weighed(l, g, par):
                    L = LAY[l]
                    act.wait_ge(h["kv_" + L], g + 1)
                    wait(act, h["out" + L], g - 1)
                    act.activation(kp[l][0:M, par, :], ps[4][0:M, :], ACT.Copy,
                                   scale=col(K_A[l], M)).then_inc(h["kv" + L], 1)

                def exponential(l, g, par):
                    L, p = LAY[l], p3[l][par][:, 0:MW]
                    act.wait_ge(h["sub" + L], g + 1)
                    act.activation(p, p, ACT.Exp, scale=ISE).then_inc(h["exp" + L], 1)

                def turned(l, g):
                    L = LAY[l]
                    act.wait_ge(h["pt" + L], g + 1)
                    wait(act, h["out" + L], g)
                    act.copy(p3T[l], ps[5][:]).then_inc(h["pte" + L], 1)

                def body(i, ph, live):
                    g0, g1, g2, g3, g4, g5, g6 = (i - n for n in range(7))
                    par, odd = ph % 2, (ph + 1) % 2
                    if live(0):
                        wait(act, h["qx"], g0)
                        act.activation(tq, group(R3, g0), ACT.Copy, bias=MAGIC, scale=col(INV)
                                       ).then_inc(h["tq"], 1)
                    if live(3):
                        turned(0, g3)
                    if live(1):
                        act.wait_ge(h["qp"], g1 + 1)
                        wait(act, h["fp"], g1)
                        act.copy(qxT, ps[0][:].bitcast(BF16)[:, 0:GW]).then_inc(h["qT"], 1)
                        keys(0, g1)
                    if live(2):
                        exponential(0, g2, par)
                        weighed(0, g2, par)
                    if live(5):
                        exponential(1, g5, odd)
                    if live(6):
                        turned(1, g6)
                    if live(4):
                        keys(1, g4)
                    if live(5):
                        weighed(1, g5, odd)
                    if live(1):
                        act.wait_ge(h["fp"], g1 + 1)
                        wait(act, h["adda"], g1 - 3)
                        act.activation(fus[0][(ph + 3) % 4], ps[0][:], ACT.Identity,
                                       bias=bcol[:, 2:3], scale=col(K_TXT)).then_inc(h["fused"], 1)

                batches(act, 8, body, NG, 4)

            @block.tensor
            def _(pe):
                pe.wait_ge(h["done"], 1)
                tb = ps[0][:].bitcast(BF16)

                def keys(l, g):
                    pe.matmul(ps[2][:, 0:MW], ternd["att" + str(l)], qimg[:, bass.ds(g * MW, MW)],
                              start=True, stop=True).then_inc(h["kp_" + LAY[l]], 1)

                def weighed(l, g):
                    for j in range(G4):
                        mm = pe.matmul(ps[4][0:M, j * D:(j + 1) * D],
                                       qimg[:, bass.ds((g * G4 + j) * M, M)], ternd["att" + str(l)],
                                       start=True, stop=True)
                    mm.then_inc(h["kv_" + LAY[l]], 1)

                def scores(l, g, ph):
                    L = LAY[l]
                    pe.wait_ge(h["kx" + L], g + 1)
                    wait(pe, h["sub" + L], g)
                    for j in range(G4):
                        mm = pe.matmul(scored[l][:, j * M:(j + 1) * M],
                                       fus[l][ph][:, j * S:(j + 1) * S],
                                       kx[l][:, j * M:(j + 1) * M], start=True, stop=True)
                    mm.then_inc(h["score" + L], 1)

                def turn(l, g, par):
                    L = LAY[l]
                    pe.wait_ge(h["norm" + L], g + 1)
                    for j in range(G4):
                        mm = pe.transpose(ps[5][:, j * S:(j + 1) * S],
                                          p3[l][par][:, j * M:j * M + P], ident)
                    mm.then_inc(h["pt" + L], 1)

                def values(l, g, par):
                    L = LAY[l]
                    pe.wait_ge(h["pte" + L], g + 1)
                    pe.wait_ge(h["kv" + L], g + 1)
                    wait(pe, h["add" + L], g)
                    for j in range(G4):
                        mm = pe.matmul(valued[l][:, j * S:(j + 1) * S],
                                       kp[l][:, par, j * D:(j + 1) * D],
                                       p3T[l][:, j * S:(j + 1) * S], start=True, stop=True)
                    mm.then_inc(h["out" + L], 1)

                def upto(n):
                    return min(n, NG) if isinstance(n, int) else n

                def body(i, ph, live):
                    g0, g1, g2, g3, g4, g5, g6 = (i - n for n in range(7))
                    par, odd = ph % 2, (ph + 1) % 2
                    if live(2):
                        pe.wait_ge(h["fused"], g2 + 1)
                        scores(0, g2, (ph + 2) % 4)
                    if live(5):
                        pe.wait_ge(h["adda"], g5 + 1)
                        scores(1, g5, (ph + 3) % 4)
                    if live(3):
                        wait(pe, h["pteb"], g3 - 3)
                        turn(0, g3, odd)
                    if live(1):
                        pe.wait_ge(h["qx"], g1 + 1)
                        wait(pe, h["fused"], g1)
                        for j in range(G4):
                            mm = pe.transpose(tb[:, j * S:(j + 1) * S],
                                              qx[odd][:, j * D:(j + 1) * D], identb[:])
                        mm.then_inc(h["qp"], 1)
                        wait(pe, h["kxb"], g1 - 3)
                        keys(0, g1)
                    if live(2):
                        wait(pe, h["kvb"], g2 - 3)
                        weighed(0, g2)
                    if live(3):
                        values(0, g3, odd)
                    if live(6):
                        pe.wait_ge(h["ptea"], upto(g6 + 4))
                        wait(pe, h["pteb"], g6)
                        turn(1, g6, par)
                    if live(4):
                        pe.wait_ge(h["kxa"], upto(g4 + 4))
                        wait(pe, h["kxb"], g4)
                        keys(1, g4)
                    if live(5):
                        pe.wait_ge(h["kva"], upto(g5 + 4))
                        wait(pe, h["kvb"], g5)
                        weighed(1, g5)
                    if live(1):
                        pe.wait_ge(h["qT"], g1 + 1)
                        pe.matmul(ps[0][:], ternd["txt"], qxT, start=True, stop=True
                                  ).then_inc(h["fp"], 1)
                    if live(6):
                        values(1, g6, par)

                batches(pe, 8, body, NG, 4)

        for n in used:
            used[n] = 0
        qf = R3[:].bitcast(BF16)
        qavg = lend(B, BF16)
        tq = [lend(GW) for n in range(2)]
        hpk = lend(NG * 4)
        hm = lend(4)
        f1w = ternd["f1"].rearrange("p (k n) -> p k n", k=2)
        f2w = ternd["f2"].rearrange("p (k n) -> p k n", k=4)
        m = {n: sem("m_" + n) for n in "qavg tq qf f1 peak b2 blank fill".split()}
        blank = sb("blank", [P, RW])
        sorted_rows = nc.dram_tensor("sorted_rows", (SORTED, RW), F32, kind="Internal").ap()

        def hidden(pe, bank, g, c):
            pe.matmul(bank, f1w[:, 0, c * P:(c + 1) * P], group(qf, g), start=True, stop=False)
            return pe.matmul(four(bank), f1w[:, 1, c * P:(c + 1) * P],
                             qavg[:, bass.ds(g * G4, G4), None].to_broadcast([P, G4, S]),
                             start=False, stop=True)

        with nc.Block() as block:
            @block.sync
            def _(sp):
                sp.wait_ge(m["blank"], 2)
                sp.dma_start(sorted_rows.rearrange("(p k) w -> p k w", p=P),
                             blank[:, None, :].to_broadcast([P, SORTED // P, RW])
                             ).then_inc(m["fill"], 16)
                sp.wait_ge(m["fill"], 16)

            @block.vector
            def _(dve):
                dlink(dve, dve.tensor_reduce(hm[:, 0:1], mags[:], AX.X, ALU.max))
                dlink(dve, dve.tensor_reduce(hm[:, 1:2], avgT[:], AX.X, ALU.max,
                                             apply_absolute_value=True))
                dve.tensor_tensor(col(AMAX), hm[:, 0:1], hm[:, 1:2], ALU.max).then_inc(s_allin, 1)
                quantum(dve, 5)
                dlink(dve, dve.tensor_tensor(col(K_F1), col(IS), col(WS + 5), ALU.mult))
                dlink(dve, dve.tensor_scalar(avgT[:], avgT[:], col(INV), MAGIC, ALU.mult, ALU.add))
                dve.tensor_scalar(qavg, avgT[:], MAGIC, None, ALU.subtract).then_inc(m["qavg"], 1)

                def body(i, par, live):
                    if live(0):
                        dve.wait_ge(m["tq"], i + 1)
                        dve.tensor_scalar(group(qf, i), tq[par], MAGIC, None, ALU.subtract
                                          ).then_inc(m["qf"], 1)
                    if live(1):
                        g = i - 1
                        dve.wait_ge(m["f1"], g + 1)
                        dve.tensor_reduce(hpk[:, bass.ds(g * 4, 4)],
                                          psum[:, 4 * (1 - par):4 * (1 - par) + 4, :], AX.X, ALU.max
                                          ).then_inc(m["peak"], 1)

                batches(dve, 2, body, NG)
                dve.wait_ge(m["peak"], NG)
                dlink(dve, dve.tensor_reduce(hm, hpk.rearrange("p (g c) -> p c g", c=4), AX.X, ALU.max))
                dlink(dve, dve.scalar_tensor_tensor(out=hm, in0=hm, scalar=col(K_F1),
                                                    in1=bcol[:, 5:9], op0=ALU.mult, op1=ALU.add))
                dlink(dve, dve.tensor_reduce(hm[:, 0:1], hm, AX.X, ALU.max))
                dve.tensor_scalar(col(AMAX), hm[:, 0:1], 0.0, None, ALU.max).then_inc(s_allin, 1)
                quantum(dve, 6)
                dlink(dve, dve.tensor_tensor(col(K_H), col(K_F1), col(INV), ALU.mult))
                dlink(dve, dve.tensor_tensor(col(K_F2), col(IS), col(WS + 6), ALU.mult))
                dlink(dve, dve.tensor_scalar(sc[:, B_F1:B_F1 + 4], bcol[:, 5:9], col(INV), None,
                                             ALU.mult))

            @block.scalar
            def _(act):
                act.wait_ge(m["qavg"], 1)

                def body(i, par, live):
                    if live(0):
                        wait(act, m["qf"], i - 1)
                        act.activation(tq[par], group(FT, i), ACT.Copy, bias=MAGIC, scale=col(INV)
                                       ).then_inc(m["tq"], 1)

                batches(act, 2, body, NG)

            @block.gpsimd
            def _(pool):
                pool.wait_ge(s_allin, 5)
                pool.partition_all_reduce(col(AALL), col(AMAX), P, RMAX).then_inc(s_allout, 1)
                with pool.Fori(0, NG) as g:
                    pool.tensor_tensor(rows4(g), rows4(g), brep[:, 1:2, :].to_broadcast([P, G4, D]),
                                       ALU.add).then_inc(m["b2"], 1)
                pool.wait_ge(s_allin, 6)
                pool.partition_all_reduce(col(AALL), col(AMAX), P, RMAX).then_inc(s_allout, 1)
                pool.memset(blank[:], 0.0).then_inc(m["blank"], 1)
                pool.wait_ge(m["blank"], 1)
                pool.memset(blank[:].bitcast(I32)[:, D + TOKEN:D + TOKEN + 1], NT).then_inc(m["blank"], 1)
                pool.iota(X[:].bitcast(I32)[:, :, D + TOKEN], [[P, B]], base=0, channel_multiplier=1
                          ).then_inc(m["b2"], 1)

            @block.tensor
            def _(pe):
                pe.wait_ge(m["qavg"], 1)

                def body(i, par, live):
                    if live(1):
                        g = i - 1
                        pe.wait_ge(m["qf"], g + 1)
                        wait(pe, m["peak"], g - 1)
                        for c in range(4):
                            mm = hidden(pe, ps[4 * (1 - par) + c], g, c)
                        mm.then_inc(m["f1"], 1)

                batches(pe, 2, body, NG)

        for n in used:
            used[n] = 0
        qavg = lend(B, BF16)
        W1 = R2[:, 0:E * F]
        W2 = R2[:, E * F:2 * E * F]
        relu = [lend(GW) for n in range(4)]
        qh = [lend(4 * GW, BF16).rearrange("p (c t) -> p c t", c=4) for n in range(2)]
        xs = lend(GW)
        xsT = lend(GW)
        stat4 = sb("stat4", [P, G4, 6])
        mom4 = sb("mom4", [P, G4, 2])
        gw = sb("gw", [P, E])
        ms2 = sb("ms2", [P, G4])
        logit = sb("logit", [P, E, B])
        x = {n: sem("x_" + n) for n in
             "w gw f1 relu qh f2 x3 xs stat mom ms mean rs xp xsT gate logit".split()}

        def extra(n, g=None):
            if g is None:
                return X[:, :, D + n]
            return Xf[:, bass.ds(g * (G4 * RW), G4 * RW)].rearrange(
                "p (j w) -> p j w", j=G4)[:, :, D + n]

        with nc.Block() as block:
            @block.sync
            def _(sp):
                for e_ in range(E):
                    sp.dma_start(W1[:, e_ * F:(e_ + 1) * F], a["w1"][e_]).then_inc(x["w"], 16)
                    sp.dma_start(W2[:, e_ * F:(e_ + 1) * F].rearrange("p (c d) -> p c d", c=4),
                                 a["w2"][e_].rearrange("(c p) d -> p c d", p=P)).then_inc(x["w"], 16)
                sp.dma_start(gw[:], a["gw"]).then_inc(x["gw"], 16)
                sp.wait_ge(x["w"], 32 * E)

            @block.vector
            def _(dve):
                dve.wait_ge(x["gw"], 16)
                dve.tensor_scalar(gw[:], gw[:], bcol[:, 10:11], None, ALU.mult).then_inc(x["gw"], 1)

                def body(i, par, live):
                    g1, g2, g3, g4 = (i - n for n in range(1, 5))
                    if live(1):
                        wait(dve, x["f2"], g1 - 1)
                        for c in range(4):
                            dve.wait_ge(x["relu"], g1 * 4 + (c + 1))
                            dve.tensor_scalar(qh[1 - par][:, c, :], relu[c], MAGIC, MAGIC, ALU.add,
                                              ALU.subtract).then_inc(x["qh"], 1)
                    if live(3):
                        dve.wait_ge(x["rs"], g3 + 1)
                        dve.wait_ge(x["mean"], g3 + 1)
                        wait(dve, x["xp"], g3)
                        for j in range(G4):
                            dve.tensor_scalar(xs[:, j * D:(j + 1) * D], row(g3 * G4 + j),
                                              extra(MEAN, g3)[:, j:j + 1], extra(RSTD, g3)[:, j:j + 1],
                                              ALU.subtract, ALU.mult).then_inc(x["xs"], 1)
                    if live(2):
                        dve.wait_ge(x["f2"], g2 + 1)
                        dve.scalar_tensor_tensor(out=rows4(g2), in0=four(ps[4]), scalar=col(K_F2),
                                                 in1=rows4(g2), op0=ALU.mult, op1=ALU.add
                                                 ).then_inc(x["x3"], 1)
                        dve.wait_ge(x["x3"], g2 + 1)
                        wait(dve, x["mom"], g2 * G4)
                        for j in range(G4):
                            dve.sem_inc(s_tick, 1)
                            dve.bn_stats(stat4[:, j, :], row(g2 * G4 + j)).then_inc(x["stat"], 1)
                        dve.wait_ge(x["stat"], g2 * G4 + G4)
                        wait(dve, x["ms"], g2)
                        wait(dve, x["mean"], g2)
                        for j in range(G4):
                            dve.sem_inc(s_tick, 1)
                            dve.bn_aggr(mom4[:, j, :], stat4[:, j, :]).then_inc(x["mom"], 1)
                        dve.wait_ge(x["mom"], g2 * G4 + G4)
                        wait(dve, x["rs"], g2)
                        dve.tensor_scalar(ms2[:], mom4[:, :, 1], 1.0 + 1e-6, 1e-11, ALU.mult, ALU.add
                                          ).then_inc(x["ms"], 1)
                        dve.tensor_copy(extra(MEAN, g2), mom4[:, :, 0]).then_inc(x["mean"], 1)
                    if live(4):
                        dve.wait_ge(x["gate"], g4 + 1)
                        dve.tensor_copy(logit[:, :, bass.ds(g4 * G4, G4)],
                                        ps[6][:, 0:G4 * E].rearrange("p (j e) -> p e j", e=E)
                                        ).then_inc(x["logit"], 1)

                batches(dve, 5, body, NG)

            @block.scalar
            def _(act):
                def body(i, par, live):
                    g3 = i - 3
                    if live(0):
                        for c in range(4):
                            act.wait_ge(x["f1"], i * 4 + (c + 1))
                            wait(act, x["qh"], i * 4 + (c - 3))
                            act.activation(relu[c], ps[c], ACT.Relu, scale=col(K_H),
                                           bias=col(B_F1 + c)).then_inc(x["relu"], 1)
                    if live(3):
                        act.wait_ge(x["xp"], g3 + 1)
                        wait(act, x["gate"], g3)
                        act.copy(xsT, ps[5]).then_inc(x["xsT"], 1)

                batches(act, 5, body, NG)

            @block.gpsimd
            def _(pool):
                def body(i, par, live):
                    g2 = i - 2
                    if live(2):
                        pool.wait_ge(x["ms"], g2 + 1)
                        pool.tensor_tensor(extra(RSTD, g2), ms2[:], col(NHALF).to_broadcast([P, G4]),
                                           ALU.pow).then_inc(x["rs"], 1)

                batches(pool, 5, body, NG)

            @block.tensor
            def _(pe):
                pe.wait_ge(x["gw"], 17)

                def body(i, par, live):
                    g1, g3, g4 = i - 1, i - 3, i - 4
                    if live(0):
                        for c in range(4):
                            wait(pe, x["relu"], i * 4 + (c - 3))
                            hidden(pe, ps[c], i, c).then_inc(x["f1"], 1)
                    if live(4):
                        pe.wait_ge(x["xsT"], g4 + 1)
                        wait(pe, x["logit"], g4)
                        for j in range(G4):
                            mm = pe.matmul(ps[6][:, j * E:(j + 1) * E], xsT[:, j * S:(j + 1) * S],
                                           gw[:], start=True, stop=True)
                        mm.then_inc(x["gate"], 1)
                    if live(3):
                        pe.wait_ge(x["xs"], g3 * G4 + G4)
                        wait(pe, x["xsT"], g3)
                        for j in range(G4):
                            mm = pe.transpose(ps[5][:, j * S:(j + 1) * S], xs[:, j * D:(j + 1) * D],
                                              ident)
                        mm.then_inc(x["xp"], 1)
                    if live(1):
                        pe.wait_ge(x["qh"], g1 * 4 + 4)
                        wait(pe, x["x3"], g1)
                        for j in range(G4):
                            for c in range(4):
                                mm = pe.matmul(ps[4][:, j * D:(j + 1) * D],
                                               qh[1 - par][:, c, j * S:(j + 1) * S], f2w[:, c, :],
                                               start=(c == 0), stop=(c == 3))
                        mm.then_inc(x["f2"], 1)

                batches(pe, 5, body, NG)

        for n in used:
            used[n] = 0
        EB = E * B
        cube = lambda t: t.rearrange("p (e b) -> p e b", e=E)
        pe_, choice, count, thr, before = (lend(EB) for n in range(5))
        ohb = lend(EB, BF16)
        trib = lend(P, BF16)
        ones = lend(EB)
        best, total5, rec5, pick, pos = (lend(B) for n in range(5))
        ends, tiles, incl, shift = lend(E + 1), lend(E), lend(E), lend(E)
        cmp = lend(TILES * E)
        et = lend(TILES)
        posi = sb("posi", [P, B], I32)
        wat = sb("wat", [1, TILES], I32)
        FD = F + D
        be, bback6 = (R3[0:E, E * F + n * FD:E * F + (n + 1) * FD] for n in range(2))
        bpart = [R3[:].bitcast(BF16)[0:E, 2 * (E * F + 2 * FD) + n * FD:
                                     2 * (E * F + 2 * FD) + (n + 1) * FD] for n in range(3)]
        bsum = R3[:].bitcast(BF16)[:, 0:2 * E * F].rearrange("p (k e f) -> p k e f", k=2, e=E)
        B1S, B2S = (R3[:].bitcast(BF16)[:, k * E * F:(k + 1) * E * F] for k in range(2))
        lflat = logit[:].rearrange("p e b -> p (e b)")
        o = {n: sem("o_" + n) for n in "bias parts rows sub exp oh count pos sorted".split()}

        with nc.Block() as block:
            @block.sync
            def _(sp):
                sp.dma_start(be[:, 0:F], a["b1"]).then_inc(o["bias"], 16)
                sp.dma_start(be[:, F:F + D], a["b2"]).then_inc(o["bias"], 16)
                sp.wait_ge(o["parts"], 4)
                for n in range(3):
                    sp.dma_start(bsum[n:n + 1, 0, :, :], bpart[n][:, 0:F]).then_inc(o["rows"], 16)
                    sp.dma_start(bsum[n:n + 1, 1, :, 0:D], bpart[n][:, F:F + D]
                                 ).then_inc(o["rows"], 16)
                sp.wait_ge(o["rows"], 96)

            @block.vector
            def _(dve):
                wide = lambda t: t[:, None, :].to_broadcast([P, E, B])
                dlink(dve, dve.tensor_reduce(best, logit[:].rearrange("p e b -> p b e"), AX.X, ALU.max))
                dve.tensor_tensor(logit[:], logit[:], wide(best), ALU.subtract).then_inc(o["sub"], 1)
                dlink(dve, dve.tensor_scalar(W1, W1, bcol[:, 10:11], None, ALU.mult))
                dlink(dve, dve.tensor_copy(trib, cst[:, C_TRI:C_TRI + P]))
                dlink(dve, dve.memset(ones, 1.0))
                dlink(dve, dve.memset(ends[:, 0:1], 0.0))
                dve.wait_ge(o["exp"], 1)
                dlink(dve, dve.tensor_reduce(total5, cube(pe_).rearrange("p e b -> p b e"), AX.X,
                                             ALU.add))
                dlink(dve, dve.reciprocal(rec5, total5))
                dlink(dve, dve.tensor_tensor(cube(pe_), cube(pe_), wide(rec5), ALU.mult))
                dlink(dve, dve.tensor_reduce(best, cube(pe_).rearrange("p e b -> p b e"), AX.X,
                                             ALU.max))
                dlink(dve, dve.tensor_scalar(extra(SCORE), best, 0.5, None, ALU.mult))
                dlink(dve, dve.tensor_tensor(cube(choice), cube(pe_), wide(best), ALU.is_equal))
                dlink(dve, dve.scalar_tensor_tensor(
                    out=cube(choice), in0=cube(choice), scalar=-float(E),
                    in1=cst[:, C_IOTA:C_IOTA + E, None].to_broadcast([P, E, B]),
                    op0=ALU.mult, op1=ALU.add))
                dlink(dve, dve.tensor_reduce(pick, cube(choice).rearrange("p e b -> p b e"), AX.X,
                                             ALU.min))
                dve.tensor_tensor(cube(ohb), cube(choice), wide(pick), ALU.is_equal
                                  ).then_inc(o["oh"], 1)
                dve.wait_ge(o["oh"], 1)
                dve.wait_ge(o["count"], 1)
                dlink(dve, dve.tensor_tensor_scan(count, ones, ps[1], 0.0, ALU.mult, ALU.add))
                dlink(dve, dve.tensor_copy(ends[:, 1:E + 1], cube(count)[:, :, B - 1]))
                dlink(dve, dve.tensor_tensor(tiles, ends[:, 1:E + 1], ends[:, 0:E], ALU.subtract))
                dlink(dve, dve.tensor_tensor(
                    cube(thr), tiles[:, :, None].to_broadcast([P, E, B]),
                    cst[:, None, C_T:C_T + B].to_broadcast([P, E, B]), ALU.is_gt))
                dlink(dve, dve.tensor_reduce(tiles, cube(thr), AX.X, ALU.add))
                dlink(dve, dve.tensor_tensor_scan(incl, ones[:, 0:E], tiles, 0.0, ALU.mult, ALU.add))
                dlink(dve, dve.tensor_tensor(shift, incl, tiles, ALU.subtract))
                dlink(dve, dve.scalar_tensor_tensor(out=shift, in0=shift, scalar=float(P),
                                                    in1=ends[:, 0:E], op0=ALU.mult, op1=ALU.subtract))
                dlink(dve, dve.tensor_tensor(count, count, ps[1], ALU.subtract))
                dlink(dve, dve.tensor_tensor(count, count, ps[0], ALU.add))
                dlink(dve, dve.tensor_tensor(cube(count), cube(count),
                                             shift[:, :, None].to_broadcast([P, E, B]), ALU.add))
                dlink(dve, dve.tensor_tensor(count, count, ohb, ALU.mult))
                dlink(dve, dve.tensor_reduce(pos, cube(count).rearrange("p e b -> p b e"), AX.X,
                                             ALU.add))
                dve.tensor_copy(posi[:], pos).then_inc(o["pos"], 1)
                dlink(dve, dve.tensor_tensor(
                    cmp[0:1].rearrange("p (t e) -> p t e", e=E),
                    cst[0:1, C_TILE:C_TILE + TILES, None].to_broadcast([1, TILES, E]),
                    incl[0:1, None, :].to_broadcast([1, TILES, E]), ALU.is_ge))
                dlink(dve, dve.tensor_reduce(et[0:1], cmp[0:1].rearrange("p (t e) -> p t e", e=E),
                                             AX.X, ALU.add))
                dlink(dve, dve.tensor_scalar(et[0:1], et[0:1], float(E - 1), None, ALU.min))
                dlink(dve, dve.tensor_scalar(wat[:], et[0:1], float(F), None, ALU.mult))
                dve.memset(R3[:, 0:E * F], 0.0).then_inc(o["parts"], 1)
                dve.wait_ge(o["bias"], 32)
                dlink(dve, dve.tensor_scalar(be[:, F:F + D], be[:, F:F + D], 2.0, None, ALU.mult))
                for n in range(3):
                    dve.tensor_copy(bpart[n], be).then_inc(o["parts"], 1)
                    if n < 2:
                        dve.wait_ge(o["parts"], n + 2)
                        dlink(dve, dve.tensor_copy(bback6, bpart[n]))
                        dlink(dve, dve.tensor_tensor(be, be, bback6, ALU.subtract))

            @block.scalar
            def _(act):
                act.activation(warm[:], bcol[:, 0:1], ACT.Exp).then_inc(s_act, 1)
                act.wait_ge(o["sub"], 1)
                act.activation(pe_, lflat, ACT.Exp).then_inc(o["exp"], 1)

            @block.tensor
            def _(pe):
                pe.wait_ge(o["oh"], 1)
                pe.matmul(ps[0], trib, ohb, start=True, stop=True)
                pe.matmul(ps[1], onesb[:], ohb, start=True, stop=True).then_inc(o["count"], 1)

            @block.gpsimd
            def _(pool):
                pool.wait_ge(o["pos"], 1)
                for b in range(B):
                    pool.indirect_dma_start(sorted_rows[:], bass.IndirectOffsetOnAxis(
                        posi[:, b:b + 1], 0), X[:, b, :], None).then_inc(o["sorted"], 16)
                pool.wait_ge(o["sorted"], 16 * B)

        for n in used:
            used[n] = 0
        SLOTS = 8
        srow = [lend(RW) for n in range(SLOTS)]
        srows = work[:, 0:SLOTS * RW].rearrange("p (s w) -> p s w", w=RW)
        xn6 = [lend(D) for n in range(2)]
        xnT6 = [lend(P) for n in range(2)]
        u6 = [lend(F) for n in range(2)]
        th6 = [lend(F) for n in range(2)]
        hT6 = [lend(F) for n in range(2)]
        put = [lend(D) for n in range(4)]
        e = {n: sem("moe_" + n) for n in
             "load xn xt xnT w1 u tr tanh h w2 out put0 put1 taken".split()}

        def pairs(i, ph, n=0):
            return (i - ph % 2) * 8 + 16 * (n + 1)

        def expert(pe, i):
            return pe.value_load(wat[0:1, bass.ds(i, 1)], min_val=0, max_val=(E - 1) * F)

        with nc.Block() as block:
            @block.sync
            def _(sp):
                def body(i, ph, live):
                    if ph % 2 == 0 and live(0):
                        wait(sp, e["put0"], i * 8 - 8 * (SLOTS - 2))
                        wait(sp, e["put1"], i * 8 - 8 * (SLOTS - 2))
                        wait(sp, e["load"], i * 8)
                        sp.dma_start(srows[:, ph:ph + 2, :],
                                     sorted_rows[bass.ds(i * P, 2 * P), :].rearrange(
                                         "(t p) w -> p t w", p=P)).then_inc(e["load"], 16)

                batches(sp, 1, body, TILES + 1, SLOTS)

            @block.vector
            def _(dve):
                def body(i, ph, live):
                    g4, g5, odd = i - 4, i - 5, (ph + 1) % 2
                    if live(4):
                        dve.wait_ge(e["tanh"], g4 + 1)
                        wait(dve, e["w2"], g4 - 1)
                        dve.scalar_tensor_tensor(out=hT6[ph % 2], in0=th6[ph % 2], scalar=1.0,
                                                 in1=ps[2 + ph % 2], op0=ALU.add, op1=ALU.mult
                                                 ).then_inc(e["h"], 1)
                    if live(5):
                        r = srow[(ph + 3) % SLOTS]
                        dve.wait_ge(e["w2"], g5 + 1)
                        wait(dve, e["put%d" % odd], pairs(g5 - 4, odd))
                        dve.scalar_tensor_tensor(out=put[(ph + 3) % 4], in0=ps[6 + odd][:, 0:D],
                                                 scalar=r[:, D + SCORE:D + SCORE + 1],
                                                 in1=r[:, 0:D], op0=ALU.mult, op1=ALU.add
                                                 ).then_inc(e["out"], 1)
                    if live(0):
                        r = srow[ph]
                        dve.wait_ge(e["load"], pairs(i, ph))
                        wait(dve, e["xt"], i - 1)
                        dve.tensor_scalar(xn6[ph % 2], r[:, 0:D], r[:, D + MEAN:D + MEAN + 1],
                                          r[:, D + RSTD:D + RSTD + 1], ALU.subtract, ALU.mult
                                          ).then_inc(e["xn"], 1)

                batches(dve, 6, body, TILES, SLOTS)

            @block.scalar
            def _(act):
                act.activation(warm[:], bcol[:, 0:1], ACT.Tanh).then_inc(s_act, 1)

                def body(i, ph, live):
                    g1, g2, g4, odd = i - 1, i - 2, i - 4, (ph + 1) % 2
                    if live(4):
                        act.wait_ge(e["tr"], g4 + 1)
                        wait(act, e["h"], g4 - 1)
                        act.activation(th6[ph % 2], ps[2 + ph % 2], ACT.Tanh, scale=0.5
                                       ).then_inc(e["tanh"], 1)
                    if live(2):
                        act.wait_ge(e["w1"], g2 + 1)
                        wait(act, e["tr"], g2 - 1)
                        act.copy(u6[ph % 2], ps[ph % 2]).then_inc(e["u"], 1)
                    if live(1):
                        act.wait_ge(e["xt"], g1 + 1)
                        wait(act, e["w1"], g1 - 1)
                        act.copy(xnT6[odd], ps[5][:, 0:P]).then_inc(e["xnT"], 1)

                batches(act, 6, body, TILES, SLOTS)

            @block.tensor
            def _(pe):
                def body(i, ph, live):
                    g1, g2, g3, g5, odd = i - 1, i - 2, i - 3, i - 5, (ph + 1) % 2
                    if live(5):
                        at = expert(pe, g5)
                        pe.wait_ge(e["h"], g5 + 1)
                        wait(pe, e["out"], g5 - 1)
                        y = ps[6 + odd][:, 0:D]
                        pe.matmul(y, onesb[:], B2S[:, bass.ds(at, D)], start=True, stop=False)
                        for c in range(4):
                            mm = pe.matmul(y, hT6[odd][:, c * P:(c + 1) * P],
                                           W2[:, bass.ds(at + c * D, D)], start=False,
                                           stop=(c == 3))
                        mm.then_inc(e["w2"], 1)
                    if live(2):
                        at = expert(pe, g2)
                        pe.wait_ge(e["xnT"], g2 + 1)
                        wait(pe, e["u"], g2 - 1)
                        pe.matmul(ps[ph % 2], onesb[:], B1S[:, bass.ds(at, F)], start=True,
                                  stop=False)
                        pe.matmul(ps[ph % 2], xnT6[ph % 2], W1[:, bass.ds(at, F)], start=False,
                                  stop=True).then_inc(e["w1"], 1)
                    if live(3):
                        pe.wait_ge(e["u"], g3 + 1)
                        wait(pe, e["h"], g3 - 1)
                        for c in range(4):
                            mm = pe.transpose(ps[2 + odd][:, c * P:(c + 1) * P],
                                              u6[odd][:, c * P:(c + 1) * P], ident)
                        mm.then_inc(e["tr"], 1)
                    if live(1):
                        pe.wait_ge(e["xn"], g1 + 1)
                        wait(pe, e["xnT"], g1)
                        pe.transpose(ps[5][:, 0:P], xn6[odd], ident).then_inc(e["xt"], 1)

                batches(pe, 6, body, TILES, SLOTS)

            @block.gpsimd
            def _(pool):
                def body(i, ph, live):
                    if live(5):
                        g5, odd = i - 5, (ph + 1) % 2
                        done = e["put%d" % odd]
                        pool.wait_ge(e["out"], g5 + 1)
                        wait(pool, done, pairs(g5 - 2, odd))
                        pool.sem_inc(e["taken"], 1)
                        r = srow[(ph + 3) % SLOTS].bitcast(I32)
                        pool.indirect_dma_start(
                            out[:], bass.IndirectOffsetOnAxis(r[:, D + TOKEN:D + TOKEN + 1], 0),
                            put[(ph + 3) % 4], None,
                            bounds_check=NT - 1, oob_is_err=False).then_inc(done, 16)

                batches(pool, 6, body, TILES, SLOTS)
                pool.wait_ge(e["put0"], 16 * (-(-TILES // 2)))
                pool.wait_ge(e["put1"], 16 * (TILES // 2))


def _laid_out(i):
    c = np.ascontiguousarray
    t = lambda w: c(np.asarray(w).T)
    g = {k: np.asarray(v) for k, v in i.items()}
    zero = np.zeros(P, np.float32)
    a = {
        "x": c(g["x"].reshape(NT, D)),
        "ctxT": t(g["ctx_768"].reshape(NC, CD)),
        "mask": c(g["mask_BxS2_bf1"].reshape(1, NC)).view(np.uint8),
        "cst": constants(),
        "wq": c(g["L0_xattn_Wq"]), "wk": c(g["L0_xattn_Wk"]),
        "wv": c(g["L0_xattn_Wv"]), "wo": c(g["L0_xattn_Wo"]),
        "wof": t(g["L0_ffn_wo"]), "uo": t(g["L0_ffn_uo"]),
        "bgate": c(np.stack([g["L0_ffn_bf"], g["L0_ffn_bi"], g["L0_ffn_bc"]])[None]),
    }
    for n in "fic":
        a["w" + n] = t(g["L0_ffn_w" + n])
        a["u" + n] = t(g["L0_ffn_u" + n])
    for n in WEIGHTS:
        a["w_" + n] = t(g["L1_xattn_W_" + n])
    a["w1"], a["w2"], a["gw"] = c(g["L1_ffn_W1"]), c(g["L1_ffn_W2"]), t(g["L1_ffn_gate_w"])
    a["b1"], a["b2"] = (c(g["L1_ffn_b" + n]) for n in "12")
    ba = [np.concatenate([g["L1_xattn_b_att" + n]] * 2) for n in "01"]
    cols = [g["L1_xattn_b_d2v"], g["L1_xattn_b_img"], g["L1_xattn_b_txt"], *ba,
            *g["L1_xattn_b_f1"].reshape(4, P), g["L0_ffn_in_c"], g["L1_ffn_rms_w"]]
    a["bcol"] = c(np.stack(cols + [zero] * (16 - len(cols)), 1))
    a["brow"] = c(np.stack([g["L0_ffn_bo"], g["L1_xattn_b_f2"], g["L1_ffn_rms_w"], *ba, zero])[None])
    return a


def kernel(**inputs):
    import concourse.bacc as bacc
    from concourse.bass_utils import run_bass_kernel_spmd as run

    arrays = _laid_out(inputs)
    nc = bacc.Bacc("TRN2", target_bir_lowering=False, num_devices=1)
    a = {n: nc.dram_tensor("in_" + n, v.shape, mybir.dt.from_np(v.dtype), kind="ExternalInput").ap()
         for n, v in arrays.items()}
    out = nc.dram_tensor("out", (NT, D), F32, kind="ExternalOutput").ap()
    xattn_ffn_kernel(nc, a, out)
    r = run(nc, [{"in_" + n: v for n, v in arrays.items()}], core_ids=[0])
    return r.results[0]["out"].reshape(B, S, D)
```

```python
from contextlib import ExitStack

import numpy as np

import concourse.bass as bass
from concourse import mybir

P = 128
B, S, D = 64, 128, 128
M, CD = 77, 96
H, HD = 16, 8
Q = 4
F = 512
E = 8
NT = B * S
NC = B * M
PW = H * M + (P - M) + 1
G4 = 4
NG = B // G4
TILES = B + E - 1
CAP = NT + P
RW = D + 4
MEAN, SCORE, TOKEN, RSTD = range(4)
MAGIC = 12582912.0
BIG = 3.3895313892515355e38

ALU = mybir.AluOpType
ACT = mybir.ActivationFunctionType
BF16 = mybir.dt.bfloat16
F32 = mybir.dt.float32
I32 = mybir.dt.int32
U8 = mybir.dt.uint8
AX = mybir.AxisListType
RMAX = bass.bass_isa.ReduceOp.max
RADD = bass.bass_isa.ReduceOp.add

WEIGHTS = ("d2v", "img", "txt", "att0", "att1", "f1", "f2")


def batches(eng, depth, body, count=B, unroll=2):
    lo = -(-depth // unroll) * unroll
    turns = (count - lo) // unroll
    for i in range(lo):
        body(i, i % unroll, lambda n, i=i: 0 <= i - n < count)
    with eng.Fori(0, turns) as turn:
        for u in range(unroll):
            body(turn * unroll + (lo + u), u, lambda n: True)
    for i in range(lo + turns * unroll, count + depth - 1):
        body(i, i % unroll, lambda n, i=i: 0 <= i - n < count)


def wait(eng, sem, value):
    if isinstance(value, int) and value <= 0:
        return
    eng.wait_ge(sem, value)


C_ID, C_KM, C_VM, C_TRI, C_IOTA, C_INV, C_T = 0, 128, 144, 656, 784, 792, 800
C_TILE = C_T + 64
C_W = C_TILE + TILES


def constants():
    c = np.zeros((P, C_W), np.float32)
    p = np.arange(P)
    c[:, C_ID:C_ID + P] = np.eye(P)
    for q in range(Q):
        for g in range(Q):
            c[:, C_KM + 4 * q + g] = p // HD == 4 * g + q
        c[:, C_VM + q * D:C_VM + (q + 1) * D] = (np.arange(D) % 32) // HD == q
    c[:, C_TRI:C_TRI + P] = p[:, None] < p[None, :]
    c[:, C_IOTA:C_IOTA + E] = np.arange(E)
    for n, count in enumerate((CD * D, D * D, D * D, D * 64, D * 64, 2 * D * F, F * D)):
        c[:, C_INV + n] = 1.0 / count
    c[:, C_T:C_T + 64] = np.arange(64) * P
    c[:, C_TILE:C_TILE + TILES] = np.arange(TILES)
    return c


class Chain:

    def __init__(self, sem):
        self.sem, self.n = sem, 0

    def __call__(self, eng, ins):
        self.n += 1
        ins.then_inc(self.sem, 1)
        eng.wait_ge(self.sem, self.n)


def xattn_ffn_kernel(nc, a, out):
    with ExitStack() as ctx:
        def sb(name, shape, dt=F32):
            return ctx.enter_context(nc.sbuf_tensor(name, shape, dt))

        def sem(name):
            return ctx.enter_context(nc.semaphore(name))

        psum = ctx.enter_context(nc.psum_tensor("psum", [P, 8, 512], F32))
        ps = [psum[:, n, :] for n in range(8)]

        X = sb("X", [P, B, RW])
        R2 = sb("R2", [P, B * D])
        R3 = sb("R3", [P, B * D])
        cst = sb("cst", [P, C_W])
        ident = cst[:, C_ID:C_ID + P]
        kT = sb("kT", [P, NC])
        qimg = sb("qimg", [P, NC], BF16)
        maskneg = sb("maskneg", [P, NC], BF16)
        work = sb("work", [P, 2 * PW + 2 * H * M])
        prob = [work[:, n * PW:(n + 1) * PW] for n in range(2)]
        kblk = [work[:, 2 * PW + n * H * M:2 * PW + (n + 1) * H * M] for n in range(2)]
        vm = [sb(f"vm{n}", [P, Q, D]) for n in range(2)]
        pts = [sb(f"pts{n}", [P, 512]) for n in range(2)]
        small = sb("small", [P, 12, P])
        raw = sb("raw", [P, 2048])
        tern = sb("tern", [P, 2176], BF16)
        sc = sb("sc", [P, 64])
        bcol = sb("bcol", [P, 16])
        brep = sb("brep", [P, 2, P])
        onesb = sb("onesb", [P, P], BF16)
        brow = sb("brow", [1, 3, P])
        bback = sb("bback", [1, 3, P])
        bsplit = sb("bsplit", [P, 3, P], BF16)
        identb = sb("identb", [P, P], BF16)
        warm = sb("warm", [P, 1])
        avgT = sb("avgT", [P, B])

        WQ, WK, WV, WO, WF, WI, WC, UF, UI, UC, WOF, UO = (small[:, n, :] for n in range(12))
        rawd = {"d2v": raw[0:CD, 0:128], "img": raw[:, 128:256], "txt": raw[:, 256:384],
                "att0": raw[:, 384:448], "att1": raw[:, 448:512],
                "f1": raw[:, 512:1536], "f2": raw[:, 1536:2048]}
        ternd = {"d2v": tern[0:CD, 0:128], "img": tern[:, 128:256], "txt": tern[:, 256:384],
                 "att0": tern[:, 384:512], "att1": tern[:, 512:640],
                 "f1": tern[:, 640:1664], "f2": tern[:, 1664:2176]}
        ctxT = R3[0:CD, 0:NC]
        V = R2[0:M, :]

        WSUM, WS, THR, NTHR = 0, 8, 16, 24
        AMAX, AALL, IS, INV, K_TMP, EPS5, MAG, NHALF, K_TXT, K_A0, K_A1, K_F1, K_H, K_F2 = \
            range(32, 46)
        K_A = (K_A0, K_A1)
        B_F1 = 48
        IMAX = 52

        def col(n, rows=P):
            return sc[0:rows, n:n + 1]

        s_load, s_ctx, s_x = sem("s_load"), sem("s_ctx"), sem("s_x")
        s_dve, s_act = sem("s_dve"), sem("s_act")
        s_tick = sem("s_tick")
        dlink = Chain(s_dve)
        s_allin, s_allout = sem("s_allin"), sem("s_allout")

        def quantum(dve, n):
            dve.wait_ge(s_allout, n)
            dlink(dve, dve.tensor_scalar(col(IS), col(AALL), 1e-8, 1.0 / 127.0, ALU.max, ALU.mult))
            dlink(dve, dve.reciprocal(col(INV), col(IS)))

        CH = 352
        NCH = NC // CH
        STREAMS = ("kT", "vis", "img")
        s_mask = sem("s_mask")
        s_bank = sem("s_bank")
        s_prod = sem("s_prod")
        s_quant = sem("s_quant")
        s_tern = sem("s_tern")
        s_kvis = sem("s_kvis")
        s_vprod, s_vbank = sem("s_vprod"), sem("s_vbank")
        s_wred, s_wsum = sem("s_wred"), sem("s_wsum")
        maskb = R3[:].bitcast(U8)[0:1, 4 * NC:5 * NC]
        img = R3[:, B * D - NC:B * D]
        NLOAD = 1 + 10 + 3

        with nc.Block() as block:
            @block.sync
            def _(sp):
                sp.dma_start(ctxT, a["ctxT"]).then_inc(s_ctx, 16)
                sp.dma_start(cst[:], a["cst"]).then_inc(s_load, 16)
                sp.dma_start(maskb, a["mask"]).then_inc(s_mask, 16)
                for name in WEIGHTS:
                    dst, src = rawd[name], a["w_" + name]
                    if name in ("f1", "f2"):
                        k = src.shape[0] // P
                        dst = dst.rearrange("p (k n) -> p k n", k=k)
                        src = src.rearrange("(k p) n -> p k n", p=P)
                    sp.dma_start(dst, src).then_inc(s_tern, 16)
                for b in range(0, B, 16):
                    sp.dma_start(X[:, b:b + 16, 0:D], a["x"][b * S:(b + 16) * S, :]
                                 .rearrange("(b s) d -> s b d", s=S)).then_inc(s_x, 16)
                sp.wait_ge(s_x, 16 * 4)

            @block.scalar
            def _(act):
                for n, name in ((1, "wk"), (2, "wv")):
                    act.dma_start(small[0:CD, n, :], a[name]).then_inc(s_ctx, 16)
                for n, name in enumerate(("wq", "wk", "wv", "wo", "wf", "wi", "wc", "uf", "ui", "uc",
                                          "wof", "uo")):
                    if name not in ("wk", "wv"):
                        act.dma_start(small[:, n, :], a[name]).then_inc(s_load, 16)
                act.dma_start(bcol[:], a["bcol"]).then_inc(s_load, 16)
                act.dma_start(brow[:], a["bgate"]).then_inc(s_load, 16)
                act.dma_start(brep[:], a["brow"].to_broadcast([P, 2, P])).then_inc(s_load, 16)
                act.wait_ge(s_bank, 2)
                act.activation(warm[:], col(EPS5), ACT.Exp).then_inc(s_act, 1)
                for n, name in enumerate(STREAMS):
                    if n:
                        act.wait_ge(s_load, 16 * NLOAD)
                        act.wait_ge(s_kvis, n)
                    dst = {"kT": kT, "vis": work, "img": img}[name]
                    with act.Fori(0, NCH // 2) as turn:
                        for u in range(2):
                            act.wait_ge(s_prod, turn * 2 + (n * NCH + u + 1))
                            act.activation(
                                dst[:, bass.ds((turn * 2 + u) * CH, CH)], ps[u][:, 0:CH],
                                ACT.Identity, bias=bcol[:, n - 1:n] if n else 0.0,
                                scale=col(K_TMP) if n else 1.0).then_inc(s_bank, 1)
                    if n < 2:
                        for g in range(n * NG // 2, (n + 1) * NG // 2):
                            act.wait_ge(s_vprod, g + 1)
                            act.copy(V[:, g * G4 * D:(g + 1) * G4 * D], ps[2 + g % 2][0:M, :]
                                     ).then_inc(s_vbank, 1)

            @block.gpsimd
            def _(pool):
                pool.wait_ge(s_allin, 1)
                pool.partition_all_reduce(col(AALL), col(AMAX), P, RMAX).then_inc(s_allout, 1)
                pool.wait_ge(s_wred, 1)
                pool.partition_all_reduce(sc[:, WS:WS + 8], sc[:, WSUM:WSUM + 8], P, RADD
                                          ).then_inc(s_wsum, 1)
                pool.wait_ge(s_allin, 2)
                pool.partition_all_reduce(col(AALL), col(AMAX), P, RMAX).then_inc(s_allout, 1)

            @block.tensor
            def _(pe):
                pe.wait_ge(s_ctx, 48)
                pe.wait_ge(s_bank, 2)
                for n, (name, w) in enumerate((("kT", WK[0:CD]), ("vis", ternd["d2v"]),
                                               ("img", ternd["img"]))):
                    if n:
                        pe.wait_ge(s_quant, n)
                    src = ctxT if n == 0 else qimg[0:CD, :] if n == 1 else qimg
                    with pe.Fori(0, NCH // 2) as turn:
                        for u in range(2):
                            pe.wait_ge(s_bank, turn * 2 + (n * NCH + u + 1))
                            pe.matmul(ps[u][:, 0:CH], w, src[:, bass.ds((turn * 2 + u) * CH, CH)],
                                      start=True, stop=True).then_inc(s_prod, 1)
                    if n < 2:
                        for b in range(n * B // 2, (n + 1) * B // 2):
                            g, j = divmod(b, G4)
                            if j == 0:
                                wait(pe, s_vbank, g - 1)
                            mm = pe.matmul(ps[2 + g % 2][0:M, j * D:(j + 1) * D],
                                           ctxT[:, b * M:(b + 1) * M], WV[0:CD], start=True, stop=True)
                            if j == G4 - 1:
                                mm.then_inc(s_vprod, 1)

            @block.vector
            def _(dve):
                dlink(dve, dve.memset(sc[:], 0.0))
                for t in (onesb, bsplit, maskneg, vm[0], vm[1]):
                    dve.memset(t[:], float(t is onesb)).then_inc(s_dve, 1)
                    dlink.n += 1
                dve.memset(col(EPS5), 1e-5).then_inc(s_bank, 1)
                dve.memset(col(MAG), MAGIC).then_inc(s_bank, 1)
                dve.wait_ge(s_ctx, 48)
                dve.tensor_reduce(col(AMAX, CD), ctxT, AX.X, ALU.max,
                                  apply_absolute_value=True).then_inc(s_allin, 1)
                dlink(dve, dve.memset(col(NHALF), -0.5))
                dve.wait_ge(s_mask, 16)
                dve.tensor_scalar(maskneg[0:1, :], maskb, -1.0, BIG, ALU.add, ALU.mult
                                  ).then_inc(s_mask, 1)
                quantum(dve, 1)
                dlink(dve, dve.tensor_scalar(work[0:CD, 0:NC], ctxT, col(INV, CD), MAGIC,
                                             ALU.mult, ALU.add))
                dlink(dve, dve.tensor_scalar(qimg[0:CD, :], work[0:CD, 0:NC], MAGIC, None,
                                             ALU.subtract))
                dve.wait_ge(s_mask, 17)
                dve.wait_ge(s_tern, 16 * len(WEIGHTS))
                for n, name in enumerate(WEIGHTS):
                    w = rawd[name]
                    dlink(dve, dve.tensor_reduce(sc[0:w.shape[0], WSUM + n:WSUM + n + 1], w, AX.X,
                                                 ALU.add, apply_absolute_value=True))
                dve.wait_ge(s_load, 16 * NLOAD)
                dve.tensor_copy(identb[:], ident).then_inc(s_wred, 1)
                dve.wait_ge(s_wsum, 1)
                dlink(dve, dve.tensor_tensor(sc[:, WS:WS + 7], sc[:, WS:WS + 7],
                                             cst[:, C_INV:C_INV + 7], ALU.mult))
                dlink(dve, dve.tensor_scalar(sc[:, WS:WS + 7], sc[:, WS:WS + 7], 1e-5, None, ALU.max))
                dve.tensor_tensor(col(K_TMP), col(IS), col(WS + 0), ALU.mult).then_inc(s_kvis, 1)
                dlink(dve, dve.tensor_scalar(sc[:, THR:THR + 7], sc[:, WS:WS + 7], 0.5, None, ALU.mult))
                dlink(dve, dve.tensor_scalar(sc[:, NTHR:NTHR + 7], sc[:, WS:WS + 7], -0.5, None,
                                             ALU.mult))
                for n, name in enumerate(WEIGHTS):
                    w, t = rawd[name], ternd[name]
                    r, c = w.shape
                    below = R3[0:r, NC:NC + c]
                    dlink(dve, dve.tensor_scalar(below, w, col(NTHR + n, r), None, ALU.is_lt))
                    for twice in range(t.shape[1] // c):
                        dlink(dve, dve.scalar_tensor_tensor(
                            out=t[:, twice * c:(twice + 1) * c], in0=w, scalar=col(THR + n, r),
                            in1=below, op0=ALU.is_gt, op1=ALU.subtract))
                    if n == 0:
                        dve.sem_inc(s_quant, 1)
                dlink(dve, dve.tensor_scalar(small[:, 4:6, :], small[:, 4:6, :], 0.5, None, ALU.mult))
                dlink(dve, dve.tensor_scalar(small[:, 7:9, :], small[:, 7:9, :], 0.25, None, ALU.mult))
                dlink(dve, dve.tensor_scalar(small[:, 9:10, :], small[:, 9:10, :], 0.5, None, ALU.mult))
                dlink(dve, dve.tensor_scalar(small[:, 11:12, :], small[:, 11:12, :], 0.5, None,
                                             ALU.mult))
                dlink(dve, dve.tensor_scalar(brow[0:1, 0:2, :], brow[0:1, 0:2, :], 0.5, None,
                                             ALU.mult))
                for part in range(3):
                    rows = bsplit[32 * part:32 * part + 1, :, :]
                    dlink(dve, dve.tensor_copy(rows, brow[0:1, :, :]))
                    if part < 2:
                        dlink(dve, dve.tensor_copy(bback[0:1], rows))
                        dlink(dve, dve.tensor_tensor(brow[0:1, :, :], brow[0:1, :, :], bback[0:1],
                                                     ALU.subtract))
                dve.wait_ge(s_bank, 2 + 2 * NCH)
                dve.tensor_reduce(col(AMAX), work[:, 0:NC], AX.X, ALU.max,
                                  apply_absolute_value=True).then_inc(s_allin, 1)
                quantum(dve, 2)
                dve.tensor_tensor(col(K_TMP), col(IS), col(WS + 1), ALU.mult).then_inc(s_kvis, 1)
                dlink(dve, dve.tensor_scalar(work[:, 0:NC], work[:, 0:NC], col(INV), MAGIC,
                                             ALU.mult, ALU.add))
                dve.tensor_scalar(qimg[:], work[:, 0:NC], MAGIC, None, ALU.subtract
                                  ).then_inc(s_quant, 1)

        def image_part(dve, i):
            def columns(n, parts=4):
                return slice(n * NC // parts, (n + 1) * NC // parts)

            if i in (0, 1):
                for n in (2 * i, 2 * i + 1):
                    dlink(dve, dve.tensor_reduce(col(IMAX + n), img[:, columns(n)], AX.X, ALU.max,
                                                 apply_absolute_value=True))
            if i == 1:
                dve.tensor_reduce(col(AMAX), sc[:, IMAX:IMAX + 4], AX.X, ALU.max).then_inc(s_allin, 1)
            if i in (2, 3):
                half = slice((i - 2) * B // 2, (i - 1) * B // 2)
                dlink(dve, dve.tensor_reduce(
                    avgT[:, half], img[:, columns(i - 2, 2)].rearrange("p (b m) -> p b m", m=M),
                    AX.X, ALU.add))
            if i == 4:
                dlink(dve, dve.tensor_scalar(avgT[:], avgT[:], 1.0 / M, None, ALU.mult))
                quantum(dve, 3)
            if i in (4, 5):
                dlink(dve, dve.tensor_scalar(img[:, columns(i - 4, 2)], img[:, columns(i - 4, 2)],
                                             col(INV), MAGIC, ALU.mult, ALU.add))
            if i in (6, 7):
                dlink(dve, dve.tensor_scalar(qimg[:, columns(i - 6, 2)], img[:, columns(i - 6, 2)],
                                             MAGIC, None, ALU.subtract))
            if i == 7:
                dlink(dve, dve.tensor_tensor(col(K_A0), col(IS), col(WS + 3), ALU.mult))
                dve.tensor_tensor(col(K_A1), col(IS), col(WS + 4), ALU.mult).then_inc(s_quant, 1)

        HX = R3
        xn = [sb(f"xn{n}", [P, D]) for n in range(2)]
        qT = [sb(f"qT{n}", [P, S]) for n in range(2)]
        xnT, x1n, x1nT = sb("xnT", [P, S]), sb("x1n", [P, D]), sb("x1nT", [P, S])
        attT, rrep = sb("attT", [P, S]), sb("rrep", [P, S])
        gate = sb("gate", [P, 3, S])
        state, keep, fresh = sb("state", [P, S]), sb("keep", [P, S]), sb("fresh", [P, S])
        peak = sb("peak", [P, Q, Q])
        total, rtot = sb("total", [P, H]), sb("rtot", [P, H])
        rwide = sb("rwide", [P, H, HD])
        stat1, stat2 = sb("stat1", [P, 6]), sb("stat2", [P, 6])
        mom1 = [sb(f"mom1_{n}", [P, 2]) for n in range(2)]
        mom2 = [sb(f"mom2_{n}", [P, 2]) for n in range(2)]
        rs1 = [sb(f"rs1_{n}", [P, 1]) for n in range(2)]
        rs2 = [sb(f"rs2_{n}", [P, 1]) for n in range(2)]
        ve1, ve2 = sb("ve1", [P, 1]), sb("ve2", [P, 1])
        QW = Q * M
        QSCALE = float(HD) ** -0.5
        bank_s, bank_t = ps[0:2], ps[2:4]
        bank_x, bank_o, bank_w, bank_g = ps[4], ps[6], ps[5], ps[7]

        names = ("stat1 mom1 ve1 rs1 xn xnp xnT qp q kb vm score peak sub exp pt pte pv total rtot rp "
                 "rwide rrep att wo x1 stat2 mom2 ve2 rs2 x1n x1p x1nT gates tanh hx mix state")
        e = {n: sem("e_" + n) for n in names.split()}

        def cols(b):
            return bass.ds(b * D, D)

        Xf = X[:].rearrange("p b w -> p (b w)")

        def row(b):
            return Xf[:, bass.ds(b * RW, D)]

        def rows4(g):
            return Xf[:, bass.ds(g * (G4 * RW), G4 * RW)].rearrange("p (j w) -> p j w", j=G4)[:, :, 0:D]

        with nc.Block() as block:
            @block.vector
            def _(dve):
                dlink(dve, dve.memset(prob[0][:, H * M:PW], 0.0))
                dlink(dve, dve.memset(prob[1][:, H * M:PW], 0.0))
                dve.memset(state[:], 0.0).then_inc(e["mix"], 2)
                dve.wait_ge(e["mix"], 2)
                dve.tensor_scalar(state[:], state[:], 1.0, bcol[:, 9:10], ALU.mult, ALU.add
                                  ).then_inc(e["mix"], 1)
                dve.wait_ge(e["mix"], 3)
                dve.tensor_scalar(state[:], state[:], 2.0, None, ALU.mult).then_inc(e["state"], 1)
                MIX0 = 3

                def body(i, par, live):
                    b0, b1, b2, b3, b4, b5, b6 = (i - n for n in range(7))
                    odd = 1 - par

                    def peaks(q):
                        dve.wait_ge(e["score"], b2 * 4 + (q + 1))
                        wait(dve, e["sub"], b2 * 4 + (q - 3))
                        s4 = bank_s[q % 2][:, 0:QW].rearrange("p (g m) -> p g m", g=Q)
                        dve.tensor_reduce(peak[:, q, :], s4, AX.X, ALU.max).then_inc(e["peak"], 1)

                    def less(q):
                        dve.wait_ge(e["peak"], b2 * 4 + (q + 1))
                        if q == 0:
                            wait(dve, e["pt"], b2 * 4 - 4)
                        s4 = bank_s[q % 2][:, 0:QW].rearrange("p (g m) -> p g m", g=Q)
                        dve.tensor_tensor(
                            prob[par][:, q * QW:(q + 1) * QW].rearrange("p (g m) -> p g m", g=Q),
                            s4, peak[:, q, :, None].to_broadcast([P, Q, M]), ALU.subtract
                            ).then_inc(e["sub"], 1)

                    if live(2):
                        peaks(0)
                    if live(1):
                        dve.wait_ge(e["rs1"], b1 + 1)
                        wait(dve, e["xnp"], b1 - 1)
                        dve.tensor_scalar(xn[odd][:], row(b1), mom1[odd][:, 0:1], rs1[odd][:],
                                          ALU.subtract, ALU.mult).then_inc(e["xn"], 1)
                    if live(2):
                        less(0)
                        peaks(1)
                    if live(5):
                        dve.wait_ge(e["rs2"], b5 + 1)
                        wait(dve, e["x1p"], b5)
                        dve.tensor_scalar(x1n[:], row(b5), mom2[odd][:, 0:1], rs2[odd][:],
                                          ALU.subtract, ALU.mult).then_inc(e["x1n"], 1)
                    if live(2):
                        less(1)
                    if live(4):
                        dve.wait_ge(e["pv"], b4 * 4 + 4)
                        dve.wait_ge(e["rrep"], b4 + 1)
                        wait(dve, e["wo"], b4)
                        dve.tensor_tensor(attT[:], bank_o[:, 0:S], rrep[:], ALU.mult
                                          ).then_inc(e["att"], 1)
                    if live(3):
                        dve.wait_ge(e["exp"], b3 * 2 + 2)
                        wait(dve, e["rtot"], b3)
                        dve.tensor_reduce(
                            total[:].rearrange("p (g q) -> p q g", q=Q),
                            prob[odd][:, 0:H * M].rearrange("p (q g m) -> p q g m", q=Q, g=Q),
                            AX.X, ALU.add).then_inc(e["total"], 1)
                    if live(3):
                        dve.wait_ge(e["total"], b3 + 1)
                        wait(dve, e["rwide"], b3)
                        dve.reciprocal(rtot[:], total[:]).then_inc(e["rtot"], 1)
                    if live(6):
                        dve.wait_ge(e["tanh"], b6 + 1)
                        dve.wait_ge(e["state"], b6 + 1)
                        dve.scalar_tensor_tensor(out=keep[:], in0=gate[:, 0, :], scalar=1.0,
                                                 in1=state[:], op0=ALU.add, op1=ALU.mult
                                                 ).then_inc(e["mix"], 1)
                        dve.scalar_tensor_tensor(out=fresh[:], in0=gate[:, 1, :], scalar=1.0,
                                                 in1=gate[:, 2, :], op0=ALU.add, op1=ALU.mult
                                                 ).then_inc(e["mix"], 1)
                    if live(4):
                        dve.wait_ge(e["wo"], b4 + 1)
                        dve.tensor_tensor(row(b4), row(b4), bank_w[:, 128:256], ALU.add
                                          ).then_inc(e["x1"], 1)
                    if live(6):
                        dve.wait_ge(e["mix"], b6 * 2 + (2 + MIX0))
                        dve.scalar_tensor_tensor(out=state[:], in0=keep[:], scalar=0.5,
                                                 in1=fresh[:], op0=ALU.mult, op1=ALU.add
                                                 ).then_inc(e["state"], 1)
                    if live(2):
                        peaks(2)
                    if live(4):
                        dve.wait_ge(e["x1"], b4 + 1)
                        wait(dve, e["mom2"], b4)
                        dve.sem_inc(s_tick, 1)
                        dve.bn_stats(stat2[:], row(b4)).then_inc(e["stat2"], 1)
                    if live(2):
                        less(2)
                        peaks(3)
                    if live(4):
                        dve.wait_ge(e["stat2"], b4 + 1)
                        wait(dve, e["x1n"], b4 - 1)
                        dve.sem_inc(s_tick, 1)
                        dve.bn_aggr(mom2[par][:], stat2[:]).then_inc(e["mom2"], 1)
                    if live(2):
                        less(3)
                    if live(0):
                        wait(dve, e["mom1"], b0)
                        dve.sem_inc(s_tick, 1)
                        dve.bn_stats(stat1[:], row(b0)).then_inc(e["stat1"], 1)
                    if live(0):
                        dve.wait_ge(e["stat1"], b0 + 1)
                        wait(dve, e["xn"], b0 - 1)
                        dve.sem_inc(s_tick, 1)
                        dve.bn_aggr(mom1[par][:], stat1[:]).then_inc(e["mom1"], 1)
                    if isinstance(i, int) and i < 8:
                        image_part(dve, i)

                batches(dve, 7, body)

            @block.scalar
            def _(act):
                act.activation(warm[:], bcol[:, 0:1], ACT.Exp).then_inc(s_act, 1)

                def body(i, par, live):
                    b1, b2, b3, b4, b5, b6 = (i - n for n in range(1, 7))
                    odd = 1 - par

                    def turned(q):
                        act.wait_ge(e["pt"], b3 * 4 + (q + 1))
                        wait(act, e["pv"], b3 * 4 + (q - 1))
                        act.copy(pts[q % 2][:], bank_t[q % 2][:]).then_inc(e["pte"], 1)

                    def exponentials(half):
                        act.wait_ge(e["sub"], b2 * 4 + (2 * half + 2))
                        part = prob[par][:, 2 * half * QW:(2 * half + 2) * QW]
                        act.activation(part, part, ACT.Exp).then_inc(e["exp"], 1)

                    if live(4):
                        act.wait_ge(e["rp"], b4 + 1)
                        wait(act, e["att"], b4)
                        act.copy(rrep[:], bank_w[:, 0:128]).then_inc(e["rrep"], 1)
                    if live(3):
                        turned(0)
                        turned(1)
                    if live(6):
                        act.wait_ge(e["gates"], b6 + 1)
                        wait(act, e["mix"], b6 * 2 + 3)
                        act.activation(gate[:], bank_g[:, 0:384].rearrange("p (g s) -> p g s", g=3),
                                       ACT.Tanh).then_inc(e["tanh"], 1)
                        act.copy(HX[:, cols(b6)], bank_g[:, 384:512]).then_inc(e["hx"], 1)
                    if live(1):
                        act.wait_ge(e["xnp"], b1 + 1)
                        wait(act, e["qp"], b1)
                        act.copy(xnT[:], bank_x[:, 0:128]).then_inc(e["xnT"], 1)
                    if live(2):
                        exponentials(0)
                    if live(3):
                        turned(2)
                    if live(5):
                        act.wait_ge(e["x1p"], b5 + 1)
                        wait(act, e["gates"], b5)
                        act.copy(x1nT[:], bank_x[:, 256:384]).then_inc(e["x1nT"], 1)
                    if live(3):
                        turned(3)
                    if live(1):
                        act.wait_ge(e["qp"], b1 + 1)
                        wait(act, e["score"], b1 * 4 - 4)
                        act.activation(qT[odd][:], bank_x[:, 128:256], ACT.Copy, scale=QSCALE
                                       ).then_inc(e["q"], 1)
                    if live(2):
                        exponentials(1)
                    if live(3):
                        act.wait_ge(e["rtot"], b3 + 1)
                        wait(act, e["rp"], b3)
                        act.copy(rwide[:], rtot[:, :, None].to_broadcast([P, H, HD])
                                 ).then_inc(e["rwide"], 1)

                    if isinstance(i, int) and i == 7:
                        act.wait_ge(s_quant, 3)

                batches(act, 7, body)

            @block.gpsimd
            def _(pool):
                def body(i, par, live):
                    b0, b1, b2, b3, b4 = (i - n for n in range(5))
                    odd = 1 - par
                    if isinstance(i, int) and i == 3:
                        pool.wait_ge(s_allin, 3)
                        pool.partition_all_reduce(col(AALL), col(AMAX), P, RMAX
                                                  ).then_inc(s_allout, 1)
                    if live(1):
                        wait(pool, e["score"], b1 * 4 - 4)
                        pool.tensor_tensor(
                            kblk[odd].rearrange("p (h m) -> p h m", m=M),
                            kT[:, None, bass.ds(b1 * M, M)].to_broadcast([P, H, M]),
                            cst[:, C_KM:C_KM + H, None].to_broadcast([P, H, M]), ALU.mult
                            ).then_inc(e["kb"], 1)
                    if live(2):
                        wait(pool, e["pv"], b2 * 4 - 4)
                        pool.tensor_tensor(
                            vm[par][0:M], V[:, None, cols(b2)].to_broadcast([M, Q, D]),
                            cst[0:M, C_VM:C_VM + Q * D].rearrange("p (q d) -> p q d", q=Q), ALU.mult
                            ).then_inc(e["vm"], 1)
                    if live(4):
                        pool.wait_ge(e["mom2"], b4 + 1)
                        wait(pool, e["rs2"], b4)
                        pool.tensor_tensor(ve2[:], mom2[par][:, 1:2], col(EPS5), ALU.add
                                           ).then_inc(e["ve2"], 1)
                        pool.wait_ge(e["ve2"], b4 + 1)
                        wait(pool, e["x1n"], b4 - 1)
                        pool.tensor_tensor(rs2[par][:], ve2[:], col(NHALF), ALU.pow
                                           ).then_inc(e["rs2"], 1)
                    if live(0):
                        pool.wait_ge(e["mom1"], b0 + 1)
                        wait(pool, e["rs1"], b0)
                        pool.tensor_tensor(ve1[:], mom1[par][:, 1:2], col(EPS5), ALU.add
                                           ).then_inc(e["ve1"], 1)
                        pool.wait_ge(e["ve1"], b0 + 1)
                        wait(pool, e["xn"], b0 - 1)
                        pool.tensor_tensor(rs1[par][:], ve1[:], col(NHALF), ALU.pow
                                           ).then_inc(e["rs1"], 1)

                batches(pool, 7, body)

            @block.tensor
            def _(pe):
                def body(i, par, live):
                    b1, b2, b3, b4, b5, b6 = (i - n for n in range(1, 7))
                    odd = 1 - par

                    def scores(q):
                        bank = bank_s[q % 2][:, 0:QW]
                        wait(pe, e["sub"], b2 * 4 + (q - 1))
                        pe.matmul(bank.rearrange("p (g m) -> p g m", g=Q), onesb[:],
                                  maskneg[:, None, bass.ds(b2 * M, M)].to_broadcast([P, Q, M]),
                                  start=True, stop=False)
                        pe.matmul(bank, qT[par][:], kblk[par][:, q * QW:(q + 1) * QW],
                                  start=False, stop=True).then_inc(e["score"], 1)

                    def turn(q):
                        wait(pe, e["pte"], b3 * 4 + (q - 1))
                        for g in range(Q):
                            at = (Q * q + g) * M
                            mm = pe.transpose(bank_t[q % 2][:, g * S:(g + 1) * S],
                                              prob[odd][:, at:at + P], ident)
                        mm.then_inc(e["pt"], 1)

                    def values(q):
                        pe.wait_ge(e["pte"], b3 * 4 + (q + 1))
                        for g in range(Q):
                            mm = pe.matmul(bank_o[32 * g:32 * g + 32, 0:S],
                                           vm[odd][:, q, 32 * g:32 * g + 32],
                                           pts[q % 2][:, g * S:(g + 1) * S],
                                           start=(q == 0), stop=(q == Q - 1))
                        mm.then_inc(e["pv"], 1)

                    if live(2):
                        pe.wait_ge(e["kb"], b2 + 1)
                        pe.wait_ge(e["q"], b2 + 1)
                        scores(0)
                        scores(1)
                    if live(4):
                        pe.wait_ge(e["rwide"], b4 + 1)
                        wait(pe, e["x1"], b4)
                        pe.matmul(bank_w[:, 0:128], rwide[:].rearrange("p h d -> p (h d)"), ident,
                                  start=True, stop=True).then_inc(e["rp"], 1)
                    if live(6):
                        pe.wait_ge(e["x1nT"], b6 + 1)
                        wait(pe, e["tanh"], b6)
                        wait(pe, e["hx"], b6)
                        for n in range(3):
                            pe.matmul(bank_g[:, n * S:(n + 1) * S], bsplit[:, n, :], onesb[:],
                                      start=(n == 0), stop=False, skip_group_check=True)
                        for n, w in enumerate((WF, WI, WC)):
                            pe.matmul(bank_g[:, n * S:(n + 1) * S], w, x1nT[:], start=False,
                                      stop=False, skip_group_check=True)
                        pe.matmul(bank_g[:, 384:512], x1nT[:], WOF, start=False, stop=False,
                                  skip_group_check=True)
                        pe.wait_ge(e["state"], b6 + 1)
                        for n, w in enumerate((UF, UI, UC)):
                            mm = pe.matmul(bank_g[:, n * S:(n + 1) * S], w, state[:], start=False,
                                           stop=(n == 2), skip_group_check=True)
                        mm.then_inc(e["gates"], 1)
                    if live(3):
                        pe.wait_ge(e["exp"], b3 * 2 + 2)
                        turn(0)
                        turn(1)
                    if live(4):
                        pe.wait_ge(e["att"], b4 + 1)
                        pe.matmul(bank_w[:, 128:256], attT[:], WO, start=True, stop=True
                                  ).then_inc(e["wo"], 1)
                    if live(1):
                        pe.wait_ge(e["xn"], b1 + 1)
                        wait(pe, e["q"], b1)
                        wait(pe, e["x1nT"], i - 5)
                        pe.transpose(bank_x[:, 0:128], xn[odd][:], ident).then_inc(e["xnp"], 1)
                    if live(2):
                        scores(2)
                    if live(3):
                        wait(pe, e["att"], b3)
                        pe.wait_ge(e["vm"], b3 + 1)
                        values(0)
                        turn(2)
                        values(1)
                    if live(5):
                        pe.wait_ge(e["x1n"], b5 + 1)
                        if live(1):
                            pe.wait_ge(e["xnT"], b1 + 1)
                        else:
                            pe.wait_ge(e["q"], B)
                            pe.wait_ge(e["x1nT"], b5)
                        pe.transpose(bank_x[:, 256:384], x1n[:], ident).then_inc(e["x1p"], 1)
                    if live(3):
                        turn(3)
                    if live(2):
                        scores(3)
                    if live(1):
                        pe.wait_ge(e["xnT"], b1 + 1)
                        if live(5):
                            pe.wait_ge(e["x1nT"], b5 + 1)
                        pe.matmul(bank_x[:, 128:256], WQ, xnT[:], start=True, stop=True
                                  ).then_inc(e["qp"], 1)
                    if live(3):
                        values(2)
                        values(3)

                batches(pe, 7, body)

        GW = G4 * D
        cfin = sb("cfin", [P, D])
        mom3 = [sb(f"mom3_{n}", [P, G4, 2]) for n in range(2)]
        stat3 = sb("stat3", [P, G4, 6])
        ve3, rs3 = sb("ve3", [P, G4]), [sb(f"rs3_{n}", [P, G4]) for n in range(2)]
        shift3 = [sb(f"shift3_{n}", [P, G4]) for n in range(2)]
        mags = sb("mags", [P, NG])
        f = {n: sem("f_" + n) for n in "cf cfin pre tanh x2 stat mom ve rs shift ln mag".split()}

        def group(t, g):
            return t[:, bass.ds(g * GW, GW)]

        def four(ap):
            return ap.rearrange("p (j d) -> p j d", j=G4)

        with nc.Block() as block:
            @block.tensor
            def _(pe):
                pe.matmul(ps[0][:, 0:D], state[:], UO, start=True, stop=True).then_inc(f["cf"], 1)

            @block.vector
            def _(dve):
                dve.wait_ge(f["cf"], 1)
                dve.tensor_tensor(cfin[:], ps[0][:, 0:D], brep[:, 0, :], ALU.add
                                  ).then_inc(f["cfin"], 1)
                dve.wait_ge(f["cfin"], 1)

                def body(i, par, live):
                    odd = 1 - par
                    g2, g3, g5 = i - 2, i - 3, i - 5
                    if live(0):
                        dve.tensor_tensor(four(group(HX, i)), four(group(HX, i)),
                                          cfin[:, None, :].to_broadcast([P, G4, D]), ALU.add
                                          ).then_inc(f["pre"], 1)
                    if live(2):
                        dve.wait_ge(f["x2"], g2 + 1)
                        wait(dve, f["mom"], g2 * G4)
                        for j in range(G4):
                            dve.sem_inc(s_tick, 1)
                            dve.bn_stats(stat3[:, j, :], row(g2 * G4 + j)
                                         ).then_inc(f["stat"], 1)
                    if live(3):
                        dve.wait_ge(f["rs"], g3 + 1)
                        wait(dve, f["ln"], g3 - 1)
                        dve.scalar_tensor_tensor(
                            out=shift3[odd][:], in0=mom3[odd][:, :, 0], scalar=-1.0,
                            in1=rs3[odd][:], op0=ALU.mult, op1=ALU.mult).then_inc(f["shift"], 1)
                    if live(5):
                        dve.wait_ge(f["ln"], g5 + 1)
                        dve.tensor_reduce(mags[:, bass.ds(g5, 1)], group(R3, g5), AX.X, ALU.max,
                                          apply_absolute_value=True).then_inc(f["mag"], 1)
                    if live(2):
                        dve.wait_ge(f["stat"], g2 * G4 + G4)
                        wait(dve, f["ln"], g2 - 1)
                        for j in range(G4):
                            dve.sem_inc(s_tick, 1)
                            dve.bn_aggr(mom3[par][:, j, :], stat3[:, j, :]).then_inc(f["mom"], 1)

                batches(dve, 6, body, NG)
                dve.wait_ge(f["mag"], NG)
                dve.tensor_reduce(col(AMAX), mags[:], AX.X, ALU.max).then_inc(s_allin, 1)
                quantum(dve, 4)
                dlink(dve, dve.tensor_tensor(col(K_TXT), col(IS), col(WS + 2), ALU.mult))

            @block.scalar
            def _(act):
                act.activation(warm[:], bcol[:, 0:1], ACT.Exp).then_inc(s_act, 1)

                def body(i, par, live):
                    if live(0):
                        act.wait_ge(f["pre"], i + 1)
                        act.activation(group(HX, i), group(HX, i), ACT.Tanh).then_inc(f["tanh"], 1)
                    if live(3):
                        g = i - 3
                        act.wait_ge(f["shift"], g + 1)
                        for j in range(G4):
                            ins = act.activation(
                                R3[:, bass.ds((g * G4 + j) * D, D)], row(g * G4 + j),
                                ACT.Identity, bias=shift3[1 - par][:, j:j + 1],
                                scale=rs3[1 - par][:, j:j + 1])
                        ins.then_inc(f["ln"], 1)

                batches(act, 6, body, NG)

            @block.gpsimd
            def _(pool):
                def body(i, par, live):
                    g1, g2 = i - 1, i - 2
                    if live(1):
                        pool.wait_ge(f["tanh"], g1 + 1)
                        pool.tensor_tensor(rows4(g1), rows4(g1), four(group(HX, g1)), ALU.add
                                           ).then_inc(f["x2"], 1)
                    if live(2):
                        pool.wait_ge(f["mom"], g2 * G4 + G4)
                        wait(pool, f["rs"], g2)
                        pool.tensor_tensor(ve3[:], mom3[par][:, :, 1], col(EPS5).to_broadcast([P, G4]),
                                           ALU.add).then_inc(f["ve"], 1)
                        pool.wait_ge(f["ve"], g2 + 1)
                        wait(pool, f["ln"], g2 - 1)
                        pool.tensor_tensor(rs3[par][:], ve3[:], col(NHALF).to_broadcast([P, G4]),
                                           ALU.pow).then_inc(f["rs"], 1)

                batches(pool, 6, body, NG)
                pool.wait_ge(s_allin, 4)
                pool.partition_all_reduce(col(AALL), col(AMAX), P, RMAX).then_inc(s_allout, 1)

        FT = R2
        MW = G4 * M
        EW = MW + (P - M) + 1
        ISE = float(D) ** -0.5
        used = {"work": 0, "kT": 0, "maskneg": 0}
        room = {"work": work[:], "kT": kT[:], "maskneg": maskneg[:].bitcast(F32)}

        def lend(width, dt=F32):
            words = -(-width * 2 // 4) if dt == BF16 else width
            for name, tile in room.items():
                at = used[name]
                if at + words <= tile.shape[1]:
                    used[name] += words
                    t = tile[:, at:at + words]
                    return t.bitcast(dt)[:, 0:width] if dt != F32 else t
            raise AssertionError("no room")

        tq = lend(GW)
        qx = [lend(GW, BF16) for n in range(2)]
        qxT = lend(GW, BF16)
        fus = [[lend(GW) for n in range(4)], [vm[n][:].rearrange("p q d -> p (q d)") for n in range(2)]
               + [pts[n][:] for n in range(2)]]
        kx = [lend(MW) for n in range(2)]
        kp = [lend(2 * GW).rearrange("p (t c) -> p t c", t=2) for n in range(2)]
        p3 = [[lend(EW) for t in range(2)] for n in range(2)]
        p3T = [lend(GW) for n in range(2)]
        mx = [sb(f"mx{n}", [P, G4]) for n in range(2)]
        sm = [sb(f"sm{n}", [P, G4]) for n in range(2)]
        rc = [sb(f"rc{n}", [P, G4]) for n in range(2)]
        b01 = sb("b01", [P, 2])
        scored = ps[3][:, 0:MW], ps[7][:, 0:MW]
        valued = ps[6], ps[1]
        LAY = ("a", "b")
        h = {n: sem("h_" + n) for n in "tq qx qp qT fp fused done mag".split()}
        for n in "kp_ kx kv_ kv score peak sub exp sum rec norm pt pte out add".split():
            for l in LAY:
                h[n + l] = sem("h_" + n + l)

        with nc.Block() as block:
            @block.vector
            def _(dve):
                for n in range(2):
                    dlink(dve, dve.memset(kp[n], 0.0))
                    for t in range(2):
                        dlink(dve, dve.memset(p3[n][t][:, MW:EW], 0.0))
                dlink(dve, dve.tensor_scalar(b01[:], bcol[:, 3:5], 0.1, None, ALU.mult))
                dve.memset(sm[0][:], 0.0).then_inc(h["done"], 1)

                def peaks(l, g):
                    L, s4 = LAY[l], scored[l].rearrange("p (j m) -> p j m", m=M)
                    dve.wait_ge(h["score" + L], g + 1)
                    wait(dve, h["sub" + L], g)
                    dve.tensor_reduce(mx[l][:], s4, AX.X, ALU.max).then_inc(h["peak" + L], 1)

                def less(l, g, par):
                    L, s4 = LAY[l], scored[l].rearrange("p (j m) -> p j m", m=M)
                    p = p3[l][par][:, 0:MW].rearrange("p (j m) -> p j m", m=M)
                    dve.wait_ge(h["peak" + L], g + 1)
                    wait(dve, h["pt" + L], g - 1)
                    dve.tensor_tensor(p, s4, mx[l][:, :, None].to_broadcast([P, G4, M]), ALU.subtract
                                      ).then_inc(h["sub" + L], 1)

                def normalise(l, g, par):
                    L, p = LAY[l], p3[l][par][:, 0:MW].rearrange("p (j m) -> p j m", m=M)
                    dve.wait_ge(h["exp" + L], g + 1)
                    wait(dve, h["rec" + L], g)
                    dve.tensor_reduce(sm[l][:], p, AX.X, ALU.add).then_inc(h["sum" + L], 1)
                    dve.wait_ge(h["sum" + L], g + 1)
                    wait(dve, h["norm" + L], g)
                    dve.reciprocal(rc[l][:], sm[l][:]).then_inc(h["rec" + L], 1)
                    dve.wait_ge(h["rec" + L], g + 1)
                    dve.scalar_tensor_tensor(
                        out=p, in0=p, scalar=0.1, in1=rc[l][:, :, None].to_broadcast([P, G4, M]),
                        op0=ALU.mult, op1=ALU.mult).then_inc(h["norm" + L], 1)

                def body(i, ph, live):
                    g2, g4, g5, g7 = (i - n for n in (2, 4, 5, 7))
                    par, odd = ph % 2, (ph + 1) % 2
                    if live(4):
                        dve.wait_ge(h["outa"], g4 + 1)
                        wait(dve, h["addb"], g4 - 3)
                        dve.scalar_tensor_tensor(out=fus[1][ph], in0=valued[0], scalar=b01[:, 0:1],
                                                 in1=fus[0][ph], op0=ALU.add, op1=ALU.add
                                                 ).then_inc(h["adda"], 1)
                    if live(2):
                        peaks(0, g2)
                    if live(5):
                        peaks(1, g5)
                    if live(2):
                        less(0, g2, par)
                    if live(5):
                        less(1, g5, odd)
                    if live(7):
                        dve.wait_ge(h["outb"], g7 + 1)
                        dve.scalar_tensor_tensor(out=group(FT, g7), in0=valued[1],
                                                 scalar=b01[:, 1:2], in1=fus[1][(ph + 1) % 4],
                                                 op0=ALU.add, op1=ALU.add).then_inc(h["addb"], 1)
                    if live(2):
                        normalise(0, g2, par)
                    if live(7):
                        dve.wait_ge(h["addb"], g7 + 1)
                        dve.tensor_reduce(mags[:, bass.ds(g7, 1)], group(FT, g7), AX.X, ALU.max,
                                          apply_absolute_value=True).then_inc(h["mag"], 1)
                    if live(5):
                        normalise(1, g5, odd)

                batches(dve, 8, body, NG, 4)

            @block.scalar
            def _(act):
                act.activation(warm[:], bcol[:, 0:1], ACT.Exp).then_inc(s_act, 1)
                act.wait_ge(h["done"], 1)

                def keys(l, g):
                    L = LAY[l]
                    act.wait_ge(h["kp_" + L], g + 1)
                    wait(act, h["score" + L], g)
                    act.activation(kx[l], ps[2][:, 0:MW], ACT.Identity,
                                   bias=bcol[:, 3 + l:4 + l], scale=col(K_A[l])
                                   ).then_inc(h["kx" + L], 1)

                def weighed(l, g, par):
                    L = LAY[l]
                    act.wait_ge(h["kv_" + L], g + 1)
                    wait(act, h["out" + L], g - 1)
                    act.activation(kp[l][0:M, par, :], ps[4][0:M, :], ACT.Copy,
                                   scale=col(K_A[l], M)).then_inc(h["kv" + L], 1)

                def exponential(l, g, par):
                    L, p = LAY[l], p3[l][par][:, 0:MW]
                    act.wait_ge(h["sub" + L], g + 1)
                    act.activation(p, p, ACT.Exp, scale=ISE).then_inc(h["exp" + L], 1)

                def turned(l, g):
                    L = LAY[l]
                    act.wait_ge(h["pt" + L], g + 1)
                    wait(act, h["out" + L], g)
                    act.copy(p3T[l], ps[5][:]).then_inc(h["pte" + L], 1)

                def body(i, ph, live):
                    g0, g1, g2, g3, g4, g5, g6 = (i - n for n in range(7))
                    par, odd = ph % 2, (ph + 1) % 2
                    if live(3):
                        turned(0, g3)
                    if live(1):
                        act.wait_ge(h["qp"], g1 + 1)
                        wait(act, h["fp"], g1)
                        act.copy(qxT, ps[0][:].bitcast(BF16)[:, 0:GW]).then_inc(h["qT"], 1)
                    if live(2):
                        exponential(0, g2, par)
                    if live(1):
                        keys(0, g1)
                    if live(2):
                        weighed(0, g2, par)
                    if live(5):
                        exponential(1, g5, odd)
                    if live(6):
                        turned(1, g6)
                    if live(1):
                        act.wait_ge(h["fp"], g1 + 1)
                        wait(act, h["adda"], g1 - 3)
                        act.activation(fus[0][(ph + 3) % 4], ps[0][:], ACT.Identity,
                                       bias=bcol[:, 2:3], scale=col(K_TXT)).then_inc(h["fused"], 1)
                    if live(4):
                        keys(1, g4)
                    if live(5):
                        weighed(1, g5, odd)

                batches(act, 8, body, NG, 4)

            @block.gpsimd
            def _(pool):
                def body(i, ph, live):
                    if live(0):
                        pool.tensor_tensor(group(R3, i), group(R3, i),
                                           col(INV).to_broadcast([P, GW]), ALU.mult
                                           ).then_inc(h["tq"], 1)
                        pool.wait_ge(h["tq"], i * 3 + 1)
                        wait(pool, h["qx"], i)
                        pool.sem_inc(h["tq"], 1)
                        pool.tensor_tensor(tq, group(R3, i), col(MAG).to_broadcast([P, GW]), ALU.add
                                           ).then_inc(h["tq"], 1)
                        pool.wait_ge(h["tq"], i * 3 + 3)
                        wait(pool, h["qp"], i - 1)
                        pool.tensor_tensor(qx[ph % 2], tq, col(MAG).to_broadcast([P, GW]),
                                           ALU.subtract).then_inc(h["qx"], 1)

                batches(pool, 8, body, NG, 4)

            @block.tensor
            def _(pe):
                pe.wait_ge(h["done"], 1)
                tb = ps[0][:].bitcast(BF16)

                def keys(l, g):
                    pe.matmul(ps[2][:, 0:MW], ternd["att" + str(l)], qimg[:, bass.ds(g * MW, MW)],
                              start=True, stop=True).then_inc(h["kp_" + LAY[l]], 1)

                def weighed(l, g):
                    for j in range(G4):
                        mm = pe.matmul(ps[4][0:M, j * D:(j + 1) * D],
                                       qimg[:, bass.ds((g * G4 + j) * M, M)], ternd["att" + str(l)],
                                       start=True, stop=True)
                    mm.then_inc(h["kv_" + LAY[l]], 1)

                def scores(l, g, ph):
                    L = LAY[l]
                    pe.wait_ge(h["kx" + L], g + 1)
                    wait(pe, h["sub" + L], g)
                    for j in range(G4):
                        mm = pe.matmul(scored[l][:, j * M:(j + 1) * M],
                                       fus[l][ph][:, j * S:(j + 1) * S],
                                       kx[l][:, j * M:(j + 1) * M], start=True, stop=True)
                    mm.then_inc(h["score" + L], 1)

                def turn(l, g, par):
                    L = LAY[l]
                    pe.wait_ge(h["norm" + L], g + 1)
                    for j in range(G4):
                        mm = pe.transpose(ps[5][:, j * S:(j + 1) * S],
                                          p3[l][par][:, j * M:j * M + P], ident)
                    mm.then_inc(h["pt" + L], 1)

                def values(l, g, par):
                    L = LAY[l]
                    pe.wait_ge(h["pte" + L], g + 1)
                    pe.wait_ge(h["kv" + L], g + 1)
                    wait(pe, h["add" + L], g)
                    for j in range(G4):
                        mm = pe.matmul(valued[l][:, j * S:(j + 1) * S],
                                       kp[l][:, par, j * D:(j + 1) * D],
                                       p3T[l][:, j * S:(j + 1) * S], start=True, stop=True)
                    mm.then_inc(h["out" + L], 1)

                def upto(n):
                    return min(n, NG) if isinstance(n, int) else n

                def body(i, ph, live):
                    g0, g1, g2, g3, g4, g5, g6 = (i - n for n in range(7))
                    par, odd = ph % 2, (ph + 1) % 2
                    if live(2):
                        pe.wait_ge(h["fused"], g2 + 1)
                        scores(0, g2, (ph + 2) % 4)
                    if live(5):
                        pe.wait_ge(h["adda"], g5 + 1)
                        scores(1, g5, (ph + 3) % 4)
                    if live(3):
                        wait(pe, h["pteb"], g3 - 3)
                        turn(0, g3, odd)
                    if live(1):
                        pe.wait_ge(h["qx"], g1 + 1)
                        wait(pe, h["fused"], g1)
                        for j in range(G4):
                            mm = pe.transpose(tb[:, j * S:(j + 1) * S],
                                              qx[odd][:, j * D:(j + 1) * D], identb[:])
                        mm.then_inc(h["qp"], 1)
                        wait(pe, h["kxb"], g1 - 3)
                        keys(0, g1)
                    if live(2):
                        wait(pe, h["kvb"], g2 - 3)
                        weighed(0, g2)
                    if live(3):
                        values(0, g3, odd)
                    if live(1):
                        pe.wait_ge(h["qT"], g1 + 1)
                        pe.matmul(ps[0][:], ternd["txt"], qxT, start=True, stop=True
                                  ).then_inc(h["fp"], 1)
                    if live(6):
                        pe.wait_ge(h["ptea"], upto(g6 + 4))
                        wait(pe, h["pteb"], g6)
                        turn(1, g6, par)
                    if live(4):
                        pe.wait_ge(h["kxa"], upto(g4 + 4))
                        wait(pe, h["kxb"], g4)
                        keys(1, g4)
                    if live(5):
                        pe.wait_ge(h["kva"], upto(g5 + 4))
                        wait(pe, h["kvb"], g5)
                        weighed(1, g5)
                    if live(6):
                        values(1, g6, par)

                batches(pe, 8, body, NG, 4)

        for n in used:
            used[n] = 0
        qf = R3[:].bitcast(BF16)
        qavg = lend(B, BF16)
        tq = [lend(GW) for n in range(2)]
        hpk = lend(NG * 4)
        hm = lend(4)
        f1w = ternd["f1"].rearrange("p (k n) -> p k n", k=2)
        f2w = ternd["f2"].rearrange("p (k n) -> p k n", k=4)
        m = {n: sem("m_" + n) for n in "qavg tq qf f1 peak b2 blank".split()}
        blank = sb("blank", [P, RW])
        sorted_rows = nc.dram_tensor("sorted_rows", (E * CAP + P, RW), F32, kind="Internal").ap()

        def hidden(pe, bank, g, c):
            pe.matmul(bank, f1w[:, 0, c * P:(c + 1) * P], group(qf, g), start=True, stop=False)
            return pe.matmul(four(bank), f1w[:, 1, c * P:(c + 1) * P],
                             qavg[:, bass.ds(g * G4, G4), None].to_broadcast([P, G4, S]),
                             start=False, stop=True)

        with nc.Block() as block:
            @block.vector
            def _(dve):
                dlink(dve, dve.tensor_reduce(hm[:, 0:1], mags[:], AX.X, ALU.max))
                dlink(dve, dve.tensor_reduce(hm[:, 1:2], avgT[:], AX.X, ALU.max,
                                             apply_absolute_value=True))
                dve.tensor_tensor(col(AMAX), hm[:, 0:1], hm[:, 1:2], ALU.max).then_inc(s_allin, 1)
                quantum(dve, 5)
                dlink(dve, dve.tensor_tensor(col(K_F1), col(IS), col(WS + 5), ALU.mult))
                dlink(dve, dve.tensor_scalar(avgT[:], avgT[:], col(INV), MAGIC, ALU.mult, ALU.add))
                dve.tensor_scalar(qavg, avgT[:], MAGIC, None, ALU.subtract).then_inc(m["qavg"], 1)

                def body(i, par, live):
                    if live(1):
                        g = i - 1
                        dve.wait_ge(m["f1"], g + 1)
                        dve.tensor_reduce(hpk[:, bass.ds(g * 4, 4)],
                                          psum[:, 4 * (1 - par):4 * (1 - par) + 4, :], AX.X, ALU.max
                                          ).then_inc(m["peak"], 1)

                batches(dve, 2, body, NG)
                dve.wait_ge(m["peak"], NG)
                dlink(dve, dve.tensor_reduce(hm, hpk.rearrange("p (g c) -> p c g", c=4), AX.X, ALU.max))
                dlink(dve, dve.scalar_tensor_tensor(out=hm, in0=hm, scalar=col(K_F1),
                                                    in1=bcol[:, 5:9], op0=ALU.mult, op1=ALU.add))
                dlink(dve, dve.tensor_reduce(hm[:, 0:1], hm, AX.X, ALU.max))
                dve.tensor_scalar(col(AMAX), hm[:, 0:1], 0.0, None, ALU.max).then_inc(s_allin, 1)
                quantum(dve, 6)
                dlink(dve, dve.tensor_tensor(col(K_H), col(K_F1), col(INV), ALU.mult))
                dlink(dve, dve.tensor_tensor(col(K_F2), col(IS), col(WS + 6), ALU.mult))
                dlink(dve, dve.tensor_scalar(sc[:, B_F1:B_F1 + 4], bcol[:, 5:9], col(INV), None,
                                             ALU.mult))

            @block.scalar
            def _(act):
                act.wait_ge(m["qavg"], 1)

                def body(i, par, live):
                    if live(0):
                        wait(act, m["qf"], i - 1)
                        act.activation(tq[par], group(FT, i), ACT.Copy, bias=MAGIC, scale=col(INV)
                                       ).then_inc(m["tq"], 1)

                batches(act, 2, body, NG)

            @block.gpsimd
            def _(pool):
                pool.wait_ge(s_allin, 5)
                pool.partition_all_reduce(col(AALL), col(AMAX), P, RMAX).then_inc(s_allout, 1)

                def body(i, par, live):
                    if live(0):
                        pool.wait_ge(m["tq"], i + 1)
                        pool.sem_inc(m["b2"], 1)
                        pool.tensor_tensor(group(qf, i), tq[par], col(MAG).to_broadcast([P, GW]),
                                           ALU.subtract).then_inc(m["qf"], 1)
                        pool.tensor_tensor(rows4(i), rows4(i),
                                           brep[:, 1:2, :].to_broadcast([P, G4, D]), ALU.add
                                           ).then_inc(m["b2"], 1)

                batches(pool, 2, body, NG)
                pool.wait_ge(s_allin, 6)
                pool.partition_all_reduce(col(AALL), col(AMAX), P, RMAX).then_inc(s_allout, 1)
                pool.memset(blank[:], 0.0).then_inc(m["blank"], 1)
                pool.wait_ge(m["blank"], 1)
                pool.memset(blank[:].bitcast(I32)[:, D + TOKEN:D + TOKEN + 1], NT).then_inc(m["blank"], 1)
                pool.iota(X[:].bitcast(I32)[:, :, D + TOKEN], [[P, B]], base=0, channel_multiplier=1
                          ).then_inc(m["b2"], 1)

            @block.tensor
            def _(pe):
                pe.wait_ge(m["qavg"], 1)

                def body(i, par, live):
                    if live(1):
                        g = i - 1
                        pe.wait_ge(m["qf"], g + 1)
                        wait(pe, m["peak"], g - 1)
                        for c in range(4):
                            mm = hidden(pe, ps[4 * (1 - par) + c], g, c)
                        mm.then_inc(m["f1"], 1)

                batches(pe, 2, body, NG)

        for n in used:
            used[n] = 0
        qavg = lend(B, BF16)
        W1 = R2[:, 0:E * F]
        W2 = R2[:, E * F:2 * E * F]
        relu = [lend(GW) for n in range(4)]
        qh = [lend(4 * GW, BF16).rearrange("p (c t) -> p c t", c=4) for n in range(2)]
        xs = lend(GW)
        xsT = lend(GW)
        stat4 = sb("stat4", [P, G4, 6])
        mom4 = sb("mom4", [P, G4, 2])
        gw = sb("gw", [P, E])
        ms2 = sb("ms2", [P, G4])
        logit = sb("logit", [P, E, B])
        RB = 4 * G4
        cube = lambda t: t.rearrange("p (e b) -> p e b", e=E)
        turned_cube = lambda t: t.rearrange("p (e b) -> p b e", e=E)
        wide = lambda t: t[:, None, :].to_broadcast([P, E, RB])
        less, chance, choice, place = (lend(E * RB) for n in range(4))
        ohb, trib = lend(E * RB, BF16), lend(P, BF16)
        ones = lend(E * RB)
        best, total5, rec5, pick, pos = (lend(RB) for n in range(5))
        ends, run, shift, number = lend(E + 1), lend(E), lend(E), lend(E)
        tiles, incl, thr = lend(E), lend(E), lend(E * B)
        cmp, et, rowf = lend(TILES * E), lend(TILES), lend(TILES)
        posi = sb("posi", [P, B], I32)
        fillat = sb("fillat", [1, E], I32)
        wat = sb("wat", [1, TILES], I32)
        rowat = sb("rowat", [1, TILES], I32)
        FD = F + D
        be, bback6 = (R3[0:E, E * F + n * FD:E * F + (n + 1) * FD] for n in range(2))
        bpart = [R3[:].bitcast(BF16)[0:E, 2 * (E * F + 2 * FD) + n * FD:
                                     2 * (E * F + 2 * FD) + (n + 1) * FD] for n in range(3)]
        bsum = R3[:].bitcast(BF16)[:, 0:2 * E * F].rearrange("p (k e f) -> p k e f", k=2, e=E)
        B1S, B2S = (R3[:].bitcast(BF16)[:, k * E * F:(k + 1) * E * F] for k in range(2))
        SOFT, CHOICE, PLACE = 4, 16, 28
        o = {n: sem("o_" + n) for n in
             "route sub exp oh count pos run bias parts rows fill sorted".split()}
        x = {n: sem("x_" + n) for n in
             "w gw f1 relu qh f2 x3 xs stat mom ms mean rs xp xsT gate logit".split()}

        def extra(n, g=None):
            if g is None:
                return X[:, :, D + n]
            return Xf[:, bass.ds(g * (G4 * RW), G4 * RW)].rearrange(
                "p (j w) -> p j w", j=G4)[:, :, D + n]

        with nc.Block() as block:
            @block.sync
            def _(sp):
                for e_ in range(E):
                    sp.dma_start(W1[:, e_ * F:(e_ + 1) * F], a["w1"][e_]).then_inc(x["w"], 16)
                    sp.dma_start(W2[:, e_ * F:(e_ + 1) * F].rearrange("p (c d) -> p c d", c=4),
                                 a["w2"][e_].rearrange("(c p) d -> p c d", p=P)).then_inc(x["w"], 16)
                sp.dma_start(gw[:], a["gw"]).then_inc(x["gw"], 16)
                sp.dma_start(be[:, 0:F], a["b1"]).then_inc(o["bias"], 16)
                sp.dma_start(be[:, F:F + D], a["b2"]).then_inc(o["bias"], 16)
                sp.dma_start(sorted_rows[E * CAP:E * CAP + P, :], blank[:]).then_inc(o["fill"], 16)
                sp.wait_ge(o["run"], 1)
                for e_ in range(E):
                    at = sp.value_load(fillat[0:1, e_:e_ + 1], min_val=0, max_val=E * CAP)
                    sp.dma_start(sorted_rows[bass.ds(at, P), :], blank[:]).then_inc(o["fill"], 16)
                sp.wait_ge(o["parts"], 4)
                for n in range(3):
                    sp.dma_start(bsum[n:n + 1, 0, :, :], bpart[n][:, 0:F]).then_inc(o["rows"], 16)
                    sp.dma_start(bsum[n:n + 1, 1, :, 0:D], bpart[n][:, F:F + D]
                                 ).then_inc(o["rows"], 16)
                sp.wait_ge(o["rows"], 96)
                sp.wait_ge(o["fill"], 16 * (E + 1))
                sp.wait_ge(x["w"], 32 * E)

            @block.vector
            def _(dve):
                dve.wait_ge(x["gw"], 16)
                dve.tensor_scalar(gw[:], gw[:], bcol[:, 10:11], None, ALU.mult).then_inc(x["gw"], 1)
                dlink(dve, dve.tensor_copy(trib, cst[:, C_TRI:C_TRI + P]))
                dlink(dve, dve.memset(ones, 1.0))
                dlink(dve, dve.memset(ends[:, 0:1], 0.0))
                dlink(dve, dve.tensor_scalar(run, cst[:, C_IOTA:C_IOTA + E], float(CAP), None, ALU.mult))

                def chained(c4, first, end, steps):
                    for n, step in enumerate(steps, first + 1):
                        last = n == first + len(steps)
                        step().then_inc(o["route"], end - n + 1 if last else 1)
                        dve.wait_ge(o["route"], c4 * (PLACE // 4) + (end if last else n))

                def softmaxed(c4):
                    chunk = logit[:, :, bass.ds(c4 * G4, RB)]
                    chained(c4, 0, SOFT, [
                        lambda: dve.tensor_reduce(best, chunk.rearrange("p e b -> p b e"), AX.X, ALU.max),
                        lambda: dve.tensor_tensor(cube(less), chunk, wide(best), ALU.subtract)])
                    dve.sem_inc(o["sub"], 4)

                def choose(c4):
                    dve.wait_ge(o["exp"], c4 + 4)
                    chained(c4, SOFT, CHOICE, [
                        lambda: dve.tensor_reduce(total5, turned_cube(chance), AX.X, ALU.add),
                        lambda: dve.reciprocal(rec5, total5),
                        lambda: dve.tensor_tensor(cube(chance), cube(chance), wide(rec5), ALU.mult),
                        lambda: dve.tensor_reduce(best, turned_cube(chance), AX.X, ALU.max),
                        lambda: dve.tensor_scalar(
                            Xf[:, bass.ds(c4 * (G4 * RW), RB * RW)].rearrange(
                                "p (j w) -> p j w", j=RB)[:, :, D + SCORE], best, 0.5, None, ALU.mult),
                        lambda: dve.tensor_tensor(cube(choice), cube(chance), wide(best), ALU.is_equal),
                        lambda: dve.scalar_tensor_tensor(
                            out=cube(choice), in0=cube(choice), scalar=-float(E),
                            in1=cst[:, C_IOTA:C_IOTA + E, None].to_broadcast([P, E, RB]),
                            op0=ALU.mult, op1=ALU.add),
                        lambda: dve.tensor_reduce(pick, turned_cube(choice), AX.X, ALU.min),
                        lambda: dve.tensor_tensor(cube(ohb), cube(choice), wide(pick), ALU.is_equal)])
                    dve.sem_inc(o["oh"], 4)

                def placed(c4):
                    here, all_ = (ps[7][:, n * E * RB:(n + 1) * E * RB] for n in range(2))
                    dve.wait_ge(o["count"], c4 + 4)
                    chained(c4, CHOICE, PLACE, [
                        lambda: dve.tensor_tensor_scan(place, ones, all_, 0.0, ALU.mult, ALU.add),
                        lambda: dve.tensor_copy(ends[:, 1:E + 1], cube(place)[:, :, RB - 1]),
                        lambda: dve.tensor_tensor(shift, run, ends[:, 0:E], ALU.subtract),
                        lambda: dve.tensor_tensor(number, ends[:, 1:E + 1], ends[:, 0:E], ALU.subtract),
                        lambda: dve.tensor_tensor(run, run, number, ALU.add),
                        lambda: dve.tensor_tensor(place, place, all_, ALU.subtract),
                        lambda: dve.tensor_tensor(place, place, here, ALU.add),
                        lambda: dve.tensor_tensor(cube(place), cube(place),
                                                  shift[:, :, None].to_broadcast([P, E, RB]), ALU.add),
                        lambda: dve.tensor_tensor(place, place, ohb, ALU.mult),
                        lambda: dve.tensor_reduce(pos, turned_cube(place), AX.X, ALU.add),
                        lambda: dve.tensor_copy(posi[:, bass.ds(c4 * G4, RB)], pos)])
                    dve.sem_inc(o["pos"], 4)

                def body(i, ph, live):
                    par = ph % 2
                    g1, g2, g3, g4 = (i - n for n in range(1, 5))
                    if live(1):
                        wait(dve, x["f2"], g1 - 1)
                        for c in range(4):
                            dve.wait_ge(x["relu"], g1 * 4 + (c + 1))
                            dve.tensor_scalar(qh[1 - par][:, c, :], relu[c], MAGIC, MAGIC, ALU.add,
                                              ALU.subtract).then_inc(x["qh"], 1)
                    if live(2):
                        dve.wait_ge(x["f2"], g2 + 1)
                        dve.scalar_tensor_tensor(out=rows4(g2), in0=four(ps[4]), scalar=col(K_F2),
                                                 in1=rows4(g2), op0=ALU.mult, op1=ALU.add
                                                 ).then_inc(x["x3"], 1)
                    if live(3):
                        dve.wait_ge(x["rs"], g3 + 1)
                        dve.wait_ge(x["mean"], g3 + 1)
                        wait(dve, x["xp"], g3)
                        for j in range(G4):
                            dve.tensor_scalar(xs[:, j * D:(j + 1) * D], row(g3 * G4 + j),
                                              extra(MEAN, g3)[:, j:j + 1], extra(RSTD, g3)[:, j:j + 1],
                                              ALU.subtract, ALU.mult).then_inc(x["xs"], 1)
                    if live(2):
                        dve.wait_ge(x["x3"], g2 + 1)
                        wait(dve, x["mom"], g2 * G4)
                        for j in range(G4):
                            dve.sem_inc(s_tick, 1)
                            dve.bn_stats(stat4[:, j, :], row(g2 * G4 + j)).then_inc(x["stat"], 1)
                    if live(4):
                        dve.wait_ge(x["gate"], g4 + 1)
                        dve.tensor_copy(logit[:, :, bass.ds(g4 * G4, G4)],
                                        ps[6][:, 0:G4 * E].rearrange("p (j e) -> p e j", e=E)
                                        ).then_inc(x["logit"], 1)
                    if live(2):
                        dve.wait_ge(x["stat"], g2 * G4 + G4)
                        wait(dve, x["ms"], g2)
                        wait(dve, x["mean"], g2)
                        for j in range(G4):
                            dve.sem_inc(s_tick, 1)
                            dve.bn_aggr(mom4[:, j, :], stat4[:, j, :]).then_inc(x["mom"], 1)
                        dve.wait_ge(x["mom"], g2 * G4 + G4)
                        wait(dve, x["rs"], g2)
                        dve.tensor_scalar(ms2[:], mom4[:, :, 1], 1.0 + 1e-6, 1e-11, ALU.mult, ALU.add
                                          ).then_inc(x["ms"], 1)
                        dve.tensor_copy(extra(MEAN, g2), mom4[:, :, 0]).then_inc(x["mean"], 1)
                    for part, route in enumerate((softmaxed, choose, placed)):
                        if ph == part and live(8 + part):
                            dve.wait_ge(x["logit"], i - ph - 4)
                            route(i - ph - 8)

                batches(dve, 8, body, NG, 4)

                dve.tensor_copy(fillat[:], run[0:1]).then_inc(o["run"], 1)
                dlink(dve, dve.scalar_tensor_tensor(
                    out=number, in0=cst[:, C_IOTA:C_IOTA + E], scalar=-float(CAP), in1=run,
                    op0=ALU.mult, op1=ALU.add))
                dlink(dve, dve.tensor_tensor(
                    cube(thr), number[:, :, None].to_broadcast([P, E, B]),
                    cst[:, None, C_T:C_T + B].to_broadcast([P, E, B]), ALU.is_gt))
                dlink(dve, dve.tensor_reduce(tiles, cube(thr), AX.X, ALU.add))
                dlink(dve, dve.tensor_tensor_scan(incl, ones[:, 0:E], tiles, 0.0, ALU.mult, ALU.add))
                past = cmp[0:1].rearrange("p (t e) -> p t e", e=E)
                dlink(dve, dve.tensor_tensor(
                    past, cst[0:1, C_TILE:C_TILE + TILES, None].to_broadcast([1, TILES, E]),
                    incl[0:1, None, :].to_broadcast([1, TILES, E]), ALU.is_ge))
                dlink(dve, dve.tensor_reduce(et[0:1], past, AX.X, ALU.add))
                dlink(dve, dve.tensor_tensor(past, past, tiles[0:1, None, :].to_broadcast([1, TILES, E]),
                                             ALU.mult))
                dlink(dve, dve.tensor_reduce(rowf[0:1], past, AX.X, ALU.add))
                dlink(dve, dve.tensor_tensor(rowf[0:1], cst[0:1, C_TILE:C_TILE + TILES], rowf[0:1],
                                             ALU.subtract))
                dlink(dve, dve.tensor_scalar(rowf[0:1], rowf[0:1], float(P), None, ALU.mult))
                dlink(dve, dve.scalar_tensor_tensor(out=rowf[0:1], in0=et[0:1], scalar=float(CAP),
                                                    in1=rowf[0:1], op0=ALU.mult, op1=ALU.add))
                dlink(dve, dve.tensor_scalar(rowat[:], rowf[0:1], float(E * CAP), None, ALU.min))
                dlink(dve, dve.tensor_scalar(wat[:], et[0:1], float(E - 1), float(F), ALU.min,
                                             ALU.mult))
                dve.wait_ge(x["w"], 32 * E)
                dlink(dve, dve.tensor_scalar(W1, W1, bcol[:, 10:11], None, ALU.mult))
                dve.memset(R3[:, 0:E * F], 0.0).then_inc(o["parts"], 1)
                dve.wait_ge(o["bias"], 32)
                dlink(dve, dve.tensor_scalar(be[:, F:F + D], be[:, F:F + D], 2.0, None, ALU.mult))
                for n in range(3):
                    dve.tensor_copy(bpart[n], be).then_inc(o["parts"], 1)
                    if n < 2:
                        dve.wait_ge(o["parts"], n + 2)
                        dlink(dve, dve.tensor_copy(bback6, bpart[n]))
                        dlink(dve, dve.tensor_tensor(be, be, bback6, ALU.subtract))

            @block.scalar
            def _(act):
                def body(i, ph, live):
                    g3 = i - 3
                    if live(0):
                        for c in range(4):
                            act.wait_ge(x["f1"], i * 4 + (c + 1))
                            wait(act, x["qh"], i * 4 + (c - 3))
                            act.activation(relu[c], ps[c], ACT.Relu, scale=col(K_H),
                                           bias=col(B_F1 + c)).then_inc(x["relu"], 1)
                    if live(3):
                        act.wait_ge(x["xp"], g3 + 1)
                        wait(act, x["gate"], g3)
                        act.copy(xsT, ps[5]).then_inc(x["xsT"], 1)
                    if ph == 0 and live(8):
                        act.wait_ge(o["sub"], i - 8 + 4)
                        act.activation(chance, less, ACT.Exp).then_inc(o["exp"], 4)

                batches(act, 8, body, NG, 4)

            @block.gpsimd
            def _(pool):
                def scatter(g):
                    for b in range(g * G4, (g + 1) * G4):
                        pool.indirect_dma_start(sorted_rows[:], bass.IndirectOffsetOnAxis(
                            posi[:, b:b + 1], 0), X[:, b, :], None).then_inc(o["sorted"], 16)

                for i in range(NG + 7):
                    g2, par = i - 2, i % 2
                    if 0 <= g2 < NG:
                        pool.wait_ge(x["ms"], g2 + 1)
                        pool.tensor_tensor(extra(RSTD, g2), ms2[:], col(NHALF).to_broadcast([P, G4]),
                                           ALU.pow).then_inc(x["rs"], 1)
                    if i >= 11:
                        pool.wait_ge(o["pos"], (i - 11) // 4 * 4 + 4)
                        scatter(i - 11)
                pool.wait_ge(o["pos"], NG)
                for g in range(NG - 4, NG):
                    scatter(g)
                pool.wait_ge(o["sorted"], 16 * B)

            @block.tensor
            def _(pe):
                pe.wait_ge(x["gw"], 17)

                def body(i, ph, live):
                    par = ph % 2
                    g1, g3, g4 = i - 1, i - 3, i - 4
                    if live(0):
                        for c in range(4):
                            wait(pe, x["relu"], i * 4 + (c - 3))
                            hidden(pe, ps[c], i, c).then_inc(x["f1"], 1)
                    if live(4):
                        pe.wait_ge(x["xsT"], g4 + 1)
                        wait(pe, x["logit"], g4)
                        for j in range(G4):
                            mm = pe.matmul(ps[6][:, j * E:(j + 1) * E], xsT[:, j * S:(j + 1) * S],
                                           gw[:], start=True, stop=True)
                        mm.then_inc(x["gate"], 1)
                    if live(3):
                        pe.wait_ge(x["xs"], g3 * G4 + G4)
                        wait(pe, x["xsT"], g3)
                        for j in range(G4):
                            mm = pe.transpose(ps[5][:, j * S:(j + 1) * S], xs[:, j * D:(j + 1) * D],
                                              ident)
                        mm.then_inc(x["xp"], 1)
                    if live(1):
                        pe.wait_ge(x["qh"], g1 * 4 + 4)
                        wait(pe, x["x3"], g1)
                        for j in range(G4):
                            for c in range(4):
                                mm = pe.matmul(ps[4][:, j * D:(j + 1) * D],
                                               qh[1 - par][:, c, j * S:(j + 1) * S], f2w[:, c, :],
                                               start=(c == 0), stop=(c == 3))
                        mm.then_inc(x["f2"], 1)
                    if ph == 1 and live(9):
                        pe.wait_ge(o["oh"], i - 9 + 4)
                        pe.matmul(ps[7][:, 0:E * RB], trib, ohb, start=True, stop=True)
                        pe.matmul(ps[7][:, E * RB:2 * E * RB], onesb[:], ohb, start=True, stop=True
                                  ).then_inc(o["count"], 4)

                batches(pe, 8, body, NG, 4)

        for n in used:
            used[n] = 0
        SLOTS = 8
        srow = [lend(RW) for n in range(SLOTS)]
        xn6 = [lend(D) for n in range(2)]
        xnT6 = [lend(P) for n in range(2)]
        u6 = [lend(F) for n in range(2)]
        th6 = [lend(F) for n in range(2)]
        hT6 = [lend(F) for n in range(2)]
        put = [lend(D) for n in range(4)]
        e = {n: sem("moe_" + n) for n in
             "load0 load1 xn xt xnT w1 u tr tanh h w2 out put0 put1 taken".split()}

        def pairs(i, ph, n=0):
            return (i - ph % 2) * 8 + 16 * (n + 1)

        def expert(pe, i):
            return pe.value_load(wat[0:1, bass.ds(i, 1)], min_val=0, max_val=(E - 1) * F)

        with nc.Block() as block:
            @block.sync
            def _(sp):
                def body(i, ph, live):
                    load, put_ = e["load%d" % (ph % 2)], e["put%d" % (ph % 2)]
                    if live(0):
                        at = sp.value_load(rowat[0:1, bass.ds(i, 1)], min_val=0, max_val=E * CAP)
                        wait(sp, load, pairs(i - 2, ph))
                        wait(sp, put_, pairs(i - SLOTS, ph))
                        sp.dma_start(srow[ph], sorted_rows[bass.ds(at, P), :]).then_inc(load, 16)

                batches(sp, 1, body, TILES, SLOTS)

            @block.vector
            def _(dve):
                def body(i, ph, live):
                    g4, g5, odd = i - 4, i - 5, (ph + 1) % 2
                    if live(4):
                        dve.wait_ge(e["tanh"], g4 + 1)
                        wait(dve, e["w2"], g4 - 1)
                        dve.scalar_tensor_tensor(out=hT6[ph % 2], in0=th6[ph % 2], scalar=1.0,
                                                 in1=ps[2 + ph % 2], op0=ALU.add, op1=ALU.mult
                                                 ).then_inc(e["h"], 1)
                    if live(5):
                        r = srow[(ph + 3) % SLOTS]
                        dve.wait_ge(e["w2"], g5 + 1)
                        wait(dve, e["put%d" % odd], pairs(g5 - 4, odd))
                        dve.scalar_tensor_tensor(out=put[(ph + 3) % 4], in0=ps[6 + odd][:, 0:D],
                                                 scalar=r[:, D + SCORE:D + SCORE + 1],
                                                 in1=r[:, 0:D], op0=ALU.mult, op1=ALU.add
                                                 ).then_inc(e["out"], 1)
                    if live(0):
                        r = srow[ph]
                        dve.wait_ge(e["load%d" % (ph % 2)], pairs(i, ph))
                        wait(dve, e["xt"], i - 1)
                        dve.tensor_scalar(xn6[ph % 2], r[:, 0:D], r[:, D + MEAN:D + MEAN + 1],
                                          r[:, D + RSTD:D + RSTD + 1], ALU.subtract, ALU.mult
                                          ).then_inc(e["xn"], 1)

                batches(dve, 6, body, TILES, SLOTS)

            @block.scalar
            def _(act):
                act.activation(warm[:], bcol[:, 0:1], ACT.Tanh).then_inc(s_act, 1)

                def body(i, ph, live):
                    g1, g2, g4, odd = i - 1, i - 2, i - 4, (ph + 1) % 2
                    if live(4):
                        act.wait_ge(e["tr"], g4 + 1)
                        wait(act, e["h"], g4 - 1)
                        act.activation(th6[ph % 2], ps[2 + ph % 2], ACT.Tanh, scale=0.5
                                       ).then_inc(e["tanh"], 1)
                    if live(2):
                        act.wait_ge(e["w1"], g2 + 1)
                        wait(act, e["tr"], g2 - 1)
                        act.copy(u6[ph % 2], ps[ph % 2]).then_inc(e["u"], 1)
                    if live(1):
                        act.wait_ge(e["xt"], g1 + 1)
                        wait(act, e["w1"], g1 - 1)
                        act.copy(xnT6[odd], ps[5][:, 0:P]).then_inc(e["xnT"], 1)

                batches(act, 6, body, TILES, SLOTS)

            @block.tensor
            def _(pe):
                def body(i, ph, live):
                    g1, g2, g3, g5, odd = i - 1, i - 2, i - 3, i - 5, (ph + 1) % 2
                    if live(5):
                        at = expert(pe, g5)
                        pe.wait_ge(e["h"], g5 + 1)
                        wait(pe, e["out"], g5 - 1)
                        y = ps[6 + odd][:, 0:D]
                        pe.matmul(y, onesb[:], B2S[:, bass.ds(at, D)], start=True, stop=False)
                        for c in range(4):
                            mm = pe.matmul(y, hT6[odd][:, c * P:(c + 1) * P],
                                           W2[:, bass.ds(at + c * D, D)], start=False,
                                           stop=(c == 3))
                        mm.then_inc(e["w2"], 1)
                    if live(2):
                        at = expert(pe, g2)
                        pe.wait_ge(e["xnT"], g2 + 1)
                        wait(pe, e["u"], g2 - 1)
                        pe.matmul(ps[ph % 2], onesb[:], B1S[:, bass.ds(at, F)], start=True,
                                  stop=False)
                        pe.matmul(ps[ph % 2], xnT6[ph % 2], W1[:, bass.ds(at, F)], start=False,
                                  stop=True).then_inc(e["w1"], 1)
                    if live(3):
                        pe.wait_ge(e["u"], g3 + 1)
                        wait(pe, e["h"], g3 - 1)
                        for c in range(4):
                            mm = pe.transpose(ps[2 + odd][:, c * P:(c + 1) * P],
                                              u6[odd][:, c * P:(c + 1) * P], ident)
                        mm.then_inc(e["tr"], 1)
                    if live(1):
                        pe.wait_ge(e["xn"], g1 + 1)
                        wait(pe, e["xnT"], g1)
                        pe.transpose(ps[5][:, 0:P], xn6[odd], ident).then_inc(e["xt"], 1)

                batches(pe, 6, body, TILES, SLOTS)

            @block.gpsimd
            def _(pool):
                def body(i, ph, live):
                    if live(5):
                        g5, odd = i - 5, (ph + 1) % 2
                        done = e["put%d" % odd]
                        pool.wait_ge(e["out"], g5 + 1)
                        wait(pool, done, pairs(g5 - 2, odd))
                        pool.sem_inc(e["taken"], 1)
                        r = srow[(ph + 3) % SLOTS].bitcast(I32)
                        pool.indirect_dma_start(
                            out[:], bass.IndirectOffsetOnAxis(r[:, D + TOKEN:D + TOKEN + 1], 0),
                            put[(ph + 3) % 4], None,
                            bounds_check=NT - 1, oob_is_err=False).then_inc(done, 16)

                batches(pool, 6, body, TILES, SLOTS)
                pool.wait_ge(e["put0"], 16 * (-(-TILES // 2)))
                pool.wait_ge(e["put1"], 16 * (TILES // 2))


def _laid_out(i):
    c = np.ascontiguousarray
    t = lambda w: c(np.asarray(w).T)
    g = {k: np.asarray(v) for k, v in i.items()}
    zero = np.zeros(P, np.float32)
    a = {
        "x": c(g["x"].reshape(NT, D)),
        "ctxT": t(g["ctx_768"].reshape(NC, CD)),
        "mask": c(g["mask_BxS2_bf1"].reshape(1, NC)).view(np.uint8),
        "cst": constants(),
        "wq": c(g["L0_xattn_Wq"]), "wk": c(g["L0_xattn_Wk"]),
        "wv": c(g["L0_xattn_Wv"]), "wo": c(g["L0_xattn_Wo"]),
        "wof": t(g["L0_ffn_wo"]), "uo": t(g["L0_ffn_uo"]),
        "bgate": c(np.stack([g["L0_ffn_bf"], g["L0_ffn_bi"], g["L0_ffn_bc"]])[None]),
    }
    for n in "fic":
        a["w" + n] = t(g["L0_ffn_w" + n])
        a["u" + n] = t(g["L0_ffn_u" + n])
    for n in WEIGHTS:
        a["w_" + n] = t(g["L1_xattn_W_" + n])
    a["w1"], a["w2"], a["gw"] = c(g["L1_ffn_W1"]), c(g["L1_ffn_W2"]), t(g["L1_ffn_gate_w"])
    a["b1"], a["b2"] = (c(g["L1_ffn_b" + n]) for n in "12")
    ba = [np.concatenate([g["L1_xattn_b_att" + n]] * 2) for n in "01"]
    cols = [g["L1_xattn_b_d2v"], g["L1_xattn_b_img"], g["L1_xattn_b_txt"], *ba,
            *g["L1_xattn_b_f1"].reshape(4, P), g["L0_ffn_in_c"], g["L1_ffn_rms_w"]]
    a["bcol"] = c(np.stack(cols + [zero] * (16 - len(cols)), 1))
    a["brow"] = c(np.stack([g["L0_ffn_bo"], g["L1_xattn_b_f2"]])[None])
    return a


def kernel(**inputs):
    import concourse.bacc as bacc
    from concourse.bass_utils import run_bass_kernel_spmd as run

    arrays = _laid_out(inputs)
    nc = bacc.Bacc("TRN2", target_bir_lowering=False, num_devices=1)
    a = {n: nc.dram_tensor("in_" + n, v.shape, mybir.dt.from_np(v.dtype), kind="ExternalInput").ap()
         for n, v in arrays.items()}
    out = nc.dram_tensor("out", (NT, D), F32, kind="ExternalOutput").ap()
    xattn_ffn_kernel(nc, a, out)
    r = run(nc, [{"in_" + n: v for n, v in arrays.items()}], core_ids=[0])
    return r.results[0]["out"].reshape(B, S, D)
```
